# Optimizing a Trainium2 kernel written in Bass

```python
import numpy as np
import jax
import jax.numpy as jnp

def _softmax(x, axis=-1):
    return jax.nn.softmax(x, axis=axis)

def _gelu(x):
    return jax.nn.gelu(x, approximate=True)

def _silu(x):
    return jax.nn.silu(x)

def _sigmoid(x):
    return jax.nn.sigmoid(x)

def _layernorm(x, axis=-1, eps=1e-05):
    m = jnp.mean(x, axis=axis, keepdims=True)
    v = jnp.var(x, axis=axis, keepdims=True)
    return (x - m) / jnp.sqrt(v + eps)

def _scatter_add(tgt, idx, src, axis=0):
    return tgt.at[idx].add(src)

def _segment_sum(src, seg, n):
    return jax.ops.segment_sum(src, seg, n)
kernel_name = 'mk_recurrent_d1_jaxref_r4_7fe1a6'

def setup_inputs(seed: int=0):
    np.random.seed(seed)
    _w = jnp.asarray

    def _L0_attn_setup():
        import jax, jax.numpy as jnp
        import numpy as np
        D_MODEL = 256
        EXPAND = 2
        D_INNER = EXPAND * D_MODEL
        D_STATE = 64
        NGROUPS = 1
        HEADDIM = 128
        NHEADS = D_INNER // HEADDIM
        D_CONV = 4
        CONV_DIM = D_INNER + 2 * NGROUPS * D_STATE
        D_IN_PROJ = 2 * D_INNER + 2 * NGROUPS * D_STATE + NHEADS
        BATCH = 2
        SEQLEN = 1024
        RMS_EPS = 1e-05
        key = jax.random.key(seed)
        ks = jax.random.split(key, 8)
        u = jax.random.normal(ks[0], (BATCH, SEQLEN, D_MODEL), jnp.float32)
        in_proj_w = jax.random.normal(ks[1], (D_IN_PROJ, D_MODEL), jnp.float32) * 0.02
        conv_w = jax.random.normal(ks[2], (CONV_DIM, D_CONV), jnp.float32) * 0.2
        conv_b = jax.random.normal(ks[3], (CONV_DIM,), jnp.float32) * 0.1
        dt_bias = jax.random.normal(ks[4], (NHEADS,), jnp.float32) * 0.5
        A_log = jnp.log(jax.random.uniform(ks[5], (NHEADS,), jnp.float32, 1.0, 16.0))
        D = jnp.ones((NHEADS,), jnp.float32)
        rms_w = jnp.ones((D_INNER,), jnp.float32)
        out_w = jax.random.normal(ks[6], (D_MODEL, D_INNER), jnp.float32) * 0.02
        return {'u': u, 'in_proj_w': in_proj_w, 'conv_w': conv_w, 'conv_b': conv_b, 'dt_bias': dt_bias, 'A_log': A_log, 'D': D, 'rms_w': rms_w, 'out_w': out_w}
    _L0_attn_in = _L0_attn_setup()

    def _L0_ffn_setup():
        import jax, jax.numpy as jnp
        import numpy as np
        H = 256
        M = 128
        E = 16
        TOP_K = 2
        SCALE = 2.5
        NORM_TOPK = True
        B, S = (1, 256)

        def _moe(x, gate_w, w_gate, w_up, w_down, ws_gate, ws_up, ws_down):
            T = x.shape[0]
            shared = jax.nn.silu(x @ ws_gate) * (x @ ws_up) @ ws_down
            scores = jax.nn.sigmoid(x.astype(jnp.float32) @ gate_w.T.astype(jnp.float32))
            topk_w, topk_idx = jax.lax.top_k(scores, TOP_K)
            if NORM_TOPK and TOP_K > 1:
                topk_w = topk_w / (topk_w.sum(-1, keepdims=True) + 1e-20)
            topk_w = topk_w * SCALE
            route = jnp.zeros((T, E), topk_w.dtype).at[jnp.arange(T)[:, None], topk_idx].set(topk_w)
            g = jnp.einsum('th,ehm->etm', x, w_gate)
            u = jnp.einsum('th,ehm->etm', x, w_up)
            eo = jnp.einsum('etm,emh->eth', jax.nn.silu(g) * u, w_down)
            routed = jnp.einsum('te,eth->th', route.astype(x.dtype), eo)
            return routed + shared
        key = jax.random.key(seed)
        ks = jax.random.split(key, 8)
        std = 0.02
        return {'hidden_states': jax.random.normal(ks[0], (B, S, H), jnp.float32), 'gate_w': jax.random.normal(ks[1], (E, H), jnp.float32) * std, 'w_gate': jax.random.normal(ks[2], (E, H, M), jnp.float32) * std, 'w_up': jax.random.normal(ks[3], (E, H, M), jnp.float32) * std, 'w_down': jax.random.normal(ks[4], (E, M, H), jnp.float32) * std, 'ws_gate': jax.random.normal(ks[5], (H, M), jnp.float32) * std, 'ws_up': jax.random.normal(ks[6], (H, M), jnp.float32) * std, 'ws_down': jax.random.normal(ks[7], (M, H), jnp.float32) * std}
    _L0_ffn_in = _L0_ffn_setup()
    _d = {'L0_attn_u': _L0_attn_in['u'], 'L0_attn_in_proj_w': _L0_attn_in['in_proj_w'], 'L0_attn_conv_w': _L0_attn_in['conv_w'], 'L0_attn_conv_b': _L0_attn_in['conv_b'], 'L0_attn_dt_bias': _L0_attn_in['dt_bias'], 'L0_attn_A_log': _L0_attn_in['A_log'], 'L0_attn_D': _L0_attn_in['D'], 'L0_attn_rms_w': _L0_attn_in['rms_w'], 'L0_attn_out_w': _L0_attn_in['out_w'], 'L0_ffn_gate_w': _L0_ffn_in['gate_w'], 'L0_ffn_w_gate': _L0_ffn_in['w_gate'], 'L0_ffn_w_up': _L0_ffn_in['w_up'], 'L0_ffn_w_down': _L0_ffn_in['w_down'], 'L0_ffn_ws_gate': _L0_ffn_in['ws_gate'], 'L0_ffn_ws_up': _L0_ffn_in['ws_up'], 'L0_ffn_ws_down': _L0_ffn_in['ws_down']}
    _x0 = _d['L0_attn_u']
    _d['L0_attn_u'] = jax.random.normal(jax.random.fold_in(jax.random.key(seed), 1), (8, 1024, 256), dtype=_x0.dtype)
    del _x0
    return _d

def reference(L0_attn_u, L0_attn_in_proj_w, L0_attn_conv_w, L0_attn_conv_b, L0_attn_dt_bias, L0_attn_A_log, L0_attn_D, L0_attn_rms_w, L0_attn_out_w, L0_ffn_gate_w, L0_ffn_w_gate, L0_ffn_w_up, L0_ffn_w_down, L0_ffn_ws_gate, L0_ffn_ws_up, L0_ffn_ws_down):

    def _L0_attn_ref(u, in_proj_w, conv_w, conv_b, dt_bias, A_log, D, rms_w, out_w):
        import jax, jax.numpy as jnp
        import numpy as np
        D_MODEL = 256
        EXPAND = 2
        D_INNER = EXPAND * D_MODEL
        D_STATE = 64
        NGROUPS = 1
        HEADDIM = 128
        NHEADS = D_INNER // HEADDIM
        D_CONV = 4
        CONV_DIM = D_INNER + 2 * NGROUPS * D_STATE
        D_IN_PROJ = 2 * D_INNER + 2 * NGROUPS * D_STATE + NHEADS
        BATCH = 2
        SEQLEN = 1024
        RMS_EPS = 1e-05
        Bsz, L, _ = u.shape
        zxbcdt = jnp.einsum('bld,ed->ble', u, in_proj_w)
        s1 = D_INNER
        s2 = 2 * D_INNER
        s3 = s2 + NGROUPS * D_STATE
        s4 = s3 + NGROUPS * D_STATE
        z = zxbcdt[..., :s1]
        x = zxbcdt[..., s1:s2]
        B_part = zxbcdt[..., s2:s3]
        C_part = zxbcdt[..., s3:s4]
        dt = zxbcdt[..., s4:]
        dt = jax.nn.softplus(dt + dt_bias)
        xBC = jnp.concatenate([x, B_part, C_part], axis=-1)
        xt = xBC.transpose(0, 2, 1)
        kern = conv_w[:, None, :]
        conv = jax.lax.conv_general_dilated(xt, kern, (1,), [(D_CONV - 1, 0)], dimension_numbers=('NCH', 'OIH', 'NCH'), feature_group_count=CONV_DIM)
        xBC = jax.nn.silu((conv + conv_b[None, :, None]).transpose(0, 2, 1))
        x_c = xBC[..., :D_INNER]
        B_c = xBC[..., D_INNER:D_INNER + NGROUPS * D_STATE]
        C_c = xBC[..., D_INNER + NGROUPS * D_STATE:]
        x_s = x_c.reshape(Bsz, L, NHEADS, HEADDIM)
        hpg = NHEADS // NGROUPS
        B_full = jnp.repeat(B_c.reshape(Bsz, L, NGROUPS, D_STATE), hpg, axis=2)
        C_full = jnp.repeat(C_c.reshape(Bsz, L, NGROUPS, D_STATE), hpg, axis=2)
        A = -jnp.exp(A_log)

        def step(state, inp):
            x_t, dt_t, B_t, C_t = inp
            decay = jnp.exp(dt_t * A)[:, :, None, None]
            state = decay * state + B_t[:, :, None, :] * x_t[..., None]
            y_t = jnp.einsum('bhpn,bhn->bhp', state, C_t)
            return (state, y_t)
        init = jnp.zeros((Bsz, NHEADS, HEADDIM, D_STATE), u.dtype)
        xs = (x_s.transpose(1, 0, 2, 3), dt.transpose(1, 0, 2), B_full.transpose(1, 0, 2, 3), C_full.transpose(1, 0, 2, 3))
        _, ys = jax.lax.scan(step, init, xs)
        y = ys.transpose(1, 0, 2, 3) + D[None, None, :, None] * x_s
        y_flat = y.reshape(Bsz, L, D_INNER)
        mu = jnp.mean(y_flat * y_flat, axis=-1, keepdims=True)
        y_flat = y_flat * jax.lax.rsqrt(mu + RMS_EPS) * rms_w
        y_flat = y_flat * jax.nn.sigmoid(z)
        return jnp.einsum('bld,ed->ble', y_flat, out_w)

    def _L0_ffn_ref(hidden_states, gate_w, w_gate, w_up, w_down, ws_gate, ws_up, ws_down):
        import jax, jax.numpy as jnp
        import numpy as np
        H = 256
        M = 128
        E = 16
        TOP_K = 2
        SCALE = 2.5
        NORM_TOPK = True
        B, S = (1, 256)

        def _moe(x, gate_w, w_gate, w_up, w_down, ws_gate, ws_up, ws_down):
            T = x.shape[0]
            shared = jax.nn.silu(x @ ws_gate) * (x @ ws_up) @ ws_down
            scores = jax.nn.sigmoid(x.astype(jnp.float32) @ gate_w.T.astype(jnp.float32))
            topk_w, topk_idx = jax.lax.top_k(scores, TOP_K)
            if NORM_TOPK and TOP_K > 1:
                topk_w = topk_w / (topk_w.sum(-1, keepdims=True) + 1e-20)
            topk_w = topk_w * SCALE
            route = jnp.zeros((T, E), topk_w.dtype).at[jnp.arange(T)[:, None], topk_idx].set(topk_w)
            g = jnp.einsum('th,ehm->etm', x, w_gate)
            u = jnp.einsum('th,ehm->etm', x, w_up)
            eo = jnp.einsum('etm,emh->eth', jax.nn.silu(g) * u, w_down)
            routed = jnp.einsum('te,eth->th', route.astype(x.dtype), eo)
            return routed + shared
        b, s, h = hidden_states.shape
        x = hidden_states.reshape(-1, h)
        out = _moe(x, gate_w, w_gate, w_up, w_down, ws_gate, ws_up, ws_down)
        return out.reshape(b, s, h)
    x = L0_attn_u
    xn = _layernorm(x, axis=-1)
    s = _L0_attn_ref(xn, L0_attn_in_proj_w, L0_attn_conv_w, L0_attn_conv_b, L0_attn_dt_bias, L0_attn_A_log, L0_attn_D, L0_attn_rms_w, L0_attn_out_w)
    g = _silu(_L0_ffn_ref(xn, L0_ffn_gate_w, L0_ffn_w_gate, L0_ffn_w_up, L0_ffn_w_down, L0_ffn_ws_gate, L0_ffn_ws_up, L0_ffn_ws_down))
    x = x + s * g
    return x

_drawn_inputs = setup_inputs


def setup_inputs(seed=0):
    import zlib

    import numpy as np

    out = dict(_drawn_inputs(seed))
    spreads = {'L0_attn_D': (1.0, 0.6), 'L0_attn_rms_w': (1.0, 0.6)}
    factors = {'L0_attn_in_proj_w': 8.0,
     'L0_attn_conv_w': 8.0,
     'L0_attn_conv_b': 8.0,
     'L0_attn_dt_bias': 8.0,
     'L0_attn_A_log': 8.0,
     'L0_attn_out_w': 8.0,
     'L0_ffn_gate_w': 8.0,
     'L0_ffn_w_gate': 8.0,
     'L0_ffn_w_up': 8.0,
     'L0_ffn_w_down': 8.0,
     'L0_ffn_ws_gate': 8.0,
     'L0_ffn_ws_up': 8.0,
     'L0_ffn_ws_down': 8.0}
    for name, (base, spread) in spreads.items():
        noise = np.random.default_rng([zlib.crc32(name.encode()), seed]).standard_normal(out[name].shape)
        drawn = base * np.exp(spread * noise) if base else spread * noise
        out[name] = jnp.asarray(drawn.astype(out[name].dtype))
    for name, factor in factors.items():
        out[name] = (out[name] * factor).astype(out[name].dtype)
    return out
```

```python
from contextlib import ExitStack

import concourse.bass as bass
from concourse import mybir

F32 = mybir.dt.float32
I32 = mybir.dt.int32
U32 = mybir.dt.uint32
ACT = mybir.ActivationFunctionType
ALU = mybir.AluOpType
AX = mybir.AxisListType

P = 128
ds = bass.ds


def ge(eng, sem, value):
    if not isinstance(value, int) or value > 0:
        eng.wait_ge(sem, value)


def ge_apart(eng, passed, *waits):
    waits = [(sem, value if isinstance(value, int) else eng.to_reg(value)) for sem, value in waits]
    eng.wait_ge(passed, 1)
    for sem, value in waits:
        ge(eng, sem, value)


def steps(eng, first, last, body, peel=2):
    head = first + peel + (first % 2)
    for p in range(first, head):
        body(p, p % 2)
    tail = last - (last - head) % 2
    with eng.Fori(head // 2, tail // 2) as i:
        body(2 * i, 0)
        body(2 * i + 1, 1)
    for p in range(tail, last):
        body(p, p % 2)


def bass_mixer_moe(nc, u, w_in, conv_w, conv_b, dt_bias, a_log, d_skip, rms_w, w_out,
                   gate_w, w_gate, w_up, w_down, ws_gate, ws_up, ws_down, out):
    BATCH, SEQ, DM = u.shape
    E, _, MF = w_gate.shape
    H = dt_bias.shape[0]
    DI = w_out.shape[0]
    NS = (w_in.shape[1] - 2 * DI - H) // 2
    TOK = BATCH * SEQ
    KC = DM // P
    NT = TOK // P
    GRP = 512
    NG = TOK // GRP
    TPG = GRP // P
    XB = DI // P
    NR = E + H
    NTILE = 2 * NT + E
    TPB = SEQ // P
    EPS_LN = 1e-5
    EPS_RMS = 1e-5
    SCALE = 2.5
    assert DI // H == P and 2 * NS == P and MF == P and SEQ == 2 * GRP

    u_rows = u.rearrange("b l d -> (b l) d")
    out_rows = out.rearrange("b l d -> (b l) d")
    xn_d = nc.dram_tensor("xn_d", [TOK, DM], F32).ap()
    xs_d = nc.dram_tensor("xs_d", [NTILE * P, DM], F32).ap()
    ys_d = nc.dram_tensor("ys_d", [NTILE * P, DM], F32).ap()
    s_d = nc.dram_tensor("s_d", [TOK, DM], F32).ap()
    dec_d = nc.dram_tensor("dec_d", [NT * H, P], F32).ap()

    def group_rows(t, g):
        return t[ds(g * GRP, GRP), :].rearrange("(a p) d -> p a d", p=P)

    outer = ExitStack()
    with outer:
        def keep(name, shape, dt=F32):
            return outer.enter_context(nc.sbuf_tensor(name, shape, dt))

        xnT = keep("xnT", [P, KC, TOK])
        ident = keep("ident", [P, P])
        ones = keep("ones", [P, P])
        slot = keep("slot", [P, 2, NT], U32)
        wtop = keep("wtop", [P, 2, NT])
        tile_expert = keep("tile_expert", [1, NTILE], I32)
        ms_all = keep("ms_all", [P, NT])
        eps = keep("eps", [P, 2])
        early = ExitStack()
        logits = early.enter_context(nc.sbuf_tensor("logits", [P, NR, NT], F32))

        with ExitStack() as ctx:
            sb = lambda n, s, d=F32: ctx.enter_context(nc.sbuf_tensor(n, s, d))
            ps = lambda n, s: ctx.enter_context(nc.psum_tensor(n, s, F32))
            sem = lambda n: ctx.enter_context(nc.semaphore(n))
            w_rt = sb("w_rt", [P, KC, NR])
            zeros = sb("zeros", [P, 3072])
            u4 = [sb(f"u4_{q}", [P, TPG, DM]) for q in range(2)]
            xn4 = [sb(f"xn4_{q}", [P, TPG, DM]) for q in range(2)]
            stat = [sb(f"stat{q}", [P, TPG, 6]) for q in range(2)]
            mv = [sb(f"mv{q}", [P, TPG, 2]) for q in range(2)]
            std = [sb(f"std{q}", [P, TPG]) for q in range(2)]
            rstd = [sb(f"rstd{q}", [P, TPG]) for q in range(2)]
            lgs = [sb(f"lgs{q}", [NR, GRP]) for q in range(2)]
            ps_t = [[ps(f"ps_t{q}{k}", [P, GRP]) for k in range(KC)] for q in range(2)]
            ps_l = [ps(f"ps_l{q}", [NR, GRP]) for q in range(2)]
            ps_lt = [ps(f"ps_lt{q}", [P, TPG, NR]) for q in range(2)]
            w_here = sem("w_here")
            u_here = [sem(f"u_here{q}") for q in range(2)]
            xn_out = [sem(f"xn_out{q}") for q in range(2)]
            zeroed = sem("zeroed")
            c_ident0 = sem("c_ident0")
            c_ident = sem("c_ident")
            c_zero = sem("c_zero")
            stats_done = sem("stats_done")
            mv_done = sem("mv_done")
            std_done = sem("std_done")
            rstd_done = sem("rstd_done")
            xn_done = sem("xn_done")
            tr_done = sem("tr_done")
            xnT_act = sem("xnT_act")
            xnT_dve = sem("xnT_dve")
            lg_done = sem("lg_done")
            lgs_done = sem("lgs_done")
            lt_done = sem("lt_done")
            lt_read = sem("lt_read")
            block = ctx.enter_context(nc.Block())

            @block.gpsimd
            def _(pool):
                pool.memset(ident[:], 0.0).then_inc(c_ident0, 1)
                pool.memset(ones[:], 1.0)
                pool.memset(eps[:, 0:1], EPS_LN)
                pool.memset(eps[:, 1:2], EPS_RMS)
                pool.wait_ge(c_ident0, 1)
                pool.affine_select(out=ident[:], in_=ident[:], compare_op=ALU.not_equal, fill=1.0, base=0,
                                   pattern=[[-1, P]], channel_multiplier=1).then_inc(c_ident, 1)

            @block.sync
            def _(sp):
                for k in range(KC):
                    sp.dma_start(w_rt[:, k, 0:E], gate_w[k * P:(k + 1) * P, :]).then_inc(w_here, 16)
                    sp.dma_start(w_rt[:, k, E:NR], w_in[k * P:(k + 1) * P, 2 * DI + 2 * NS:]).then_inc(w_here, 16)
                for g in range(2):
                    sp.dma_start(u4[g][:], group_rows(u_rows, g)).then_inc(u_here[g], 16)

                def step(g, q, more=True):
                    sp.wait_ge(xn_done, g + 1)
                    sp.dma_start(group_rows(xn_d, g), xn4[q][:]).then_inc(xn_out[q], 16)
                    if more:
                        sp.dma_start(u4[q][:], group_rows(u_rows, g + 2)).then_inc(u_here[q], 16)

                with sp.Fori(0, NG // 2 - 1) as i:
                    step(2 * i, 0)
                    step(2 * i + 1, 1)
                for g in range(NG - 2, NG):
                    step(g, g % 2, more=False)
                for q in range(2):
                    sp.wait_ge(xn_out[q], 16 * (NG // 2))

            @block.vector
            def _(dve):
                dve.memset(zeros[:], 0.0).then_inc(c_zero, 1)

                def normalise(g, q):
                    dve.wait_ge(u_here[q], 16 * (g // 2 + 1) if isinstance(g, int) else (g - q) * 8 + 16)
                    for a in range(TPG):
                        last = dve.bn_stats(stat[q][:, a, :], u4[q][:, a, :])
                    last.then_inc(stats_done, 1)
                    ge_apart(dve, c_zero, (stats_done, g + 1))
                    for a in range(TPG):
                        last = dve.bn_aggr(mv[q][:, a, :], stat[q][:, a, :])
                    last.then_inc(mv_done, 1)

                def finish(g, q):
                    dve.wait_ge(std_done, g + 1)
                    dve.reciprocal(rstd[q][:], std[q][:]).then_inc(rstd_done, 1)
                    dve.wait_ge(rstd_done, g + 1)
                    ge(dve, xn_out[q], (g - q) * 8 if not isinstance(g, int) else 16 * (g // 2))
                    ge(dve, tr_done, g - 1)
                    for a in range(TPG):
                        last = dve.tensor_scalar(xn4[q][:, a, :], u4[q][:, a, :], mv[q][:, a, 0:1],
                                                 rstd[q][:, a:a + 1], ALU.subtract, ALU.mult)
                    last.then_inc(xn_done, 1)

                def take_back(g, q):
                    dve.wait_ge(tr_done, g + 1)
                    dve.tensor_copy(xnT[:, 1, ds(g * GRP, GRP)], ps_t[q][1][:]).then_inc(xnT_dve, 1)

                def logits_out(g, q):
                    dve.wait_ge(lt_done, g + 1)
                    dve.tensor_copy(logits[:, :, ds(g * TPG, TPG)],
                                    ps_lt[q][:].rearrange("p a e -> p e a")).then_inc(lt_read, 1)

                def step(g, q):
                    normalise(g, q)
                    if not isinstance(g, int) or g >= 1:
                        take_back(g - 1, 1 - q)
                    finish(g, q)
                    if not isinstance(g, int) or g >= 2:
                        logits_out(g - 2, q)

                steps(dve, 0, NG, step, peel=4)
                take_back(NG - 1, 1)
                logits_out(NG - 2, 0)
                logits_out(NG - 1, 1)

            @block.scalar
            def _(act):
                act.wait_ge(c_zero, 1)
                for r in range(NTILE // 12):
                    act.dma_start(xs_d[r * 12 * P:(r + 1) * 12 * P, :].rearrange("(p r) d -> p (r d)", p=P),
                                  zeros[:]).then_inc(zeroed, 16)
                act.wait_ge(c_ident, 1)

                def stdev(g, q):
                    act.wait_ge(mv_done, g + 1)
                    act.activation(std[q][:], mv[q][:, :, 1], ACT.Sqrt, bias=eps[:, 0:1]).then_inc(std_done, 1)

                def take_back(g, q):
                    act.wait_ge(tr_done, g + 1)
                    act.activation(xnT[:, 0, ds(g * GRP, GRP)], ps_t[q][0][:], ACT.Copy).then_inc(xnT_act, 1)

                def logits_back(g, q):
                    act.wait_ge(lg_done, g + 1)
                    ge(act, lt_done, g - 1)
                    act.activation(lgs[q][:], ps_l[q][:], ACT.Copy).then_inc(lgs_done, 1)

                def step(g, q):
                    stdev(g, q)
                    if not isinstance(g, int) or g >= 1:
                        take_back(g - 1, 1 - q)
                    if not isinstance(g, int) or g >= 2:
                        logits_back(g - 2, q)

                steps(act, 0, NG, step, peel=4)
                take_back(NG - 1, 1)
                logits_back(NG - 2, 0)
                logits_back(NG - 1, 1)
                act.wait_ge(zeroed, 16 * (NTILE // 12))

            @block.tensor
            def _(pe):
                pe.wait_ge(c_ident, 1)
                pe.wait_ge(w_here, 64)

                def turn(g, q):
                    pe.wait_ge(xn_done, g + 1)
                    ge(pe, xnT_act, g - 1)
                    ge(pe, xnT_dve, g - 1)
                    for a in range(TPG):
                        for k in range(KC):
                            last = pe.transpose(ps_t[q][k][:, a * P:(a + 1) * P], xn4[q][:, a, k * P:(k + 1) * P],
                                                ident[:])
                    last.then_inc(tr_done, 1)

                def product(g, q):
                    pe.wait_ge(xnT_act, g + 1)
                    pe.wait_ge(xnT_dve, g + 1)
                    ge(pe, lgs_done, g - 1)
                    for k in range(KC):
                        last = pe.matmul(ps_l[q][:], w_rt[:, k, :], xnT[:, k, ds(g * GRP, GRP)],
                                         start=(k == 0), stop=(k == KC - 1))
                    last.then_inc(lg_done, 1)

                def turn_logits(g, q):
                    ge_apart(pe, c_ident, (lgs_done, g + 1), (lt_read, g - 1))
                    for a in range(TPG):
                        last = pe.transpose(ps_lt[q][:, a, :], lgs[q][:, a * P:(a + 1) * P], ident[0:NR, 0:NR])
                    last.then_inc(lt_done, 1)

                def step(g, q):
                    turn(g, q)
                    if not isinstance(g, int) or g >= 1:
                        product(g - 1, 1 - q)
                    if not isinstance(g, int) or g >= 2:
                        turn_logits(g - 2, q)

                steps(pe, 0, NG, step, peel=4)
                product(NG - 1, 1)
                turn_logits(NG - 2, 0)
                turn_logits(NG - 1, 1)

        with ExitStack() as ctx:
            sb = lambda n, s, d=F32: ctx.enter_context(nc.sbuf_tensor(n, s, d))
            ps = lambda n, s: ctx.enter_context(nc.psum_tensor(n, s, F32))
            sem = lambda n: ctx.enter_context(nc.semaphore(n))
            T3 = [P, E, NT]
            iota_e = sb("iota_e", T3)
            iota_t = sb("iota_t", [1, NTILE])
            tri = sb("tri", [P, P])
            score = sb("score", T3)
            score2 = sb("score2", T3)
            hot = [sb(f"hot{c}", T3) for c in range(2)]
            tmp = sb("tmp", T3)
            cum = sb("cum", T3)
            onesr = sb("onesr", T3)
            best = sb("best", [P, 2, NT])
            pick = sb("pick", [P, NT])
            den = sb("den", [P, NT])
            before = sb("before", [P, E])
            count = sb("count", [P, E])
            tiles_i = sb("tiles_i", [P, E], I32)
            tiles = sb("tiles", [P, E])
            tiles_in = sb("tiles_in", [P, E])
            offset = sb("offset", [P, E])
            slot_f = sb("slot_f", [P, NT])
            passed = sb("passed", [1, NTILE, E])
            owner = sb("owner", [1, NTILE])
            owner2 = sb("owner2", [1, NTILE])
            dtb = sb("dtb", [P, H])
            alog = sb("alog", [P, H])
            arate = sb("arate", [P, H])
            D3 = [P, NT, H]
            dtx = sb("dtx", D3)
            dta = sb("dta", D3)
            dte = sb("dte", D3)
            dts = sb("dts", D3)
            dtq = sb("dtq", D3)
            dtp = sb("dtp", D3)
            dec = sb("dec", D3)
            decT = sb("decT", [P, 2, P])
            ps_c = ps("ps_c", [P, 2, 256])
            ps_d = ps("ps_d", [P, 2, P])
            p_here = sem("p_here")
            c_pool = sem("c_pool")
            c_iota = sem("c_iota")
            scored = sem("scored")
            abs_done = sem("abs_done")
            exp_done = sem("exp_done")
            rate_exp = sem("rate_exp")
            log_done = sem("log_done")
            dec_done = sem("dec_done")
            dec_turned = sem("dec_turned")
            decT_done = sem("decT_done")
            dec_out = sem("dec_out")
            counted = sem("counted")
            summed = sem("summed")
            dve_seq = sem("dve_seq")
            block = ctx.enter_context(nc.Block())

            @block.sync
            def _(sp):
                sp.dma_start(dtb[:], dt_bias.partition_broadcast(P)).then_inc(p_here, 16)
                sp.dma_start(alog[:], a_log.partition_broadcast(P)).then_inc(p_here, 16)
                sp.wait_ge(decT_done, 1)
                sp.dma_start(dec_d.rearrange("(c r) t -> r c t", r=P), decT[:]).then_inc(dec_out, 16)
                sp.wait_ge(dec_out, 16)

            @block.gpsimd
            def _(pool):
                pool.iota(iota_e[:], pattern=[[1, E], [0, NT]], base=-E, channel_multiplier=0,
                          allow_small_or_imprecise_dtypes=True).then_inc(c_iota, 1)
                pool.iota(iota_t[:], pattern=[[1, NTILE]], base=0, channel_multiplier=0,
                          allow_small_or_imprecise_dtypes=True).then_inc(c_iota, 1)
                pool.affine_select(out=tri[:], in_=ones[:], compare_op=ALU.is_gt, fill=0.0, base=0,
                                   pattern=[[1, P]], channel_multiplier=-1).then_inc(c_pool, 1)

            @block.scalar
            def _(act):
                act.activation(score[:], logits[:, 0:E, :], ACT.Sigmoid).then_inc(scored, 1)
                act.wait_ge(abs_done, 1)
                act.activation(dte[:], dta[:], ACT.Exp, scale=-1.0).then_inc(exp_done, 1)
                act.wait_ge(p_here, 32)
                act.activation(arate[:], alog[:], ACT.Exp).then_inc(rate_exp, 1)
                act.wait_ge(log_done, 1)
                act.activation(dec[:], dta[:], ACT.Exp, scale=-1.0).then_inc(dec_done, 1)
                act.wait_ge(dec_turned, 1)
                act.activation(decT[:], ps_d[:], ACT.Copy).then_inc(decT_done, 1)

            @block.tensor
            def _(pe):
                pe.wait_ge(c_pool, 1)
                pe.wait_ge(counted, 1)
                pe.matmul(ps_c[:, 0, 0:E], tri[:], count[:], start=True, stop=True)
                pe.matmul(ps_c[:, 1, 0:E], ones[:], count[:], start=True, stop=True).then_inc(summed, 1)
                pe.wait_ge(dec_done, 1)
                flat = dec[:].rearrange("p j h -> p (j h)")
                for c in range(2):
                    last = pe.transpose(ps_d[:, c, :], flat[:, c * P:(c + 1) * P], ident[:])
                last.then_inc(dec_turned, 1)

            @block.vector
            def _(dve):
                seq = [0]

                def link(ins):
                    seq[0] += 1
                    ins.then_inc(dve_seq, 1)
                    dve.wait_ge(dve_seq, seq[0])

                bc = [P, NT, H]
                dve.wait_ge(p_here, 32)
                link(dve.tensor_tensor(dtx[:], logits[:, E:NR, :].rearrange("p h j -> p j h"),
                                       dtb[:].unsqueeze(1).broadcast_to(bc), ALU.add))
                dve.scalar_tensor_tensor(dta[:], dtx[:], -1.0, dtx[:], ALU.mult, ALU.max).then_inc(abs_done, 1)

                def choose(c, src):
                    by_tok = [P, E, NT]
                    link(dve.tensor_reduce(best[:, c, :], src[:].rearrange("p e j -> p j e"), AX.X, ALU.max))
                    link(dve.tensor_tensor(tmp[:], src[:], best[:, c, :].unsqueeze(1).broadcast_to(by_tok),
                                           ALU.is_equal))
                    link(dve.tensor_tensor(tmp[:], tmp[:], iota_e[:], ALU.mult))
                    link(dve.tensor_reduce(pick[:], tmp[:].rearrange("p e j -> p j e"), AX.X, ALU.min))
                    link(dve.tensor_tensor(hot[c][:], iota_e[:], pick[:].unsqueeze(1).broadcast_to(by_tok),
                                           ALU.is_equal))

                dve.wait_ge(scored, 1)
                dve.wait_ge(c_iota, 2)
                choose(0, score)
                link(dve.scalar_tensor_tensor(score2[:], hot[0][:], -4.0, score[:], ALU.mult, ALU.add))
                choose(1, score2)
                link(dve.tensor_tensor(den[:], best[:, 0, :], best[:, 1, :], ALU.add))
                link(dve.tensor_scalar(den[:], den[:], 1e-20, None, ALU.add))
                link(dve.reciprocal(den[:], den[:]))
                for c in range(2):
                    link(dve.tensor_tensor(wtop[:, c, :], best[:, c, :], den[:], ALU.mult))
                link(dve.tensor_scalar(wtop[:], wtop[:], SCALE, None, ALU.mult))
                link(dve.memset(onesr[:], 1.0))
                link(dve.tensor_tensor(tmp[:], hot[0][:], hot[1][:], ALU.add))
                flat = lambda t: t[:].rearrange("p e j -> p (e j)")
                link(dve.tensor_tensor_scan(flat(cum), flat(onesr), flat(tmp), 0.0, ALU.mult, ALU.add))
                link(dve.memset(before[:], 0.0))
                link(dve.tensor_copy(before[:, 1:E], cum[:, 0:E - 1, NT - 1]))
                link(dve.tensor_tensor(count[:], cum[:, :, NT - 1], before[:], ALU.subtract))
                dve.tensor_tensor(cum[:], cum[:], tmp[:], ALU.subtract).then_inc(counted, 1)

                dve.wait_ge(exp_done, 1)
                link(dve.tensor_scalar(dtp[:], dte[:], 2.0, None, ALU.add))
                link(dve.reciprocal(dtp[:], dtp[:]))
                link(dve.tensor_tensor(dts[:], dte[:], dtp[:], ALU.mult))
                link(dve.tensor_tensor(dtq[:], dts[:], dts[:], ALU.mult))
                link(dve.tensor_scalar(dtp[:], dtq[:], 1.0 / 17, None, ALU.mult))
                for c in (15, 13, 11, 9, 7, 5, 3):
                    link(dve.scalar_tensor_tensor(dtp[:], dtp[:], 1.0 / c, dtq[:], ALU.add, ALU.mult))
                link(dve.scalar_tensor_tensor(dts[:], dtp[:], 1.0, dts[:], ALU.add, ALU.mult))
                link(dve.tensor_scalar(dts[:], dts[:], 2.0, None, ALU.mult))
                link(dve.scalar_tensor_tensor(dtx[:], dtx[:], 0.0, dts[:], ALU.max, ALU.add))
                dve.wait_ge(rate_exp, 1)
                dve.tensor_tensor(dta[:], dtx[:], arate[:].unsqueeze(1).broadcast_to(bc),
                                  ALU.mult).then_inc(log_done, 1)

                dve.wait_ge(summed, 1)
                link(dve.tensor_scalar(tiles_i[:], ps_c[:, 1, 0:E], float(P - 1), None, ALU.add))
                link(dve.tensor_scalar(tiles_i[:], tiles_i[:], 7, None, ALU.logical_shift_right))
                link(dve.tensor_copy(tiles[:], tiles_i[:]))
                link(dve.tensor_tensor_scan(tiles_in[:], onesr[:, 0, 0:E], tiles[:], 0.0, ALU.mult, ALU.add))
                link(dve.tensor_tensor(offset[:], tiles_in[:], tiles[:], ALU.subtract))
                link(dve.scalar_tensor_tensor(offset[:], offset[:], float(P), ps_c[:, 0, 0:E], ALU.mult, ALU.add))
                link(dve.tensor_tensor(offset[:], offset[:], before[:], ALU.subtract))
                link(dve.tensor_tensor(cum[:], cum[:], offset[:].unsqueeze(2).broadcast_to([P, E, NT]), ALU.add))
                for c in range(2):
                    link(dve.tensor_tensor(tmp[:], hot[c][:], cum[:], ALU.mult))
                    link(dve.tensor_reduce(slot_f[:], tmp[:].rearrange("p e j -> p j e"), AX.X, ALU.add))
                    link(dve.tensor_copy(slot[:, c, :], slot_f[:]))
                link(dve.tensor_tensor(passed[:], tiles_in[0:1, :].unsqueeze(1).broadcast_to([1, NTILE, E]),
                                       iota_t[:].unsqueeze(2).broadcast_to([1, NTILE, E]), ALU.is_le))
                link(dve.tensor_reduce(owner[:], passed[:], AX.X, ALU.add))
                link(dve.tensor_scalar(owner2[:], owner[:], float(E - 1), None, ALU.min))
                link(dve.tensor_copy(tile_expert[:], owner2[:]))

        early.close()
        wgu = keep("wgu", [P, KC, E, 2 * MF])
        with ExitStack() as ctx:
            sb = lambda n, s, d=F32: ctx.enter_context(nc.sbuf_tensor(n, s, d))
            ps = lambda n, s: ctx.enter_context(nc.psum_tensor(n, s, F32))
            sem = lambda n: ctx.enter_context(nc.semaphore(n))
            two = lambda n, s, d=F32: [sb(f"{n}{q}", s, d) for q in range(2)]
            win = sb("win", [P, KC, 2 * DI + 2 * NS])
            wo = sb("wo", [P, H, DM])
            cw = sb("cw", [P, XB + 1, 4])
            cb = sb("cb", [P, XB + 1])
            rw = sb("rw", [P, H])
            dsk = sb("dsk", [P, H])
            cin = sb("cin", [P, XB + 1, 3 + SEQ])
            cacc = two("cacc", [P, GRP])
            xc = two("xc", [P, XB, GRP])
            bmat = two("bmat", [NS, GRP])
            cmat = two("cmat", [NS, GRP])
            gate = two("gate", [P, H, P])
            dbc = two("dbc", [P, H, P])
            L = sb("L", [P, H, P])
            lin = two("lin", [NS, H, P])
            first = sb("first", [NS, H, P])
            eye4 = sb("eye4", [P, H, P])
            eyeD = sb("eyeD", [P, H, P])
            M = two("M", [P, H, P])
            xtok = two("xtok", [P, H, P])
            btok = two("btok", [P, NS])
            CL = two("CL", [NS, H, P])
            BL = two("BL", [P, H, NS])
            yg = sb("yg", [P, H, P])
            ysq = sb("ysq", [P, H, P])
            state = sb("state", [NS, H, P])
            sout = two("sout", [P, DM])
            stage = two("stage", [P, DM])
            sidx = two("sidx", [P, 2], U32)
            ps_p = [ps(f"ps_p{q}", [P, GRP]) for q in range(2)]
            ps_x = ps("ps_x", [P, H, P])
            ps_bg = ps("ps_bg", [P, GRP])
            ps_y = ps("ps_y", [P, H, P])
            ps_s = ps("ps_s", [NS, H, P])
            ps_o = ps("ps_o", [P, GRP])
            ps_z = ps("ps_z", [P, H, P])
            w_here = sem("w_here3")
            exp_here = sem("exp_here")
            dec_here = [sem(f"dec_here{q}") for q in range(2)]
            stage_here = [sem(f"stage_here{q}") for q in range(2)]
            s_out = [sem(f"s_out{q}") for q in range(2)]
            scattered = [sem(f"scattered{q}") for q in range(2)]
            idx_done = sem("idx_done")
            consts = sem("consts")
            wo_done = sem("wo_done")
            eye_done = sem("eye_done")
            projected = sem("projected")
            cin_done = sem("cin_done")
            conv_seq = sem("conv_seq")
            conv_done = sem("conv_done")
            silu_done = sem("silu_done")
            turned = sem("turned")
            xtok_done = sem("xtok_done")
            btok_done = sem("btok_done")
            z_done = sem("z_done")
            gate_done = sem("gate_done")
            d_seq = sem("d_seq")
            L_done = sem("L_done")
            lin_done = sem("lin_done")
            M_done = sem("M_done")
            MD_done = sem("MD_done")
            CL_done = sem("CL_done")
            BL_done = sem("BL_done")
            y_done = sem("y_done")
            s_done = sem("s_done")
            st_done = sem("st_done")
            yg_done = sem("yg_done")
            ysq_done = sem("ysq_done")
            o_done = sem("o_done")
            sout_done = sem("sout_done")
            block = ctx.enter_context(nc.Block())
            PBLK = [[0, 1], [2, 3], [4], []]
            SBLK = [[], [0, 1], [2, 3], [4]]
            NB = XB + 1

            def evac_bank(q, b):
                return (NB * q + b) % 2

            def some(n):
                return not isinstance(n, int) or n >= 0

            def chunks(p, k):
                return 4 * (p - 1) + k, 2 * (p - 1) + k // 2

            @block.sync
            def _(sp):
                for k in range(KC):
                    sp.dma_start(win[:, k, :], w_in[k * P:(k + 1) * P, 0:2 * DI + 2 * NS]).then_inc(w_here, 16)
                with nc.allow_non_contiguous_dma(reason="a few parameters per partition"):
                    sp.dma_start(cw[:], conv_w.rearrange("(b p) k -> p b k", p=P)).then_inc(w_here, 16)
                    sp.dma_start(cb[:], conv_b.rearrange("(b p) -> p b", p=P)).then_inc(w_here, 16)
                    sp.dma_start(rw[:], rms_w.rearrange("(h p) -> p h", p=P)).then_inc(w_here, 16)
                sp.dma_start(dsk[:], d_skip.partition_broadcast(P)).then_inc(w_here, 16)
                sp.dma_start(wo[:], w_out.rearrange("(h p) d -> p h d", p=P)).then_inc(w_here, 16)

                def load(n, before, q):
                    ge(sp, lin_done, n - 1)
                    sp.dma_start(dbc[q][:].rearrange("p h t -> p (h t)"),
                                 dec_d[ds(n * H, H), :].rearrange("h t -> (h t)").partition_broadcast(P)
                                 ).then_inc(dec_here[q], 16)
                    ge(sp, scattered[q], 32 * before)
                    sp.dma_start(stage[q][:], xn_d[ds(n * P, P), :]).then_inc(stage_here[q], 16)

                def store(n, q):
                    sp.wait_ge(sout_done, n + 1)
                    sp.dma_start(s_d[ds(n * P, P), :], sout[q][:]).then_inc(s_out[q], 16)

                def step(p, _):
                    for k in range(4):
                        n, before = chunks(p, k)
                        load(n, before, k % 2)
                        if some(n - 3):
                            store(n - 3, 1 - k % 2)

                steps(sp, 1, NG + 1, step)
                for n in range(NT - 3, NT):
                    store(n, n % 2)
                sp.wait_ge(exp_here, 16 * 2 * KC)
                for q in range(2):
                    sp.wait_ge(s_out[q], 16 * (NT // 2))

            @block.gpsimd
            def _(pool):
                pool.memset(cin[:, :, 0:3], 0.0)
                pool.memset(first[:], 0.0).then_inc(consts, 1)
                for h in range(H):
                    last = pool.tensor_copy(eye4[:, h, :], ident[:])
                last.then_inc(eye_done, 1)
                pool.wait_ge(w_here, 16 * (KC + 5))
                for h in range(H):
                    last = pool.tensor_scalar(eyeD[:, h, :], ident[:], dsk[:, h:h + 1], None, ALU.mult)
                last.then_inc(eye_done, 1)
                pool.wait_ge(eye_done, 2)

                def step(p, _):
                    for k in range(4):
                        n, before = chunks(p, k)
                        q = k % 2
                        gq = k % 2
                        pool.wait_ge(stage_here[q], 16 * before + 16)
                        ge(pool, scattered[q], 32 * before)
                        pool.tensor_copy(sidx[q][:], slot[:, :, ds(n, 1)].rearrange("p c o -> p (c o)")
                                         ).then_inc(idx_done, 1)
                        ge_apart(pool, eye_done, (idx_done, n + 1))
                        for c in range(2):
                            pool.indirect_dma_start(
                                out=xs_d, out_offset=bass.IndirectOffsetOnAxis(ap=sidx[q][:, c:c + 1], axis=0),
                                in_=stage[q][:], in_offset=None).then_inc(scattered[q], 16)
                        pool.wait_ge(silu_done, (XB + 2) * p)
                        pool.wait_ge(lin_done, n + 1)
                        ge(pool, y_done, n - 1)
                        pool.tensor_tensor(CL[q][:], lin[q][:],
                                           cmat_of[0](p)[:, k * P:(k + 1) * P].unsqueeze(1).broadcast_to([NS, H, P]),
                                           ALU.mult).then_inc(CL_done, 1)
                        pool.wait_ge(btok_done, n + 1)
                        ge(pool, s_done, n - 1)
                        pool.tensor_tensor(BL[q][:], L[:, :, P - 1:P].broadcast_to([P, H, NS]),
                                           btok[q][:].unsqueeze(1).broadcast_to([P, H, NS]),
                                           ALU.mult).then_inc(BL_done, 1)
                        pool.wait_ge(M_done, n + 1)
                        pool.tensor_tensor(M[q][:], M[q][:], eyeD[:], ALU.add).then_inc(MD_done, 1)

                cmat_of = [None]

                def with_parity(p, q):
                    cmat_of[0] = lambda _: cmat[1 - q]
                    step(p, q)

                steps(pool, 1, NG + 1, with_parity)
                for q in range(2):
                    pool.wait_ge(scattered[q], 16 * NT)

            @block.scalar
            def _(act):
                for k in range(KC):
                    act.dma_start(wgu[:, k, :, 0:MF], w_gate[:, k * P:(k + 1) * P, :].rearrange("e p m -> p e m")
                                  ).then_inc(exp_here, 16)
                    act.dma_start(wgu[:, k, :, MF:2 * MF], w_up[:, k * P:(k + 1) * P, :].rearrange("e p m -> p e m")
                                  ).then_inc(exp_here, 16)
                act.wait_ge(consts, 1)

                def evac(p, q, b):
                    act.wait_ge(projected, NB * p + b + 1)
                    ge(act, conv_done, NB * (p - 1) + b + 1)
                    act.activation(cin[:, b, 3 + q * GRP:3 + (q + 1) * GRP], ps_p[evac_bank(q, b)][:], ACT.Copy
                                   ).then_inc(cin_done, 1)

                def silu(p, q, b):
                    act.wait_ge(conv_done, NB * p + b + 1)
                    src = cacc[(NB * q + b) % 2]
                    if b < XB:
                        act.activation(xc[q][:, b, :], src[:], ACT.Silu).then_inc(silu_done, 1)
                    else:
                        act.activation(bmat[q][:], src[0:NS, :], ACT.Silu).then_inc(silu_done, 1)
                        act.activation(cmat[q][:], src[NS:2 * NS, :], ACT.Silu).then_inc(silu_done, 1)

                def token_side(n, q):
                    act.wait_ge(turned, n + 1)
                    ge(act, s_done, n - 1)
                    ge(act, BL_done, n - 1)
                    act.activation(btok[q][:], ps_bg[:, 0:NS], ACT.Copy).then_inc(btok_done, 1)
                    act.activation(xtok[q][:], ps_x[:], ACT.Copy).then_inc(xtok_done, 1)

                def gates(n, q):
                    act.wait_ge(z_done, n + 1)
                    ge(act, yg_done, n - 1)
                    act.activation(gate[q][:], ps_z[:], ACT.Tanh, scale=0.5).then_inc(gate_done, 1)

                def square(n):
                    act.wait_ge(yg_done, n + 1)
                    ge(act, o_done, n)
                    act.activation(ysq[:], ps_y[:], ACT.Square).then_inc(ysq_done, 1)

                def result(n, before, q):
                    act.wait_ge(o_done, n + 1)
                    ge(act, s_out[q], 16 * before)
                    act.activation(ms_all[:, ds(n, 1)], ps_o[:, DM:DM + 1], ACT.Copy)
                    act.activation(sout[q][:], ps_o[:, 0:DM], ACT.Copy).then_inc(sout_done, 1)

                def step(p, q, proj=True, scan=True):
                    for k in range(4):
                        n, before = chunks(p, k)
                        if scan:
                            token_side(n, k % 2)
                            if some(n - 2):
                                result(n - 2, before - 1, k % 2)
                        if proj:
                            for b in PBLK[k]:
                                evac(p, q, b)
                            for b in SBLK[k]:
                                if k == 1 and b == 0:
                                    ge(act, turned, 4 * (p - 1))
                                    ge(act, CL_done, 4 * (p - 1))
                                silu(p, q, b)
                        if scan:
                            if some(n - 1):
                                square(n - 1)
                            gates(n, k % 2)

                step(0, 0, scan=False)
                steps(act, 1, NG, step)
                step(NG, 0, proj=False)
                square(NT - 1)
                result(NT - 2, NT // 2 - 1, 0)
                result(NT - 1, NT // 2 - 1, 1)

            @block.vector
            def _(dve):
                dve.wait_ge(w_here, 16 * (KC + 5))
                for h in range(H):
                    last = dve.tensor_scalar(wo[:, h, :], wo[:, h, :], rw[:, h:h + 1], 0.5, ALU.mult, ALU.mult)
                last.then_inc(wo_done, 1)
                dve.wait_ge(eye_done, 1)

                def conv(p, q, b, c0):
                    dve.wait_ge(cin_done, NB * p + b + 1)
                    acc = cacc[(NB * q + b) % 2]
                    j = NB * p + b
                    ge(dve, silu_done, (XB + 2) * p + b - 1 if b >= 2 else (XB + 2) * p + b - 2 + (0 if b == 0 else 1))
                    src = cin[:, b, q * GRP:q * GRP + GRP + 3]
                    dve.tensor_scalar(acc[:], src[:, 0:GRP], cw[:, b, 0:1], cb[:, b:b + 1], ALU.mult, ALU.add
                                      ).then_inc(conv_seq, 1)
                    for t in range(1, 4):
                        dve.wait_ge(conv_seq, 3 * j + t)
                        dve.scalar_tensor_tensor(acc[:], src[:, t:t + GRP], cw[:, b, t:t + 1], acc[:], ALU.mult,
                                                 ALU.add).then_inc(conv_seq if t < 3 else conv_done, 1)

                def scans(n, before, q):
                    dve.wait_ge(dec_here[q], 16 * before + 16)
                    ge(dve, lin_done, n)
                    dve.tensor_copy(first[:, :, 0], dbc[q][0:NS, :, 0]).then_inc(d_seq, 1)
                    dve.wait_ge(d_seq, 2 * n + 1)
                    dve.memset(dbc[q][:, :, 0], 0.0).then_inc(d_seq, 1)
                    dve.wait_ge(d_seq, 2 * n + 2)
                    row = lambda t: t.rearrange("p h t -> p (h t)")
                    ge(dve, BL_done, n)
                    ge(dve, M_done, n)
                    dve.tensor_tensor_scan(row(L[:]), row(dbc[q][:]), row(eye4[:]), 0.0, ALU.mult, ALU.add
                                           ).then_inc(L_done, 1)
                    ge(dve, CL_done, n - 1)
                    dve.tensor_tensor_scan(row(lin[q][:]), row(dbc[q][0:NS]), row(first[:]), 0.0, ALU.mult, ALU.add
                                           ).then_inc(lin_done, 1)

                def mix(n, q):
                    dve.wait_ge(btok_done, n + 1)
                    dve.wait_ge(L_done, n + 1)
                    ge(dve, y_done, n - 1)
                    dve.tensor_tensor(M[q][:], L[:], ps_bg[:, P:2 * P].unsqueeze(1).broadcast_to([P, H, P]),
                                      ALU.mult).then_inc(M_done, 1)

                def gated(n, q):
                    dve.wait_ge(y_done, n + 1)
                    dve.wait_ge(gate_done, n + 1)
                    ge(dve, o_done, n)
                    dve.scalar_tensor_tensor(yg[:], gate[q][:], 1.0, ps_y[:], ALU.add, ALU.mult).then_inc(yg_done, 1)

                def carry(n, q, fresh):
                    dve.wait_ge(s_done, n + 1)
                    ge(dve, st_done, n)
                    if fresh:
                        dve.tensor_copy(state[:], ps_s[:]).then_inc(st_done, 1)
                        return
                    for h in range(H):
                        last = dve.scalar_tensor_tensor(state[:, h, :], state[:, h, :], lin[q][:, h, P - 1:P],
                                                        ps_s[:, h, :], ALU.mult, ALU.add)
                    last.then_inc(st_done, 1)

                def step(p, q, proj=True, scan=True):
                    for k in range(4):
                        n, before = chunks(p, k)
                        if scan:
                            scans(n, before, k % 2)
                            mix(n, k % 2)
                        if proj:
                            for b in PBLK[k]:
                                conv(p, q, b, 0)
                        if scan:
                            if some(n - 1):
                                gated(n - 1, 1 - k % 2)
                                carry(n - 1, 1 - k % 2, fresh=(q == 1 and k == 1))

                step(0, 0, scan=False)
                steps(dve, 1, NG, step)
                step(NG, 0, proj=False)
                gated(NT - 1, 1)

            @block.tensor
            def _(pe):
                pe.wait_ge(w_here, 16 * (KC + 5))
                pe.wait_ge(wo_done, 1)

                def project(p, q, b):
                    ge(pe, cin_done, NB * p + b - 1)
                    for k in range(KC):
                        last = pe.matmul(ps_p[evac_bank(q, b)][:], win[:, k, DI + b * P:DI + (b + 1) * P],
                                         xnT[:, k, ds(p * GRP, GRP)], start=(k == 0), stop=(k == KC - 1))
                    last.then_inc(projected, 1)

                def turn(p, q, n, k):
                    pe.wait_ge(silu_done, (XB + 2) * p)
                    ge(pe, xtok_done, n)
                    ge(pe, btok_done, n)
                    ge(pe, M_done, n)
                    t = slice(k * P, (k + 1) * P)
                    for b in range(XB):
                        pe.transpose(ps_x[:, b, :], xc[1 - q][:, b, t], ident[:])
                    pe.transpose(ps_bg[:, 0:NS], bmat[1 - q][:, t], ident[0:NS, 0:NS])
                    pe.matmul(ps_bg[:, P:2 * P], bmat[1 - q][:, t], cmat[1 - q][:, t], start=True, stop=True
                              ).then_inc(turned, 1)

                def zed(n):
                    ge(pe, gate_done, n)
                    for h in range(H):
                        for k in range(KC):
                            last = pe.matmul(ps_z[:, h, :], win[:, k, h * P:(h + 1) * P], xnT[:, k, ds(n * P, P)],
                                             start=(k == 0), stop=(k == KC - 1))
                    last.then_inc(z_done, 1)

                def mixed(n, q, fresh):
                    pe.wait_ge(MD_done, n + 1)
                    pe.wait_ge(xtok_done, n + 1)
                    pe.wait_ge(CL_done, n + 1)
                    ge(pe, st_done, n)
                    ge(pe, yg_done, n)
                    ge(pe, ysq_done, n)
                    for h in range(H):
                        last = pe.matmul(ps_y[:, h, :], xtok[q][:, h, :], M[q][:, h, :], start=True, stop=fresh)
                        if not fresh:
                            last = pe.matmul(ps_y[:, h, :], state[:, h, :], CL[q][:, h, :], start=False, stop=True)
                    last.then_inc(y_done, 1)

                def new_state(n, q):
                    pe.wait_ge(BL_done, n + 1)
                    for h in range(H):
                        last = pe.matmul(ps_s[:, h, :], BL[q][:, h, :], xtok[q][:, h, :], start=True, stop=True)
                    last.then_inc(s_done, 1)

                def output(n):
                    pe.wait_ge(yg_done, n + 1)
                    pe.wait_ge(ysq_done, n + 1)
                    ge(pe, sout_done, n)
                    for h in range(H):
                        pe.matmul(ps_o[:, 0:DM], yg[:, h, :], wo[:, h, :], start=(h == 0), stop=(h == H - 1))
                    for h in range(H):
                        last = pe.matmul(ps_o[:, DM:DM + 1], ysq[:, h, :], ones[:, 0:1], start=(h == 0),
                                         stop=(h == H - 1))
                    last.then_inc(o_done, 1)

                def step(p, q, proj=True, scan=True):
                    for k in range(4):
                        n, _ = chunks(p, k)
                        if scan:
                            turn(p, q, n, k)
                            if some(n - 2):
                                output(n - 2)
                        if proj:
                            for b in PBLK[k]:
                                project(p, q, b)
                        if scan:
                            if some(n - 1):
                                mixed(n - 1, 1 - k % 2, fresh=(q == 1 and k == 1))
                                new_state(n - 1, 1 - k % 2)
                            zed(n)

                step(0, 0, scan=False)
                steps(pe, 1, NG, step)
                step(NG, 0, proj=False)
                output(NT - 2)
                mixed(NT - 1, 1, fresh=False)
                output(NT - 1)

        NX = NTILE // TPG
        with ExitStack() as ctx:
            sb = lambda n, s, d=F32: ctx.enter_context(nc.sbuf_tensor(n, s, d))
            ps = lambda n, s: ctx.enter_context(nc.psum_tensor(n, s, F32))
            sem = lambda n: ctx.enter_context(nc.semaphore(n))
            two = lambda n, s, d=F32: [sb(f"{n}{q}", s, d) for q in range(2)]
            wd = sb("wd", [P, E, DM])
            x4 = two("x4", [P, TPG, DM])
            y4 = two("y4", [P, TPG, DM])
            xT = two("xT", [P, KC, P])
            sg = two("sg", [P, MF])
            hid = two("hid", [P, MF])
            hidT = two("hidT", [P, P])
            ps_t = [ps(f"px_t{q}", [P, KC, P]) for q in range(2)]
            ps_g = [ps(f"px_g{q}", [P, 2 * MF]) for q in range(2)]
            ps_h = [ps(f"px_h{q}", [P, P]) for q in range(2)]
            ps_y = [ps(f"px_y{q}", [P, DM]) for q in range(2)]
            wd_here = sem("wd_here")
            x_here = [sem(f"x_here{q}") for q in range(2)]
            y_out = [sem(f"y_out{q}") for q in range(2)]
            x_turned = sem("x_turned")
            xT_done = sem("xT_done")
            gu_done = sem("gu_done")
            sg_done = sem("sg_done")
            hid_done = sem("hid_done")
            h_turned = sem("h_turned")
            hidT_done = sem("hidT_done")
            down_done = sem("down_done")
            y4_done = sem("y4_done")
            block = ctx.enter_context(nc.Block())

            @block.sync
            def _(sp):
                sp.dma_start(wd[:], w_down.rearrange("e m d -> m e d")).then_inc(wd_here, 16)

                def step(p, q):
                    ge(sp, x_turned, TPG * (p - 1))
                    sp.dma_start(x4[q][:], group_rows(xs_d, p)).then_inc(x_here[q], 16)
                    if some(p - 2):
                        store(p - 2, q)

                def store(p, q):
                    sp.wait_ge(y4_done, TPG * (p + 1))
                    sp.dma_start(group_rows(ys_d, p), y4[q][:]).then_inc(y_out[q], 16)

                steps(sp, 0, NX, step)
                store(NX - 2, 0)
                store(NX - 1, 1)
                for q in range(2):
                    sp.wait_ge(y_out[q], 16 * (NX // 2))

            @block.tensor
            def _(pe):
                def turn(p, q, a):
                    n = TPG * p + a
                    if a == 0:
                        pe.wait_ge(x_here[q], (p - q) * 8 + 16 if not isinstance(p, int) else 16 * (p // 2) + 16)
                    ge(pe, xT_done, n - 1)
                    for k in range(KC):
                        last = pe.transpose(ps_t[a % 2][:, k, :], x4[q][:, a, k * P:(k + 1) * P], ident[:])
                    last.then_inc(x_turned, 1)

                def up(n, q):
                    e = pe.value_load(tile_expert[0:1, ds(n, 1)], min_val=0, max_val=E - 1)
                    pe.wait_ge(xT_done, n + 1)
                    ge(pe, hid_done, n - 1)
                    for k in range(KC):
                        last = pe.matmul(ps_g[q][:], xT[q][:, k, :], wgu[:, k, e, :], start=(k == 0),
                                         stop=(k == KC - 1))
                    last.then_inc(gu_done, 1)

                def turn_hidden(n, q):
                    pe.wait_ge(hid_done, n + 1)
                    ge(pe, hidT_done, n - 1)
                    pe.transpose(ps_h[q][:], hid[q][:], ident[:]).then_inc(h_turned, 1)

                def down(n, q):
                    e = pe.value_load(tile_expert[0:1, ds(n, 1)], min_val=0, max_val=E - 1)
                    pe.wait_ge(hidT_done, n + 1)
                    ge(pe, y4_done, n - 1)
                    pe.matmul(ps_y[q][:], hidT[q][:], wd[:, e, :], start=True, stop=True).then_inc(down_done, 1)

                def step(p, q):
                    for a in range(TPG):
                        n = TPG * p + a
                        turn(p, q, a)
                        if some(n - 3):
                            down(n - 3, 1 - a % 2)
                        if some(n - 1):
                            up(n - 1, 1 - a % 2)
                        if some(n - 2):
                            turn_hidden(n - 2, a % 2)

                pe.wait_ge(wd_here, 16)
                steps(pe, 0, NX, step)
                down(NTILE - 3, 1)
                up(NTILE - 1, 1)
                turn_hidden(NTILE - 2, 0)
                down(NTILE - 2, 0)
                turn_hidden(NTILE - 1, 1)
                down(NTILE - 1, 1)

            @block.scalar
            def _(act):
                def xT_copy(n, q):
                    act.wait_ge(x_turned, n + 1)
                    ge(act, gu_done, n - 1)
                    act.activation(xT[q][:], ps_t[q][:], ACT.Copy).then_inc(xT_done, 1)

                def silu(n, q):
                    act.wait_ge(gu_done, n + 1)
                    ge(act, hid_done, n - 1)
                    act.activation(sg[q][:], ps_g[q][:, 0:MF], ACT.Silu).then_inc(sg_done, 1)

                def hidT_copy(n, q):
                    act.wait_ge(h_turned, n + 1)
                    ge(act, down_done, n - 1)
                    act.activation(hidT[q][:], ps_h[q][:], ACT.Copy).then_inc(hidT_done, 1)

                def step(p, q):
                    for a in range(TPG):
                        n = TPG * p + a
                        xT_copy(n, a % 2)
                        if some(n - 1):
                            silu(n - 1, 1 - a % 2)
                        if some(n - 2):
                            hidT_copy(n - 2, a % 2)

                steps(act, 0, NX, step)
                silu(NTILE - 1, 1)
                hidT_copy(NTILE - 2, 0)
                hidT_copy(NTILE - 1, 1)

            @block.vector
            def _(dve):
                def hidden(n, q):
                    dve.wait_ge(sg_done, n + 1)
                    ge(dve, h_turned, n - 1)
                    dve.tensor_tensor(hid[q][:], sg[q][:], ps_g[q][:, MF:2 * MF], ALU.mult).then_inc(hid_done, 1)

                def result(p, q, a, qa):
                    dve.wait_ge(down_done, TPG * p + a + 1)
                    if a == 0:
                        ge(dve, y_out[q], (p - q) * 8 if not isinstance(p, int) else 16 * (p // 2))
                    dve.tensor_copy(y4[q][:, a, :], ps_y[qa][:]).then_inc(y4_done, 1)

                def step(p, q):
                    for a in range(TPG):
                        n = TPG * p + a
                        if some(n - 1):
                            hidden(n - 1, 1 - a % 2)
                        if some(n - 3):
                            if a == 3:
                                result(p, q, 0, 0)
                            else:
                                result(p - 1, 1 - q, a + 1, (a + 1) % 2)

                steps(dve, 0, NX, step)
                result(NX - 1, 1, 1, 1)
                hidden(NTILE - 1, 1)
                result(NX - 1, 1, 2, 0)
                result(NX - 1, 1, 3, 1)

        with ExitStack() as ctx:
            sb = lambda n, s, d=F32: ctx.enter_context(nc.sbuf_tensor(n, s, d))
            ps = lambda n, s: ctx.enter_context(nc.psum_tensor(n, s, F32))
            sem = lambda n: ctx.enter_context(nc.semaphore(n))
            two = lambda n, s, d=F32: [sb(f"{n}{q}", s, d) for q in range(2)]
            wsg = sb("wsg", [P, KC, MF])
            wsu = sb("wsu", [P, KC, MF])
            wsd = sb("wsd", [MF, DM])
            msq = sb("msq", [P, NT])
            rms = sb("rms", [P, NT])
            u4 = two("fu4", [P, TPG, DM])
            s4 = two("fs4", [P, TPG, DM])
            o4 = two("fo4", [P, TPG, DM])
            RING = 2
            rows = [[[sb(f"rows{q}{a}{c}", [P, DM]) for c in range(2)] for a in range(TPG)] for q in range(RING)]
            hsg = two("hsg", [P, GRP])
            hs = two("hs", [P, GRP])
            acc = two("acc", [P, DM])
            gsil = two("gsil", [P, DM])
            gidx = [[sb(f"gidx{q}{a}", [P, 2], U32) for a in range(TPG)] for q in range(2)]
            ps_g = [ps(f"pf_g{q}", [P, GRP]) for q in range(2)]
            ps_u = [ps(f"pf_u{q}", [P, GRP]) for q in range(2)]
            ps_y = [ps(f"pf_y{q}", [P, DM]) for q in range(2)]
            ws_here = sem("ws_here")
            us_here = [sem(f"us_here{q}") for q in range(2)]
            rows_here = [[sem(f"rows_here{q}{a}") for a in range(TPG)] for q in range(2)]
            o_out = [sem(f"o_out{q}") for q in range(2)]
            gi_done = sem("gi_done")
            rms_done = sem("rms_done")
            rms_inv = sem("rms_inv")
            up_done = sem("up_done")
            hsg_done = sem("hsg_done")
            hs_done = sem("hs_done")
            dn_done = sem("dn_done")
            m_seq = sem("m_seq")
            acc_done = sem("acc_done")
            gs_done = sem("gs_done")
            sg_done = sem("fsg_done")
            o4_done = sem("o4_done")
            block = ctx.enter_context(nc.Block())

            def parity_count(p, q):
                return p // 2 if isinstance(p, int) else (p - q)

            def times16(p, q, extra):
                return 16 * (p // 2) + 16 * extra if isinstance(p, int) else (p - q) * 8 + 16 * extra

            @block.sync
            def _(sp):
                for k in range(KC):
                    sp.dma_start(wsg[:, k, :], ws_gate[k * P:(k + 1) * P, :]).then_inc(ws_here, 16)
                    sp.dma_start(wsu[:, k, :], ws_up[k * P:(k + 1) * P, :]).then_inc(ws_here, 16)
                sp.dma_start(wsd[:], ws_down).then_inc(ws_here, 16)

                def store(p, q):
                    sp.wait_ge(o4_done, TPG * (p + 1))
                    sp.dma_start(group_rows(out_rows, p), o4[q][:]).then_inc(o_out[q], 16)

                def step(p, q):
                    ge(sp, o4_done, TPG * (p - 1))
                    sp.dma_start(u4[q][:], group_rows(u_rows, p)).then_inc(us_here[q], 16)
                    sp.dma_start(s4[q][:], group_rows(s_d, p)).then_inc(us_here[q], 16)
                    if some(p - 2):
                        store(p - 2, q)

                steps(sp, 0, NG, step)
                store(NG - 2, 0)
                store(NG - 1, 1)
                for q in range(2):
                    sp.wait_ge(o_out[q], 16 * (NG // 2))

            @block.gpsimd
            def _(pool):
                def step(p, q):
                    for a in range(TPG):
                        ge(pool, rows_here[q][a], 2 * times16(p, q, 0))
                        last = pool.tensor_copy(gidx[q][a][:], slot[:, :, ds(TPG * p + a, 1)].rearrange(
                            "p c o -> p (c o)"))
                    last.then_inc(gi_done, 1)
                    pool.wait_ge(gi_done, p + 1)
                    for a in range(TPG):
                        ge_apart(pool, gi_done, (acc_done, TPG * (p - 2) + a + 1))
                        for c in range(2):
                            pool.indirect_dma_start(
                                out=rows[q][a][c][:], out_offset=None, in_=ys_d,
                                in_offset=bass.IndirectOffsetOnAxis(ap=gidx[q][a][:, c:c + 1], axis=0)
                            ).then_inc(rows_here[q][a], 16)

                steps(pool, 0, NG, step)

            @block.tensor
            def _(pe):
                pe.wait_ge(ws_here, 16 * (2 * KC + 1))

                def up(p, q):
                    ge(pe, hs_done, p - 1)
                    for bank, w in ((ps_g, wsg), (ps_u, wsu)):
                        for k in range(KC):
                            last = pe.matmul(bank[q][:], w[:, k, :], xnT[:, k, ds(p * GRP, GRP)], start=(k == 0),
                                             stop=(k == KC - 1))
                    last.then_inc(up_done, 1)

                def down(p, q):
                    pe.wait_ge(hs_done, p + 1)
                    for a in range(TPG):
                        ge(pe, acc_done, TPG * p + a - 1)
                        pe.matmul(ps_y[a % 2][:], hs[q][:, a * P:(a + 1) * P], wsd[:], start=True, stop=True
                                  ).then_inc(dn_done, 1)

                def step(p, q):
                    up(p, q)
                    if some(p - 1):
                        down(p - 1, 1 - q)

                steps(pe, 0, NG, step)
                down(NG - 1, 1)

            @block.scalar
            def _(act):
                act.activation(rms[:], ms_all[:], ACT.Sqrt, bias=eps[:, 1:2], scale=1.0 / DI).then_inc(rms_done, 1)

                def silu_up(p, q):
                    act.wait_ge(up_done, p + 1)
                    ge(act, hs_done, p - 1)
                    act.activation(hsg[q][:], ps_g[q][:], ACT.Silu).then_inc(hsg_done, 1)

                def silu_out(n, q):
                    act.wait_ge(acc_done, n + 1)
                    ge(act, sg_done, n - 1)
                    act.activation(gsil[q][:], acc[q][:], ACT.Silu).then_inc(gs_done, 1)

                def step(p, q):
                    silu_up(p, q)
                    if some(p - 1):
                        for a in range(TPG):
                            silu_out(TPG * (p - 1) + a, a % 2)

                steps(act, 0, NG, step)
                for a in range(TPG):
                    silu_out(TPG * (NG - 1) + a, a % 2)

            @block.vector
            def _(dve):
                dve.wait_ge(rms_done, 1)
                dve.reciprocal(msq[:], rms[:]).then_inc(rms_inv, 1)
                dve.wait_ge(rms_inv, 1)

                def hidden(p, q):
                    dve.wait_ge(hsg_done, p + 1)
                    ge(dve, dn_done, TPG * (p - 1))
                    dve.tensor_tensor(hs[q][:], hsg[q][:], ps_u[q][:], ALU.mult).then_inc(hs_done, 1)

                def merge(p, q, a):
                    n = TPG * p + a
                    dve.wait_ge(dn_done, n + 1)
                    dve.wait_ge(rows_here[q][a], 2 * times16(p, q, 1))
                    ge(dve, gs_done, n - 1)
                    y = acc[a % 2]
                    dve.scalar_tensor_tensor(y[:], rows[q][a][0][:], wtop[:, 0, ds(n, 1)], ps_y[a % 2][:], ALU.mult,
                                             ALU.add).then_inc(m_seq, 1)
                    dve.wait_ge(m_seq, n + 1)
                    dve.scalar_tensor_tensor(y[:], rows[q][a][1][:], wtop[:, 1, ds(n, 1)], y[:], ALU.mult,
                                             ALU.add).then_inc(acc_done, 1)

                def gate_out(p, q, a):
                    n = TPG * p + a
                    if a == 0:
                        dve.wait_ge(us_here[q], 2 * times16(p, q, 1))
                        ge(dve, o_out[q], times16(p, q, 0))
                    dve.wait_ge(gs_done, n + 1)
                    dve.scalar_tensor_tensor(o4[q][:, a, :], s4[q][:, a, :], msq[:, ds(n, 1)], gsil[a % 2][:],
                                             ALU.mult, ALU.mult).then_inc(sg_done, 1)
                    dve.wait_ge(sg_done, n + 1)
                    dve.tensor_tensor(o4[q][:, a, :], o4[q][:, a, :], u4[q][:, a, :], ALU.add).then_inc(o4_done, 1)

                def pair(p, q):
                    for a in range(TPG):
                        merge(p, q, a)
                        if a >= 1:
                            gate_out(p, q, a - 1)
                    gate_out(p, q, TPG - 1)

                def step(p, q):
                    hidden(p, q)
                    if some(p - 1):
                        pair(p - 1, 1 - q)

                steps(dve, 0, NG, step)
                pair(NG - 1, 1)


_INS = ['L0_attn_u', 'L0_attn_in_proj_w', 'L0_attn_conv_w', 'L0_attn_conv_b', 'L0_attn_dt_bias', 'L0_attn_A_log',
        'L0_attn_D', 'L0_attn_rms_w', 'L0_attn_out_w', 'L0_ffn_gate_w', 'L0_ffn_w_gate', 'L0_ffn_w_up',
        'L0_ffn_w_down', 'L0_ffn_ws_gate', 'L0_ffn_ws_up', 'L0_ffn_ws_down']
_TURNED = ('L0_attn_in_proj_w', 'L0_attn_out_w', 'L0_ffn_gate_w')


def kernel(**inputs):
    import numpy as _np
    import concourse.bacc as _bacc
    from concourse import mybir as _mybir
    from concourse.bass_utils import run_bass_kernel_spmd as _run

    nc = _bacc.Bacc("TRN2", target_bir_lowering=False, num_devices=1)
    arrays, args = {}, []
    for name in _INS:
        a = _np.asarray(inputs[name])
        a = _np.ascontiguousarray(a.T if name in _TURNED else a)
        arrays[f"in_{name}_dram"] = a
        args.append(nc.dram_tensor(f"in_{name}_dram", a.shape, _mybir.dt.from_np(a.dtype), kind="ExternalInput").ap())
    shape = inputs['L0_attn_u'].shape
    args.append(nc.dram_tensor("out_0_dram", shape, _mybir.dt.float32, kind="ExternalOutput").ap())
    bass_mixer_moe(nc, *args)
    r = _run(nc, [arrays], core_ids=[0])
    return r.results[0]["out_0_dram"]
```

```python
from contextlib import ExitStack

import concourse.bass as bass
from concourse import mybir

F32 = mybir.dt.float32
I32 = mybir.dt.int32
U32 = mybir.dt.uint32
ACT = mybir.ActivationFunctionType
ALU = mybir.AluOpType
AX = mybir.AxisListType

P = 128
ds = bass.ds


def ge(eng, sem, value):
    if not isinstance(value, int) or value > 0:
        eng.wait_ge(sem, value)


def ge_apart(eng, passed, *waits):
    waits = [(sem, value if isinstance(value, int) else eng.to_reg(value)) for sem, value in waits]
    eng.wait_ge(passed, 1)
    for sem, value in waits:
        ge(eng, sem, value)


def times(dmas, p, q, now):
    return 16 * dmas * (p // 2 + now) if isinstance(p, int) else (p - q) * (8 * dmas) + 16 * dmas * now


def reached(p, least):
    return not isinstance(p, int) or p >= least


def steps(eng, first, last, body, peel=2):
    head = first + peel + (first % 2)
    for p in range(first, head):
        body(p, p % 2)
    tail = last - (last - head) % 2
    with eng.Fori(head // 2, tail // 2) as i:
        body(2 * i, 0)
        body(2 * i + 1, 1)
    for p in range(tail, last):
        body(p, p % 2)


def bass_mixer_moe(nc, u, w_in, conv_w, conv_b, dt_bias, a_log, d_skip, rms_w, w_out,
                   gate_w, w_gate, w_up, w_down, ws_gate, ws_up, ws_down, out):
    BATCH, SEQ, DM = u.shape
    E, _, MF = w_gate.shape
    H = dt_bias.shape[0]
    DI = w_out.shape[0]
    NS = (w_in.shape[1] - 2 * DI - H) // 2
    TOK = BATCH * SEQ
    KC = DM // P
    NT = TOK // P
    GRP = 512
    NG = TOK // GRP
    TPG = GRP // P
    XB = DI // P
    NR = E + H
    NTILE = 2 * NT + E
    TPB = SEQ // P
    EPS_LN = 1e-5
    EPS_RMS = 1e-5
    SCALE = 2.5
    assert DI // H == P and 2 * NS == P and MF == P and SEQ == 2 * GRP

    u_rows = u.rearrange("b l d -> (b l) d")
    out_rows = out.rearrange("b l d -> (b l) d")
    xn_d = nc.dram_tensor("xn_d", [TOK, DM], F32).ap()
    tok_d = nc.dram_tensor("tok_d", [NTILE * P, 1], F32).ap()
    ys_d = nc.dram_tensor("ys_d", [NTILE * P, DM], F32).ap()
    s_d = nc.dram_tensor("s_d", [TOK, DM], F32).ap()
    dec_d = nc.dram_tensor("dec_d", [NT * H, P], F32).ap()

    def group_rows(t, g):
        return t[ds(g * GRP, GRP), :].rearrange("(a p) d -> p a d", p=P)

    outer = ExitStack()
    with outer:
        def keep(name, shape, dt=F32):
            return outer.enter_context(nc.sbuf_tensor(name, shape, dt))

        xnT = keep("xnT", [P, KC, TOK])
        ident = keep("ident", [P, P])
        ones = keep("ones", [P, P])
        slot = keep("slot", [P, 2, NT], U32)
        wtop = keep("wtop", [P, 2, NT])
        tile_expert = keep("tile_expert", [1, NTILE], I32)
        ms_all = keep("ms_all", [P, NT])
        eps = keep("eps", [P, 2])
        wgu = keep("wgu", [P, KC, E, 2 * MF])
        scratch = wgu[:].rearrange("p k e m -> p (k e m)")
        logits = scratch[:, 0:NR * NT].rearrange("p (e j) -> p e j", e=NR)

        with ExitStack() as ctx:
            sb = lambda n, s, d=F32: ctx.enter_context(nc.sbuf_tensor(n, s, d))
            ps = lambda n, s: ctx.enter_context(nc.psum_tensor(n, s, F32))
            sem = lambda n: ctx.enter_context(nc.semaphore(n))
            w_rt = sb("w_rt", [P, KC, NR])
            zeros = sb("zeros", [P, NTILE])
            u4 = [sb(f"u4_{q}", [P, TPG, DM]) for q in range(2)]
            xn4 = [sb(f"xn4_{q}", [P, TPG, DM]) for q in range(2)]
            stat = [sb(f"stat{q}", [P, TPG, 6]) for q in range(2)]
            mv = [sb(f"mv{q}", [P, TPG, 2]) for q in range(2)]
            std = [sb(f"std{q}", [P, TPG]) for q in range(2)]
            rstd = [sb(f"rstd{q}", [P, TPG]) for q in range(2)]
            lgs = [sb(f"lgs{q}", [NR, GRP]) for q in range(2)]
            ps_t = [[ps(f"ps_t{q}{k}", [P, GRP]) for k in range(KC)] for q in range(2)]
            ps_l = [ps(f"ps_l{q}", [NR, GRP]) for q in range(2)]
            ps_lt = [ps(f"ps_lt{q}", [P, TPG, NR]) for q in range(2)]
            w_here = sem("w_here")
            u_here = [sem(f"u_here{q}") for q in range(2)]
            xn_out = [sem(f"xn_out{q}") for q in range(2)]
            zeroed = sem("zeroed")
            c_ident0 = sem("c_ident0")
            c_ident = sem("c_ident")
            c_zero = sem("c_zero")
            stats_done = sem("stats_done")
            mv_done = sem("mv_done")
            std_done = sem("std_done")
            rstd_done = sem("rstd_done")
            xn_done = sem("xn_done")
            tr_done = sem("tr_done")
            xnT_act = sem("xnT_act")
            xnT_dve = sem("xnT_dve")
            lg_done = sem("lg_done")
            lgs_done = sem("lgs_done")
            lt_done = sem("lt_done")
            lt_read = sem("lt_read")
            block = ctx.enter_context(nc.Block())

            @block.gpsimd
            def _(pool):
                pool.memset(ident[:], 0.0).then_inc(c_ident0, 1)
                pool.memset(ones[:], 1.0)
                pool.memset(eps[:, 0:1], EPS_LN)
                pool.memset(eps[:, 1:2], EPS_RMS)
                pool.wait_ge(c_ident0, 1)
                pool.affine_select(out=ident[:], in_=ident[:], compare_op=ALU.not_equal, fill=1.0, base=0,
                                   pattern=[[-1, P]], channel_multiplier=1).then_inc(c_ident, 1)

            @block.sync
            def _(sp):
                for k in range(KC):
                    sp.dma_start(w_rt[:, k, 0:E], gate_w[k * P:(k + 1) * P, :]).then_inc(w_here, 16)
                    sp.dma_start(w_rt[:, k, E:NR], w_in[k * P:(k + 1) * P, 2 * DI + 2 * NS:]).then_inc(w_here, 16)
                for g in range(2):
                    sp.dma_start(u4[g][:], group_rows(u_rows, g)).then_inc(u_here[g], 16)

                def step(g, q, more=True):
                    sp.wait_ge(xn_done, g + 1)
                    sp.dma_start(group_rows(xn_d, g), xn4[q][:]).then_inc(xn_out[q], 16)
                    if more:
                        sp.dma_start(u4[q][:], group_rows(u_rows, g + 2)).then_inc(u_here[q], 16)

                with sp.Fori(0, NG // 2 - 1) as i:
                    step(2 * i, 0)
                    step(2 * i + 1, 1)
                for g in range(NG - 2, NG):
                    step(g, g % 2, more=False)
                for q in range(2):
                    sp.wait_ge(xn_out[q], 16 * (NG // 2))

            @block.vector
            def _(dve):
                dve.memset(zeros[:], 0.0).then_inc(c_zero, 1)

                def normalise(g, q):
                    dve.wait_ge(u_here[q], times(1, g, q, 1))
                    for a in range(TPG):
                        last = dve.bn_stats(stat[q][:, a, :], u4[q][:, a, :])
                    last.then_inc(stats_done, 1)
                    ge_apart(dve, c_zero, (stats_done, g + 1))
                    for a in range(TPG):
                        last = dve.bn_aggr(mv[q][:, a, :], stat[q][:, a, :])
                    last.then_inc(mv_done, 1)

                def finish(g, q):
                    dve.wait_ge(std_done, g + 1)
                    dve.reciprocal(rstd[q][:], std[q][:]).then_inc(rstd_done, 1)
                    dve.wait_ge(rstd_done, g + 1)
                    ge(dve, xn_out[q], times(1, g, q, 0))
                    ge(dve, tr_done, g - 1)
                    for a in range(TPG):
                        last = dve.tensor_scalar(xn4[q][:, a, :], u4[q][:, a, :], mv[q][:, a, 0:1],
                                                 rstd[q][:, a:a + 1], ALU.subtract, ALU.mult)
                    last.then_inc(xn_done, 1)

                def take_back(g, q):
                    dve.wait_ge(tr_done, g + 1)
                    dve.tensor_copy(xnT[:, 1, ds(g * GRP, GRP)], ps_t[q][1][:]).then_inc(xnT_dve, 1)

                def logits_out(g, q):
                    dve.wait_ge(lt_done, g + 1)
                    dve.tensor_copy(logits[:, :, ds(g * TPG, TPG)],
                                    ps_lt[q][:].rearrange("p a e -> p e a")).then_inc(lt_read, 1)

                def step(g, q):
                    normalise(g, q)
                    if reached(g, 1):
                        take_back(g - 1, 1 - q)
                    finish(g, q)
                    if reached(g, 4):
                        logits_out(g - 4, q)

                steps(dve, 0, NG, step, peel=6)
                take_back(NG - 1, 1)
                for g in range(NG - 4, NG):
                    logits_out(g, g % 2)

            @block.scalar
            def _(act):
                act.wait_ge(c_zero, 1)
                act.dma_start(tok_d.rearrange("(p r) o -> p (r o)", p=P), zeros[:]).then_inc(zeroed, 16)
                act.wait_ge(c_ident, 1)

                def stdev(g, q):
                    act.wait_ge(mv_done, g + 1)
                    act.activation(std[q][:], mv[q][:, :, 1], ACT.Sqrt, bias=eps[:, 0:1]).then_inc(std_done, 1)

                def take_back(g, q):
                    act.wait_ge(tr_done, g + 1)
                    act.activation(xnT[:, 0, ds(g * GRP, GRP)], ps_t[q][0][:], ACT.Copy).then_inc(xnT_act, 1)

                def logits_back(g, q):
                    act.wait_ge(lg_done, g + 1)
                    ge(act, lt_done, g - 1)
                    act.activation(lgs[q][:], ps_l[q][:], ACT.Copy).then_inc(lgs_done, 1)

                def step(g, q):
                    stdev(g, q)
                    if reached(g, 1):
                        take_back(g - 1, 1 - q)
                    if reached(g, 3):
                        logits_back(g - 3, 1 - q)

                steps(act, 0, NG, step, peel=6)
                take_back(NG - 1, 1)
                for g in range(NG - 3, NG):
                    logits_back(g, g % 2)
                act.wait_ge(zeroed, 16)

            @block.tensor
            def _(pe):
                pe.wait_ge(c_ident, 1)
                pe.wait_ge(w_here, 64)

                def turn(g, q):
                    pe.wait_ge(xn_done, g + 1)
                    ge(pe, xnT_act, g - 1)
                    ge(pe, xnT_dve, g - 1)
                    for a in range(TPG):
                        for k in range(KC):
                            last = pe.transpose(ps_t[q][k][:, a * P:(a + 1) * P], xn4[q][:, a, k * P:(k + 1) * P],
                                                ident[:])
                    last.then_inc(tr_done, 1)

                def product(g, q):
                    pe.wait_ge(xnT_act, g + 1)
                    pe.wait_ge(xnT_dve, g + 1)
                    ge(pe, lgs_done, g - 1)
                    for k in range(KC):
                        last = pe.matmul(ps_l[q][:], w_rt[:, k, :], xnT[:, k, ds(g * GRP, GRP)],
                                         start=(k == 0), stop=(k == KC - 1))
                    last.then_inc(lg_done, 1)

                def turn_logits(g, q):
                    ge_apart(pe, c_ident, (lgs_done, g + 1), (lt_read, g - 1))
                    for a in range(TPG):
                        last = pe.transpose(ps_lt[q][:, a, :], lgs[q][:, a * P:(a + 1) * P], ident[0:NR, 0:NR])
                    last.then_inc(lt_done, 1)

                def step(g, q):
                    turn(g, q)
                    if reached(g, 2):
                        product(g - 2, q)
                    if reached(g, 3):
                        turn_logits(g - 3, 1 - q)

                steps(pe, 0, NG, step, peel=6)
                product(NG - 2, 0)
                turn_logits(NG - 3, 1)
                product(NG - 1, 1)
                turn_logits(NG - 2, 0)
                turn_logits(NG - 1, 1)

        tokf = keep("tokf", [P, NT])
        with ExitStack() as ctx:
            sb = lambda n, s, d=F32: ctx.enter_context(nc.sbuf_tensor(n, s, d))
            ps = lambda n, s: ctx.enter_context(nc.psum_tensor(n, s, F32))
            sem = lambda n: ctx.enter_context(nc.semaphore(n))
            two = lambda n, s, d=F32: [sb(f"{n}{q}", s, d) for q in range(2)]
            win = sb("win", [P, KC, 2 * DI + 2 * NS])
            wo = sb("wo", [P, H, DM])
            cw = sb("cw", [P, XB + 1, 4])
            cb = sb("cb", [P, XB + 1])
            rw = sb("rw", [P, H])
            dsk = sb("dsk", [P, H])
            cin = sb("cin", [P, XB + 1, 3 + SEQ])
            cacc = two("cacc", [P, GRP])
            xc = two("xc", [P, XB, GRP])
            bmat = two("bmat", [NS, GRP])
            cmat = two("cmat", [NS, GRP])
            gate = two("gate", [P, H, P])
            dbc = two("dbc", [P, H, P])
            L = sb("L", [P, H, P])
            lin = two("lin", [NS, H, P])
            first = sb("first", [NS, H, P])
            eye4 = sb("eye4", [P, H, P])
            eyeD = sb("eyeD", [P, H, P])
            M = two("M", [P, H, P])
            xtok = two("xtok", [P, H, P])
            btok = two("btok", [P, NS])
            CL = two("CL", [NS, H, P])
            BL = two("BL", [P, H, NS])
            yg = sb("yg", [P, H, P])
            ysq = sb("ysq", [P, H, P])
            state = sb("state", [NS, H, P])
            sout = two("sout", [P, DM])
            sidx = two("sidx", [P, 2], U32)
            sval = two("sval", [P, 1])
            score = logits[:, 0:E, :]
            big = lambda i: scratch[:, NR * NT + i * E * NT:NR * NT + (i + 1) * E * NT].rearrange(
                "p (e j) -> p e j", e=E)
            score2, iota_e, hot0, hot1, tmp, cum = [big(i) for i in range(6)]
            hot = [hot0, hot1]
            spare = scratch[:, (NR + 6 * E) * NT:]
            best = spare[:, 0:2 * NT].rearrange("p (c j) -> p c j", c=2)
            pick, den, slot_f = [spare[:, (2 + i) * NT:(3 + i) * NT] for i in range(3)]
            before, count, tiles, tiles_in, offset, tiles_f = [
                spare[:, 5 * NT + i * E:5 * NT + (i + 1) * E] for i in range(6)]
            tiles_i = tiles_f.bitcast(I32)
            iota_t = spare[0:1, 5 * NT + 6 * E:5 * NT + 6 * E + NTILE]
            passed = scratch[0:1, 0:NTILE * E].rearrange("p (t e) -> p t e", e=E)
            owner, owner2 = [tmp[0:1].rearrange("p e j -> p (e j)")[:, i * NTILE:(i + 1) * NTILE] for i in range(2)]
            assert NTILE * E <= (NR + E) * NT
            tri = sb("tri", [P, P])
            dtb = sb("dtb", [P, H])
            alog = sb("alog", [P, H])
            arate = sb("arate", [P, H])
            halves = [t[:].rearrange("p h t -> p (h t)")[:, i * NT * H:(i + 1) * NT * H]
                      for t in (L, M[0], M[1], yg) for i in range(2)]
            dtx, dta, dte, dts, dtq, dtp, dec = [t.rearrange("p (j h) -> p j h", h=H) for t in halves[0:7]]
            dec_flat = halves[6]
            decT = ysq[:, 0:2, :]
            ps_p = [ps(f"ps_p{q}", [P, GRP]) for q in range(2)]
            ps_x = ps("ps_x", [P, H, P])
            ps_bg = ps("ps_bg", [P, GRP])
            ps_y = ps("ps_y", [P, H, P])
            ps_s = ps("ps_s", [P, H, P])
            ps_o = ps("ps_o", [P, GRP])
            ps_z = ps("ps_z", [P, H, P])
            w_here = sem("w_here3")
            exp_here = sem("exp_here")
            p_here = sem("p_here")
            c_tri = sem("c_tri")
            c_iota = sem("c_iota")
            scored = sem("scored")
            abs_done = sem("abs_done")
            exp_done = sem("exp_done")
            rate_exp = sem("rate_exp")
            log_done = sem("log_done")
            dec_done = sem("dec_done")
            dec_turned = sem("dec_turned")
            decT_done = sem("decT_done")
            dec_out = sem("dec_out")
            counted = sem("counted")
            summed = sem("summed")
            counts_read = sem("counts_read")
            slots_done = sem("slots_done")
            routed = sem("routed")
            dve_seq = sem("dve_seq")
            dec_here = [sem(f"dec_here{q}") for q in range(2)]
            s_out = [sem(f"s_out{q}") for q in range(2)]
            scattered = [sem(f"scattered{q}") for q in range(2)]
            idx_done = sem("idx_done")
            consts = sem("consts")
            wo_done = sem("wo_done")
            eye_done = sem("eye_done")
            projected = sem("projected")
            cin_done = sem("cin_done")
            conv_seq = sem("conv_seq")
            conv_done = sem("conv_done")
            silu_done = sem("silu_done")
            turned = sem("turned")
            xtok_done = sem("xtok_done")
            btok_done = sem("btok_done")
            z_done = sem("z_done")
            gate_done = sem("gate_done")
            d_seq = sem("d_seq")
            L_done = sem("L_done")
            lin_done = sem("lin_done")
            M_done = sem("M_done")
            MD_done = sem("MD_done")
            CL_done = sem("CL_done")
            BL_done = sem("BL_done")
            y_done = sem("y_done")
            s_done = sem("s_done")
            st_done = sem("st_done")
            yg_done = sem("yg_done")
            ysq_done = sem("ysq_done")
            o_done = sem("o_done")
            sout_done = sem("sout_done")
            block = ctx.enter_context(nc.Block())
            NB = XB + 1
            ORDER = [XB] + list(range(XB))
            PBLK = [[0, 1], [2], [3], [4]]

            def turns_at(q, j):
                return (NB * q + j) % 2

            def some(n):
                return reached(n, 0)

            def chunks(p, k):
                return 4 * (p - 1) + k, 2 * (p - 1) + k // 2

            @block.sync
            def _(sp):
                for k in range(KC):
                    sp.dma_start(win[:, k, :], w_in[k * P:(k + 1) * P, 0:2 * DI + 2 * NS]).then_inc(w_here, 16)
                with nc.allow_non_contiguous_dma(reason="a few parameters per partition"):
                    sp.dma_start(cw[:], conv_w.rearrange("(b p) k -> p b k", p=P)).then_inc(w_here, 16)
                    sp.dma_start(cb[:], conv_b.rearrange("(b p) -> p b", p=P)).then_inc(w_here, 16)
                    sp.dma_start(rw[:], rms_w.rearrange("(h p) -> p h", p=P)).then_inc(w_here, 16)
                sp.dma_start(dtb[:], dt_bias.partition_broadcast(P)).then_inc(p_here, 16)
                sp.dma_start(alog[:], a_log.partition_broadcast(P)).then_inc(p_here, 16)
                sp.dma_start(dsk[:], d_skip.partition_broadcast(P)).then_inc(w_here, 16)
                sp.dma_start(wo[:], w_out.rearrange("(h p) d -> p h d", p=P)).then_inc(w_here, 16)

                sp.wait_ge(decT_done, 1)
                sp.dma_start(dec_d.rearrange("(c r) t -> r c t", r=P), decT).then_inc(dec_out, 16)
                sp.wait_ge(dec_out, 16)

                def load(n, before, q):
                    ge(sp, lin_done, n - 1)
                    sp.dma_start(dbc[q][:].rearrange("p h t -> p (h t)"),
                                 dec_d[ds(n * H, H), :].rearrange("h t -> (h t)").partition_broadcast(P)
                                 ).then_inc(dec_here[q], 16)

                def store(n, q):
                    sp.wait_ge(sout_done, n + 1)
                    sp.dma_start(s_d[ds(n * P, P), :], sout[q][:]).then_inc(s_out[q], 16)

                def step(p, _):
                    for k in range(4):
                        n, before = chunks(p, k)
                        load(n, before, k % 2)
                        if some(n - 3):
                            store(n - 3, 1 - k % 2)

                steps(sp, 1, NG + 1, step)
                for n in range(NT - 3, NT):
                    store(n, n % 2)
                sp.wait_ge(exp_here, 16 * 2 * KC)
                for q in range(2):
                    sp.wait_ge(s_out[q], 16 * (NT // 2))

            @block.gpsimd
            def _(pool):
                pool.memset(cin[:, :, 0:3], 0.0)
                pool.memset(first[:], 0.0).then_inc(consts, 1)
                pool.affine_select(out=tri[:], in_=ones[:], compare_op=ALU.is_gt, fill=0.0, base=0,
                                   pattern=[[1, P]], channel_multiplier=-1).then_inc(c_tri, 1)
                for h in range(H):
                    last = pool.tensor_copy(eye4[:, h, :], ident[:])
                last.then_inc(eye_done, 1)
                pool.iota(iota_e, pattern=[[1, E], [0, NT]], base=-E, channel_multiplier=0,
                          allow_small_or_imprecise_dtypes=True).then_inc(c_iota, 1)
                pool.iota(iota_t, pattern=[[1, NTILE]], base=0, channel_multiplier=0,
                          allow_small_or_imprecise_dtypes=True).then_inc(c_iota, 1)
                pool.iota(tokf[:], pattern=[[P, NT]], base=0, channel_multiplier=1,
                          allow_small_or_imprecise_dtypes=True).then_inc(c_iota, 1)
                pool.wait_ge(w_here, 16 * (KC + 5))
                for h in range(H):
                    last = pool.tensor_scalar(eyeD[:, h, :], ident[:], dsk[:, h:h + 1], None, ALU.mult)
                last.then_inc(eye_done, 1)
                pool.wait_ge(eye_done, 2)
                pool.wait_ge(c_iota, 3)

                def scatter(m, before, q):
                    ge(pool, scattered[q], 32 * before)
                    pool.tensor_copy(sidx[q][:], slot[:, :, ds(m, 1)].rearrange("p c o -> p (c o)"))
                    pool.tensor_copy(sval[q][:], tokf[:, ds(m, 1)]).then_inc(idx_done, 1)
                    ge_apart(pool, eye_done, (idx_done, m + 1))
                    for c in range(2):
                        pool.indirect_dma_start(
                            out=tok_d, out_offset=bass.IndirectOffsetOnAxis(ap=sidx[q][:, c:c + 1], axis=0),
                            in_=sval[q][:], in_offset=None).then_inc(scattered[q], 16)

                def step(p, _):
                    for k in range(4):
                        n, before = chunks(p, k)
                        q = k % 2
                        pool.wait_ge(silu_done, (XB + 2) * p)
                        pool.wait_ge(lin_done, n + 1)
                        ge(pool, y_done, n - 1)
                        pool.tensor_tensor(CL[q][:], lin[q][:],
                                           cmat_of[0](p)[:, k * P:(k + 1) * P].unsqueeze(1).broadcast_to([NS, H, P]),
                                           ALU.mult).then_inc(CL_done, 1)
                        pool.wait_ge(btok_done, n + 1)
                        ge(pool, s_done, n - 1)
                        pool.tensor_tensor(BL[q][:], L[:, :, P - 1:P].broadcast_to([P, H, NS]),
                                           btok[q][:].unsqueeze(1).broadcast_to([P, H, NS]),
                                           ALU.mult).then_inc(BL_done, 1)
                        pool.wait_ge(M_done, n + 1)
                        pool.tensor_tensor(M[q][:], M[q][:], eyeD[:], ALU.add).then_inc(MD_done, 1)
                        if isinstance(p, int) and p == 3:
                            if k == 0:
                                pool.wait_ge(slots_done, 1)
                            for m in range(3 * k, 3 * k + 3):
                                scatter(m, m // 2, m % 2)
                        elif reached(p, 4):
                            scatter(n, before, q)

                cmat_of = [None]

                def with_parity(p, q):
                    cmat_of[0] = lambda _: cmat[1 - q]
                    step(p, q)

                steps(pool, 1, NG + 1, with_parity)
                for q in range(2):
                    pool.wait_ge(scattered[q], 16 * NT)

            @block.scalar
            def _(act):
                act.wait_ge(consts, 1)
                act.activation(score, score, ACT.Sigmoid).then_inc(scored, 1)
                act.wait_ge(p_here, 32)
                act.activation(arate[:], alog[:], ACT.Exp).then_inc(rate_exp, 1)

                def experts_in():
                    act.wait_ge(routed, 1)
                    for k in range(KC):
                        rows = slice(k * P, (k + 1) * P)
                        act.dma_start(wgu[:, k, :, 0:MF], w_gate[:, rows, :].rearrange("e p m -> p e m")
                                      ).then_inc(exp_here, 16)
                        act.dma_start(wgu[:, k, :, MF:2 * MF], w_up[:, rows, :].rearrange("e p m -> p e m")
                                      ).then_inc(exp_here, 16)

                def evac(p, q, j):
                    b = ORDER[j]
                    act.wait_ge(projected, NB * p + j + 1)
                    ge(act, conv_done, NB * (p - 1) + j + 1)
                    act.activation(cin[:, b, 3 + q * GRP:3 + (q + 1) * GRP], ps_p[turns_at(q, j)][:], ACT.Copy)
                    ge(act, silu_done, (XB + 2) * p + j if j >= 2 else (XB + 2) * p - 1 + j)
                    act.activation(cacc[turns_at(q, j)][:], ps_p[turns_at(q, j)][:], ACT.Identity,
                                   bias=cb[:, b:b + 1], scale=cw[:, b, 3:4]).then_inc(cin_done, 1)

                def silu(p, q, j):
                    if j == 0:
                        ge(act, turned, 4 * (p - 1))
                        ge(act, CL_done, 4 * (p - 1))
                    act.wait_ge(conv_done, NB * p + j + 1)
                    src = cacc[turns_at(q, j)]
                    if ORDER[j] < XB:
                        act.activation(xc[q][:, ORDER[j], :], src[:], ACT.Silu).then_inc(silu_done, 1)
                    else:
                        act.activation(bmat[q][:], src[0:NS, :], ACT.Silu).then_inc(silu_done, 1)
                        act.activation(cmat[q][:], src[NS:2 * NS, :], ACT.Silu).then_inc(silu_done, 1)

                def token_side(n, q):
                    act.wait_ge(turned, n + 1)
                    ge(act, s_done, n - 1)
                    ge(act, BL_done, n - 1)
                    act.activation(btok[q][:], ps_bg[:, 0:NS], ACT.Copy).then_inc(btok_done, 1)
                    act.activation(xtok[q][:], ps_x[:], ACT.Copy).then_inc(xtok_done, 1)

                def gates(n, q):
                    act.wait_ge(z_done, n + 1)
                    ge(act, yg_done, n - 1)
                    act.activation(gate[q][:], ps_z[:], ACT.Tanh, scale=0.5).then_inc(gate_done, 1)

                def square(n):
                    act.wait_ge(yg_done, n + 1)
                    ge(act, o_done, n)
                    act.activation(ysq[:], ps_y[:], ACT.Square).then_inc(ysq_done, 1)

                def result(n, before, q):
                    act.wait_ge(o_done, n + 1)
                    ge(act, s_out[q], 16 * before)
                    act.activation(ms_all[:, ds(n, 1)], ps_o[:, DM:DM + 1], ACT.Copy)
                    act.activation(sout[q][:], ps_o[:, 0:DM], ACT.Copy).then_inc(sout_done, 1)

                def step(p, q, proj=True, scan=True):
                    for k in range(4):
                        n, before = chunks(p, k)
                        if scan:
                            token_side(n, k % 2)
                            if some(n - 1):
                                gates(n - 1, 1 - k % 2)
                            if some(n - 2):
                                result(n - 2, before - 1, k % 2)
                        if proj:
                            for j in PBLK[k]:
                                evac(p, q, j)
                        if scan and some(n - 1):
                            square(n - 1)
                        if not scan and k == 0:
                            act.wait_ge(abs_done, 1)
                            act.activation(dte, dta, ACT.Exp, scale=-1.0).then_inc(exp_done, 1)
                        if not scan and k == 1:
                            act.wait_ge(log_done, 1)
                            act.activation(dec, dta, ACT.Exp, scale=-1.0).then_inc(dec_done, 1)
                        if not scan and k == 2:
                            act.wait_ge(dec_turned, 1)
                            act.activation(decT, ps_s[:, 0:2, :], ACT.Copy).then_inc(decT_done, 1)
                        if proj:
                            for j in PBLK[k]:
                                silu(p, q, j)
                    if isinstance(p, int) and p == 3:
                        experts_in()

                step(0, 0, scan=False)
                steps(act, 1, NG, step)
                step(NG, 0, proj=False)
                gates(NT - 1, 1)
                square(NT - 1)
                result(NT - 2, NT // 2 - 1, 0)
                result(NT - 1, NT // 2 - 1, 1)

            @block.vector
            def _(dve):
                dve.wait_ge(w_here, 16 * (KC + 5))
                for h in range(H):
                    last = dve.tensor_scalar(wo[:, h, :], wo[:, h, :], rw[:, h:h + 1], 0.5, ALU.mult, ALU.mult)
                last.then_inc(wo_done, 1)
                dve.wait_ge(eye_done, 1)

                seq = [0]

                def link(ins):
                    seq[0] += 1
                    ins.then_inc(dve_seq, 1)
                    dve.wait_ge(dve_seq, seq[0])

                bc = [P, NT, H]

                def step_size_in():
                    dve.wait_ge(p_here, 32)
                    link(dve.tensor_tensor(dtx, logits[:, E:NR, :].rearrange("p h j -> p j h"),
                                           dtb[:].unsqueeze(1).broadcast_to(bc), ALU.add))
                    dve.scalar_tensor_tensor(dta, dtx, -1.0, dtx, ALU.mult, ALU.max).then_inc(abs_done, 1)

                def step_size_out():
                    dve.wait_ge(exp_done, 1)
                    link(dve.tensor_scalar(dtp, dte, 2.0, None, ALU.add))
                    link(dve.reciprocal(dtp, dtp))
                    link(dve.tensor_tensor(dts, dte, dtp, ALU.mult))
                    link(dve.tensor_tensor(dtq, dts, dts, ALU.mult))
                    link(dve.tensor_scalar(dtp, dtq, 1.0 / 17, None, ALU.mult))
                    for c in (15, 13, 11, 9, 7, 5, 3):
                        link(dve.scalar_tensor_tensor(dtp, dtp, 1.0 / c, dtq, ALU.add, ALU.mult))
                    link(dve.scalar_tensor_tensor(dts, dtp, 1.0, dts, ALU.add, ALU.mult))
                    link(dve.tensor_scalar(dts, dts, 2.0, None, ALU.mult))
                    link(dve.scalar_tensor_tensor(dtx, dtx, 0.0, dts, ALU.max, ALU.add))
                    dve.wait_ge(rate_exp, 1)
                    dve.tensor_tensor(dta, dtx, arate[:].unsqueeze(1).broadcast_to(bc), ALU.mult
                                      ).then_inc(log_done, 1)

                def choose(c, src):
                    by_tok = [P, E, NT]
                    link(dve.tensor_reduce(best[:, c, :], src.rearrange("p e j -> p j e"), AX.X, ALU.max))
                    link(dve.tensor_tensor(tmp, src, best[:, c, :].unsqueeze(1).broadcast_to(by_tok), ALU.is_equal))
                    link(dve.tensor_tensor(tmp, tmp, iota_e, ALU.mult))
                    link(dve.tensor_reduce(pick, tmp.rearrange("p e j -> p j e"), AX.X, ALU.min))
                    link(dve.tensor_tensor(hot[c], iota_e, pick.unsqueeze(1).broadcast_to(by_tok), ALU.is_equal))

                def first_choice():
                    dve.wait_ge(scored, 1)
                    dve.wait_ge(c_iota, 3)
                    choose(0, score)
                    link(dve.scalar_tensor_tensor(score2, hot[0], -4.0, score, ALU.mult, ALU.add))

                def second_choice():
                    choose(1, score2)
                    link(dve.tensor_tensor(den, best[:, 0, :], best[:, 1, :], ALU.add))
                    link(dve.tensor_scalar(den, den, 1e-20, None, ALU.add))
                    link(dve.reciprocal(den, den))
                    for c in range(2):
                        link(dve.tensor_tensor(wtop[:, c, :], best[:, c, :], den, ALU.mult))
                    link(dve.tensor_scalar(wtop[:], wtop[:], SCALE, None, ALU.mult))

                def count_choices():
                    link(dve.tensor_tensor(tmp, hot[0], hot[1], ALU.add))
                    flat = lambda t: t.rearrange("p e j -> p (e j)")
                    link(dve.tensor_tensor_scan(flat(cum), flat(tmp), flat(tmp), 0.0, ALU.add, ALU.max))
                    link(dve.memset(before, 0.0))
                    link(dve.tensor_copy(before[:, 1:E], cum[:, 0:E - 1, NT - 1]))
                    dve.tensor_tensor(count, cum[:, :, NT - 1], before, ALU.subtract).then_inc(counted, 1)
                    dve.wait_ge(counted, 1)
                    link(dve.tensor_tensor(cum, cum, tmp, ALU.subtract))

                def place_experts():
                    dve.wait_ge(summed, 1)
                    link(dve.tensor_scalar(tiles_i, ps_s[:, 1, 0:E], float(P - 1), None, ALU.add))
                    link(dve.tensor_scalar(tiles_i, tiles_i, 7, None, ALU.logical_shift_right))
                    link(dve.tensor_copy(tiles, tiles_i))
                    link(dve.tensor_tensor_scan(tiles_in, tiles, tiles, 0.0, ALU.add, ALU.max))
                    link(dve.tensor_tensor(offset, tiles_in, tiles, ALU.subtract))
                    link(dve.scalar_tensor_tensor(offset, offset, float(P), ps_s[:, 0, 0:E], ALU.mult, ALU.add))
                    dve.tensor_tensor(offset, offset, before, ALU.subtract).then_inc(counts_read, 1)
                    dve.wait_ge(counts_read, 1)
                    link(dve.tensor_tensor(cum, cum, offset.unsqueeze(2).broadcast_to([P, E, NT]), ALU.add))

                def place_tokens():
                    for c in range(2):
                        link(dve.tensor_tensor(tmp, hot[c], cum, ALU.mult))
                        link(dve.tensor_reduce(slot_f, tmp.rearrange("p e j -> p j e"), AX.X, ALU.add))
                        if c == 0:
                            link(dve.tensor_copy(slot[:, c, :], slot_f))
                    dve.tensor_copy(slot[:, 1, :], slot_f).then_inc(slots_done, 1)

                def own_tiles():
                    te = [1, NTILE, E]
                    link(dve.tensor_tensor(passed, tiles_in[0:1, :].unsqueeze(1).broadcast_to(te),
                                           iota_t.unsqueeze(2).broadcast_to(te), ALU.is_le))
                    link(dve.tensor_reduce(owner, passed, AX.X, ALU.add))
                    link(dve.tensor_scalar(owner2, owner, float(E - 1), None, ALU.min))
                    dve.tensor_copy(tile_expert[:], owner2).then_inc(routed, 1)

                def conv(p, q, j):
                    b = ORDER[j]
                    acc = cacc[turns_at(q, j)]
                    src = cin[:, b, q * GRP:q * GRP + GRP + 3]
                    dve.wait_ge(cin_done, NB * p + j + 1)
                    for t in range(3):
                        if t > 0:
                            dve.wait_ge(conv_seq, 2 * (NB * p + j) + t)
                        dve.scalar_tensor_tensor(acc[:], src[:, t:t + GRP], cw[:, b, t:t + 1], acc[:], ALU.mult,
                                                 ALU.add).then_inc(conv_seq if t < 2 else conv_done, 1)

                def scans(n, before, q):
                    dve.wait_ge(dec_here[q], 16 * before + 16)
                    ge(dve, lin_done, n)
                    dve.tensor_copy(first[:, :, 0], dbc[q][0:NS, :, 0]).then_inc(d_seq, 1)
                    dve.wait_ge(d_seq, 2 * n + 1)
                    dve.memset(dbc[q][:, :, 0], 0.0).then_inc(d_seq, 1)
                    dve.wait_ge(d_seq, 2 * n + 2)
                    row = lambda t: t.rearrange("p h t -> p (h t)")
                    ge(dve, BL_done, n)
                    ge(dve, M_done, n)
                    dve.tensor_tensor_scan(row(L[:]), row(dbc[q][:]), row(eye4[:]), 0.0, ALU.mult, ALU.add
                                           ).then_inc(L_done, 1)
                    ge(dve, CL_done, n - 1)
                    dve.tensor_tensor_scan(row(lin[q][:]), row(dbc[q][0:NS]), row(first[:]), 0.0, ALU.mult, ALU.add
                                           ).then_inc(lin_done, 1)

                def mix(n, q):
                    dve.wait_ge(btok_done, n + 1)
                    dve.wait_ge(L_done, n + 1)
                    ge(dve, y_done, n - 1)
                    dve.tensor_tensor(M[q][:], L[:], ps_bg[:, P:2 * P].unsqueeze(1).broadcast_to([P, H, P]),
                                      ALU.mult).then_inc(M_done, 1)

                def gated(n, q):
                    dve.wait_ge(y_done, n + 1)
                    dve.wait_ge(gate_done, n + 1)
                    ge(dve, o_done, n)
                    dve.scalar_tensor_tensor(yg[:], gate[q][:], 1.0, ps_y[:], ALU.add, ALU.mult).then_inc(yg_done, 1)

                def carry(n, q, fresh):
                    dve.wait_ge(s_done, n + 1)
                    ge(dve, st_done, n)
                    if fresh:
                        dve.tensor_copy(state[:], ps_s[0:NS]).then_inc(st_done, 1)
                        return
                    for h in range(H):
                        last = dve.scalar_tensor_tensor(state[:, h, :], state[:, h, :], lin[q][:, h, P - 1:P],
                                                        ps_s[0:NS, h, :], ALU.mult, ALU.add)
                    last.then_inc(st_done, 1)

                def step(p, q, proj=True, scan=True):
                    for k in range(4):
                        n, before = chunks(p, k)
                        if scan:
                            scans(n, before, k % 2)
                            mix(n, k % 2)
                        if not scan and k == 0:
                            step_size_in()
                        if not scan and k == 1:
                            step_size_out()
                        if isinstance(p, int) and p == 2 and k == 1:
                            place_experts()
                        if proj:
                            conv(p, q, PBLK[k][0])
                        if scan and some(n - 1):
                            gated(n - 1, 1 - k % 2)
                            carry(n - 1, 1 - k % 2, fresh=(q == 1 and k == 1))
                        if proj:
                            for j in PBLK[k][1:]:
                                conv(p, q, j)
                        if isinstance(p, int) and p == 1 and k == 0:
                            first_choice()
                        if isinstance(p, int) and p == 1 and k == 2:
                            second_choice()
                        if isinstance(p, int) and p == 2 and k == 0:
                            count_choices()
                        if isinstance(p, int) and p == 2 and k == 2:
                            place_tokens()
                        if isinstance(p, int) and p == 3 and k == 0:
                            own_tiles()

                step(0, 0, scan=False)
                steps(dve, 1, NG, step)
                step(NG, 0, proj=False)
                gated(NT - 1, 1)

            @block.tensor
            def _(pe):
                pe.wait_ge(w_here, 16 * (KC + 5))
                pe.wait_ge(wo_done, 1)

                def project(p, q, j):
                    b = ORDER[j]
                    ge(pe, cin_done, NB * p + j - 1)
                    for k in range(KC):
                        last = pe.matmul(ps_p[turns_at(q, j)][:], win[:, k, DI + b * P:DI + (b + 1) * P],
                                         xnT[:, k, ds(p * GRP, GRP)], start=(k == 0), stop=(k == KC - 1))
                    last.then_inc(projected, 1)

                def turn(p, q, n, k):
                    pe.wait_ge(silu_done, (XB + 2) * p)
                    ge(pe, xtok_done, n)
                    ge(pe, btok_done, n)
                    ge(pe, M_done, n)
                    t = slice(k * P, (k + 1) * P)
                    for b in range(XB):
                        pe.transpose(ps_x[:, b, :], xc[1 - q][:, b, t], ident[:])
                    pe.transpose(ps_bg[:, 0:NS], bmat[1 - q][:, t], ident[0:NS, 0:NS])
                    pe.matmul(ps_bg[:, P:2 * P], bmat[1 - q][:, t], cmat[1 - q][:, t], start=True, stop=True
                              ).then_inc(turned, 1)

                def zed(n):
                    ge(pe, gate_done, n)
                    for h in range(H):
                        for k in range(KC):
                            last = pe.matmul(ps_z[:, h, :], win[:, k, h * P:(h + 1) * P], xnT[:, k, ds(n * P, P)],
                                             start=(k == 0), stop=(k == KC - 1))
                    last.then_inc(z_done, 1)

                def mixed(n, q, fresh):
                    pe.wait_ge(MD_done, n + 1)
                    pe.wait_ge(xtok_done, n + 1)
                    pe.wait_ge(CL_done, n + 1)
                    ge(pe, st_done, n)
                    ge(pe, yg_done, n)
                    ge(pe, ysq_done, n)
                    for h in range(H):
                        last = pe.matmul(ps_y[:, h, :], xtok[q][:, h, :], M[q][:, h, :], start=True, stop=fresh)
                        if not fresh:
                            last = pe.matmul(ps_y[:, h, :], state[:, h, :], CL[q][:, h, :], start=False, stop=True)
                    last.then_inc(y_done, 1)

                def new_state(n, q):
                    pe.wait_ge(BL_done, n + 1)
                    for h in range(H):
                        last = pe.matmul(ps_s[0:NS, h, :], BL[q][:, h, :], xtok[q][:, h, :], start=True, stop=True)
                    last.then_inc(s_done, 1)

                def output(n):
                    pe.wait_ge(yg_done, n + 1)
                    pe.wait_ge(ysq_done, n + 1)
                    ge(pe, sout_done, n)
                    for h in range(H):
                        pe.matmul(ps_o[:, 0:DM], yg[:, h, :], wo[:, h, :], start=(h == 0), stop=(h == H - 1))
                    for h in range(H):
                        last = pe.matmul(ps_o[:, DM:DM + 1], ysq[:, h, :], ones[:, 0:1], start=(h == 0),
                                         stop=(h == H - 1))
                    last.then_inc(o_done, 1)

                def step(p, q, proj=True, scan=True):
                    for k in range(4):
                        n, _ = chunks(p, k)
                        if scan:
                            turn(p, q, n, k)
                            if some(n - 2):
                                output(n - 2)
                        if proj:
                            for j in PBLK[k]:
                                project(p, q, j)
                        if not scan and k == 2:
                            pe.wait_ge(dec_done, 1)
                            for c in range(2):
                                last = pe.transpose(ps_s[:, c, :], dec_flat[:, c * P:(c + 1) * P], ident[:])
                            last.then_inc(dec_turned, 1)
                        if scan:
                            if some(n - 1):
                                mixed(n - 1, 1 - k % 2, fresh=(q == 1 and k == 1))
                                if isinstance(p, int) and p == 2 and k == 1:
                                    pe.wait_ge(counts_read, 1)
                                new_state(n - 1, 1 - k % 2)
                            zed(n)
                            if isinstance(p, int) and p == 2 and k == 0:
                                pe.wait_ge(c_tri, 1)
                                pe.wait_ge(counted, 1)
                                ge(pe, st_done, n)
                                pe.matmul(ps_s[:, 0, 0:E], tri[:], count, start=True, stop=True)
                                pe.matmul(ps_s[:, 1, 0:E], ones[:], count, start=True, stop=True
                                          ).then_inc(summed, 1)

                step(0, 0, scan=False)
                steps(pe, 1, NG, step)
                step(NG, 0, proj=False)
                output(NT - 2)
                mixed(NT - 1, 1, fresh=False)
                output(NT - 1)

        NX = NTILE // TPG
        with ExitStack() as ctx:
            sb = lambda n, s, d=F32: ctx.enter_context(nc.sbuf_tensor(n, s, d))
            ps = lambda n, s: ctx.enter_context(nc.psum_tensor(n, s, F32))
            sem = lambda n: ctx.enter_context(nc.semaphore(n))
            two = lambda n, s, d=F32: [sb(f"{n}{q}", s, d) for q in range(2)]
            wd = sb("wd", [P, E, DM])
            x4 = two("x4", [P, TPG, DM])
            RT = NTILE // 2
            tok_rows = sb("tok_rows", [RT, 2, P])
            tok_all = sb("tok_all", [P, 2, RT], U32)
            gi4 = two("gi4", [P, TPG], U32)
            y4 = two("y4", [P, TPG, DM])
            xT = two("xT", [P, KC, P])
            sg = two("sg", [P, MF])
            hid = two("hid", [P, MF])
            hidT = two("hidT", [P, P])
            ps_t = [ps(f"px_t{q}", [P, KC, P]) for q in range(2)]
            ps_g = [ps(f"px_g{q}", [P, 2 * MF]) for q in range(2)]
            ps_h = [ps(f"px_h{q}", [P, P]) for q in range(2)]
            ps_y = [ps(f"px_y{q}", [P, DM]) for q in range(2)]
            wd_here = sem("wd_here")
            tr_here = sem("tr_here")
            tr_turned = sem("tr_turned")
            tok_done = sem("tok_done")
            gi_done = sem("gi4_done")
            x_here = [sem(f"x_here{q}") for q in range(2)]
            y_out = [sem(f"y_out{q}") for q in range(2)]
            x_turned = sem("x_turned")
            xT_done = sem("xT_done")
            gu_done = sem("gu_done")
            sg_done = sem("sg_done")
            hid_done = sem("hid_done")
            h_turned = sem("h_turned")
            hidT_done = sem("hidT_done")
            down_done = sem("down_done")
            y4_done = sem("y4_done")
            block = ctx.enter_context(nc.Block())

            @block.sync
            def _(sp):
                sp.dma_start(tok_rows[:], tok_d.rearrange("(c r p) o -> r c (p o)", c=2, p=P)).then_inc(tr_here, 16)
                sp.dma_start(wd[:], w_down.rearrange("e m d -> m e d")).then_inc(wd_here, 16)

                def store(p, q):
                    sp.wait_ge(y4_done, TPG * (p + 1))
                    sp.dma_start(group_rows(ys_d, p), y4[q][:]).then_inc(y_out[q], 16)

                steps(sp, 0, NX, store)
                for q in range(2):
                    sp.wait_ge(y_out[q], 16 * (NX // 2))

            @block.gpsimd
            def _(pool):
                pool.wait_ge(tok_done, 1)
                numbers = tok_all[:].rearrange("p c r -> p (c r)")

                def step(p, q):
                    ge(pool, x_here[q], times(TPG, p, q, 0))
                    pool.tensor_copy(gi4[q][:], numbers[:, ds(TPG * p, TPG)]).then_inc(gi_done, 1)
                    ge_apart(pool, tok_done, (gi_done, p + 1), (x_turned, TPG * (p - 1)))
                    for a in range(TPG):
                        pool.indirect_dma_start(
                            out=x4[q][:, a, :], out_offset=None, in_=xn_d,
                            in_offset=bass.IndirectOffsetOnAxis(ap=gi4[q][:, a:a + 1], axis=0)
                        ).then_inc(x_here[q], 16)

                steps(pool, 0, NX, step)

            @block.tensor
            def _(pe):
                def turn(p, q, a):
                    n = TPG * p + a
                    if a == 0:
                        pe.wait_ge(x_here[q], times(TPG, p, q, 1))
                    ge(pe, xT_done, n - 1)
                    for k in range(KC):
                        last = pe.transpose(ps_t[a % 2][:, k, :], x4[q][:, a, k * P:(k + 1) * P], ident[:])
                    last.then_inc(x_turned, 1)

                owners = [[pe.alloc_register(f"owner{q}{a}") for a in range(TPG)] for q in range(2)]

                def owner_of(q, a):
                    return pe.snap(owners[q][a], min_val=0, max_val=E - 1)

                def up(n, q, gq, a):
                    e = owner_of(gq, a)
                    pe.wait_ge(xT_done, n + 1)
                    ge(pe, hid_done, n - 1)
                    for k in range(KC):
                        last = pe.matmul(ps_g[q][:], xT[q][:, k, :], wgu[:, k, e, :], start=(k == 0),
                                         stop=(k == KC - 1))
                    last.then_inc(gu_done, 1)

                def turn_hidden(n, q):
                    pe.wait_ge(hid_done, n + 1)
                    ge(pe, hidT_done, n - 1)
                    pe.transpose(ps_h[q][:], hid[q][:], ident[:]).then_inc(h_turned, 1)

                def down(n, q, gq, a):
                    e = owner_of(gq, a)
                    pe.wait_ge(hidT_done, n + 1)
                    ge(pe, y4_done, n - 1)
                    pe.matmul(ps_y[q][:], hidT[q][:], wd[:, e, :], start=True, stop=True).then_inc(down_done, 1)

                def step(p, q):
                    pe.load(owners[q], tile_expert[0:1, ds(TPG * p, TPG)])
                    for a in range(TPG):
                        n = TPG * p + a
                        turn(p, q, a)
                        if some(n - 3):
                            down(n - 3, 1 - a % 2, q if a == 3 else 1 - q, (a + 1) % TPG)
                        if some(n - 1):
                            up(n - 1, 1 - a % 2, 1 - q if a == 0 else q, (a - 1) % TPG)
                        if some(n - 2):
                            turn_hidden(n - 2, a % 2)

                pe.wait_ge(tr_here, 16)
                for c in range(2):
                    last = pe.transpose(ps_t[0][:, c, 0:RT], tok_rows[:, c, :], ident[0:RT, 0:RT])
                last.then_inc(tr_turned, 1)
                pe.wait_ge(tok_done, 1)
                pe.wait_ge(wd_here, 16)
                steps(pe, 0, NX, step)
                down(NTILE - 3, 1, 1, 1)
                up(NTILE - 1, 1, 1, 3)
                turn_hidden(NTILE - 2, 0)
                down(NTILE - 2, 0, 1, 2)
                turn_hidden(NTILE - 1, 1)
                down(NTILE - 1, 1, 1, 3)

            @block.scalar
            def _(act):
                def xT_copy(n, q):
                    act.wait_ge(x_turned, n + 1)
                    ge(act, gu_done, n - 1)
                    act.activation(xT[q][:], ps_t[q][:], ACT.Copy).then_inc(xT_done, 1)

                def silu(n, q):
                    act.wait_ge(gu_done, n + 1)
                    ge(act, hid_done, n - 1)
                    act.activation(sg[q][:], ps_g[q][:, 0:MF], ACT.Silu).then_inc(sg_done, 1)

                def hidT_copy(n, q):
                    act.wait_ge(h_turned, n + 1)
                    ge(act, down_done, n - 1)
                    act.activation(hidT[q][:], ps_h[q][:], ACT.Copy).then_inc(hidT_done, 1)

                def step(p, q):
                    for a in range(TPG):
                        n = TPG * p + a
                        xT_copy(n, a % 2)
                        if some(n - 1):
                            silu(n - 1, 1 - a % 2)
                        if some(n - 2):
                            hidT_copy(n - 2, a % 2)

                steps(act, 0, NX, step)
                silu(NTILE - 1, 1)
                hidT_copy(NTILE - 2, 0)
                hidT_copy(NTILE - 1, 1)

            @block.vector
            def _(dve):
                def hidden(n, q):
                    dve.wait_ge(sg_done, n + 1)
                    ge(dve, h_turned, n - 1)
                    dve.tensor_tensor(hid[q][:], sg[q][:], ps_g[q][:, MF:2 * MF], ALU.mult).then_inc(hid_done, 1)

                def result(p, q, a, qa):
                    dve.wait_ge(down_done, TPG * p + a + 1)
                    if a == 0:
                        ge(dve, y_out[q], times(1, p, q, 0))
                    dve.tensor_copy(y4[q][:, a, :], ps_y[qa][:]).then_inc(y4_done, 1)

                def step(p, q):
                    for a in range(TPG):
                        n = TPG * p + a
                        if some(n - 1):
                            hidden(n - 1, 1 - a % 2)
                        if some(n - 3):
                            if a == 3:
                                result(p, q, 0, 0)
                            else:
                                result(p - 1, 1 - q, a + 1, (a + 1) % 2)

                dve.wait_ge(tr_turned, 1)
                dve.tensor_copy(tok_all[:], ps_t[0][:, :, 0:RT]).then_inc(tok_done, 1)
                steps(dve, 0, NX, step)
                result(NX - 1, 1, 1, 1)
                hidden(NTILE - 1, 1)
                result(NX - 1, 1, 2, 0)
                result(NX - 1, 1, 3, 1)

        with ExitStack() as ctx:
            sb = lambda n, s, d=F32: ctx.enter_context(nc.sbuf_tensor(n, s, d))
            ps = lambda n, s: ctx.enter_context(nc.psum_tensor(n, s, F32))
            sem = lambda n: ctx.enter_context(nc.semaphore(n))
            two = lambda n, s, d=F32: [sb(f"{n}{q}", s, d) for q in range(2)]
            wsg = sb("wsg", [P, KC, MF])
            wsu = sb("wsu", [P, KC, MF])
            wsd = sb("wsd", [MF, DM])
            msq = sb("msq", [P, NT])
            rms = sb("rms", [P, NT])
            u4 = two("fu4", [P, TPG, DM])
            s4 = two("fs4", [P, TPG, DM])
            o4 = two("fo4", [P, TPG, DM])
            RING = 2
            rows = [[[sb(f"rows{q}{a}{c}", [P, DM]) for c in range(2)] for a in range(TPG)] for q in range(RING)]
            hsg = two("hsg", [P, GRP])
            hs = two("hs", [P, GRP])
            acc = two("acc", [P, DM])
            gsil = two("gsil", [P, DM])
            gidx = [[sb(f"gidx{q}{a}", [P, 2], U32) for a in range(TPG)] for q in range(2)]
            ps_g = [ps(f"pf_g{q}", [P, GRP]) for q in range(2)]
            ps_u = [ps(f"pf_u{q}", [P, GRP]) for q in range(2)]
            ps_y = [ps(f"pf_y{q}", [P, DM]) for q in range(2)]
            ws_here = sem("ws_here")
            us_here = [sem(f"us_here{q}") for q in range(2)]
            rows_here = [[sem(f"rows_here{q}{a}") for a in range(TPG)] for q in range(2)]
            o_out = [sem(f"o_out{q}") for q in range(2)]
            gi_done = sem("gi_done")
            rms_done = sem("rms_done")
            rms_inv = sem("rms_inv")
            up_done = sem("up_done")
            hsg_done = sem("hsg_done")
            hs_done = sem("hs_done")
            dn_done = sem("dn_done")
            m_seq = sem("m_seq")
            acc_done = sem("acc_done")
            gs_done = sem("gs_done")
            sg_done = sem("fsg_done")
            o4_done = sem("o4_done")
            block = ctx.enter_context(nc.Block())

            @block.sync
            def _(sp):
                for k in range(KC):
                    sp.dma_start(wsg[:, k, :], ws_gate[k * P:(k + 1) * P, :]).then_inc(ws_here, 16)
                    sp.dma_start(wsu[:, k, :], ws_up[k * P:(k + 1) * P, :]).then_inc(ws_here, 16)
                sp.dma_start(wsd[:], ws_down).then_inc(ws_here, 16)

                def store(p, q):
                    sp.wait_ge(o4_done, TPG * (p + 1))
                    sp.dma_start(group_rows(out_rows, p), o4[q][:]).then_inc(o_out[q], 16)

                def step(p, q):
                    ge(sp, o4_done, TPG * (p - 1))
                    sp.dma_start(u4[q][:], group_rows(u_rows, p)).then_inc(us_here[q], 16)
                    sp.dma_start(s4[q][:], group_rows(s_d, p)).then_inc(us_here[q], 16)
                    if some(p - 2):
                        store(p - 2, q)

                steps(sp, 0, NG, step)
                store(NG - 2, 0)
                store(NG - 1, 1)
                for q in range(2):
                    sp.wait_ge(o_out[q], 16 * (NG // 2))

            @block.gpsimd
            def _(pool):
                def step(p, q):
                    for a in range(TPG):
                        ge(pool, rows_here[q][a], times(2, p, q, 0))
                        last = pool.tensor_copy(gidx[q][a][:], slot[:, :, ds(TPG * p + a, 1)].rearrange(
                            "p c o -> p (c o)"))
                    last.then_inc(gi_done, 1)
                    pool.wait_ge(gi_done, p + 1)
                    for a in range(TPG):
                        ge_apart(pool, gi_done, (acc_done, TPG * (p - 2) + a + 1))
                        for c in range(2):
                            pool.indirect_dma_start(
                                out=rows[q][a][c][:], out_offset=None, in_=ys_d,
                                in_offset=bass.IndirectOffsetOnAxis(ap=gidx[q][a][:, c:c + 1], axis=0)
                            ).then_inc(rows_here[q][a], 16)

                steps(pool, 0, NG, step)

            @block.tensor
            def _(pe):
                pe.wait_ge(ws_here, 16 * (2 * KC + 1))

                def up(p, q):
                    ge(pe, hs_done, p - 1)
                    for bank, w in ((ps_g, wsg), (ps_u, wsu)):
                        for k in range(KC):
                            last = pe.matmul(bank[q][:], w[:, k, :], xnT[:, k, ds(p * GRP, GRP)], start=(k == 0),
                                             stop=(k == KC - 1))
                    last.then_inc(up_done, 1)

                def down(p, q):
                    pe.wait_ge(hs_done, p + 1)
                    for a in range(TPG):
                        ge(pe, acc_done, TPG * p + a - 1)
                        pe.matmul(ps_y[a % 2][:], hs[q][:, a * P:(a + 1) * P], wsd[:], start=True, stop=True
                                  ).then_inc(dn_done, 1)

                def step(p, q):
                    up(p, q)
                    if some(p - 1):
                        down(p - 1, 1 - q)

                steps(pe, 0, NG, step)
                down(NG - 1, 1)

            @block.scalar
            def _(act):
                act.activation(rms[:], ms_all[:], ACT.Sqrt, bias=eps[:, 1:2], scale=1.0 / DI).then_inc(rms_done, 1)

                def silu_up(p, q):
                    act.wait_ge(up_done, p + 1)
                    ge(act, hs_done, p - 1)
                    act.activation(hsg[q][:], ps_g[q][:], ACT.Silu).then_inc(hsg_done, 1)

                def silu_out(n, q):
                    act.wait_ge(acc_done, n + 1)
                    ge(act, sg_done, n - 1)
                    act.activation(gsil[q][:], acc[q][:], ACT.Silu).then_inc(gs_done, 1)

                def step(p, q):
                    silu_up(p, q)
                    if some(p - 1):
                        for a in range(TPG):
                            silu_out(TPG * (p - 1) + a, a % 2)

                steps(act, 0, NG, step)
                for a in range(TPG):
                    silu_out(TPG * (NG - 1) + a, a % 2)

            @block.vector
            def _(dve):
                dve.wait_ge(rms_done, 1)
                dve.reciprocal(msq[:], rms[:]).then_inc(rms_inv, 1)
                dve.wait_ge(rms_inv, 1)

                def hidden(p, q):
                    dve.wait_ge(hsg_done, p + 1)
                    ge(dve, dn_done, TPG * (p - 1))
                    dve.tensor_tensor(hs[q][:], hsg[q][:], ps_u[q][:], ALU.mult).then_inc(hs_done, 1)

                def merge(p, q, a):
                    n = TPG * p + a
                    dve.wait_ge(dn_done, n + 1)
                    dve.wait_ge(rows_here[q][a], times(2, p, q, 1))
                    ge(dve, gs_done, n - 1)
                    y = acc[a % 2]
                    dve.scalar_tensor_tensor(y[:], rows[q][a][0][:], wtop[:, 0, ds(n, 1)], ps_y[a % 2][:], ALU.mult,
                                             ALU.add).then_inc(m_seq, 1)
                    dve.wait_ge(m_seq, n + 1)
                    dve.scalar_tensor_tensor(y[:], rows[q][a][1][:], wtop[:, 1, ds(n, 1)], y[:], ALU.mult,
                                             ALU.add).then_inc(acc_done, 1)

                def gate_out(p, q, a):
                    n = TPG * p + a
                    if a == 0:
                        dve.wait_ge(us_here[q], times(2, p, q, 1))
                        ge(dve, o_out[q], times(1, p, q, 0))
                    dve.wait_ge(gs_done, n + 1)
                    dve.scalar_tensor_tensor(o4[q][:, a, :], s4[q][:, a, :], msq[:, ds(n, 1)], gsil[a % 2][:],
                                             ALU.mult, ALU.mult).then_inc(sg_done, 1)
                    dve.wait_ge(sg_done, n + 1)
                    dve.tensor_tensor(o4[q][:, a, :], o4[q][:, a, :], u4[q][:, a, :], ALU.add).then_inc(o4_done, 1)

                def pair(p, q):
                    for a in range(TPG):
                        merge(p, q, a)
                        if a >= 1:
                            gate_out(p, q, a - 1)
                    gate_out(p, q, TPG - 1)

                def step(p, q):
                    hidden(p, q)
                    if some(p - 1):
                        pair(p - 1, 1 - q)

                steps(dve, 0, NG, step)
                pair(NG - 1, 1)


_INS = ['L0_attn_u', 'L0_attn_in_proj_w', 'L0_attn_conv_w', 'L0_attn_conv_b', 'L0_attn_dt_bias', 'L0_attn_A_log',
        'L0_attn_D', 'L0_attn_rms_w', 'L0_attn_out_w', 'L0_ffn_gate_w', 'L0_ffn_w_gate', 'L0_ffn_w_up',
        'L0_ffn_w_down', 'L0_ffn_ws_gate', 'L0_ffn_ws_up', 'L0_ffn_ws_down']
_TURNED = ('L0_attn_in_proj_w', 'L0_attn_out_w', 'L0_ffn_gate_w')


def kernel(**inputs):
    import numpy as _np
    import concourse.bacc as _bacc
    from concourse import mybir as _mybir
    from concourse.bass_utils import run_bass_kernel_spmd as _run

    nc = _bacc.Bacc("TRN2", target_bir_lowering=False, num_devices=1)
    arrays, args = {}, []
    for name in _INS:
        a = _np.asarray(inputs[name])
        a = _np.ascontiguousarray(a.T if name in _TURNED else a)
        arrays[f"in_{name}_dram"] = a
        args.append(nc.dram_tensor(f"in_{name}_dram", a.shape, _mybir.dt.from_np(a.dtype), kind="ExternalInput").ap())
    shape = inputs['L0_attn_u'].shape
    args.append(nc.dram_tensor("out_0_dram", shape, _mybir.dt.float32, kind="ExternalOutput").ap())
    bass_mixer_moe(nc, *args)
    r = _run(nc, [arrays], core_ids=[0])
    return r.results[0]["out_0_dram"]
```

```python
from contextlib import ExitStack

import concourse.bass as bass
from concourse import mybir

F32 = mybir.dt.float32
F16 = mybir.dt.float16
F32R = mybir.dt.float32r
I32 = mybir.dt.int32
U32 = mybir.dt.uint32
ACT = mybir.ActivationFunctionType
ALU = mybir.AluOpType
AX = mybir.AxisListType

P = 128
ds = bass.ds


def ge(eng, sem, value):
    if not isinstance(value, int) or value > 0:
        eng.wait_ge(sem, value)


def ge_apart(eng, passed, *waits):
    waits = [(sem, value if isinstance(value, int) else eng.to_reg(value)) for sem, value in waits]
    eng.wait_ge(passed, 1)
    for sem, value in waits:
        ge(eng, sem, value)


def times(dmas, p, q, now, period=2):
    if isinstance(p, int):
        return 16 * dmas * (p // period + now)
    return (p - q) * (16 // period * dmas) + 16 * dmas * now


def reached(p, least):
    return not isinstance(p, int) or p >= least


def steps(eng, first, last, body, peel=2, period=2):
    head = -(-(first + peel) // period) * period
    for p in range(first, head):
        body(p, p % period)
    tail = last - (last - head) % period
    with eng.Fori(head // period, tail // period) as i:
        for q in range(period):
            body(period * i + q, q)
    for p in range(tail, last):
        body(p, p % period)


def bass_mixer_moe(nc, u, w_in, conv_w, conv_b, dt_bias, a_log, d_skip, rms_w, w_out,
                   gate_w, w_gate, w_up, w_down, ws_gate, ws_up, ws_down, out):
    BATCH, SEQ, DM = u.shape
    E, _, MF = w_gate.shape
    H = dt_bias.shape[0]
    DI = w_out.shape[0]
    NS = (w_in.shape[1] - 2 * DI - H) // 2
    TOK = BATCH * SEQ
    KC = DM // P
    NT = TOK // P
    GRP = 512
    NG = TOK // GRP
    TPG = GRP // P
    XB = DI // P
    NR = E + H
    NTILE = 2 * NT + E
    TPB = SEQ // P
    EPS_LN = 1e-5
    EPS_RMS = 1e-5
    SCALE = 2.5
    HI, LO = 0, 1
    PARTS = ((HI, HI), (HI, LO), (LO, HI))
    WS = 64.0
    CIN = 2 * DI + 2 * NS
    assert DI // H == P and 2 * NS == P and MF == P and SEQ == 2 * GRP

    u_rows = u.rearrange("b l d -> (b l) d")
    out_rows = out.rearrange("b l d -> (b l) d")
    xn_d = nc.dram_tensor("xn_d", [TOK, 2 * DM], F16).ap()
    tok_d = nc.dram_tensor("tok_d", [NTILE * P, 1], F32).ap()
    ys_d = nc.dram_tensor("ys_d", [NTILE * P, DM], F32).ap()
    s_d = nc.dram_tensor("s_d", [TOK, DM], F32).ap()
    lin_d = nc.dram_tensor("lin_d", [NT * H, P], F32).ap()
    dec_d = nc.dram_tensor("dec_d", [NT * H, P], F32).ap()

    def split_product(pe, to, weight, moving):
        for k in range(KC):
            for n, (cw, cx) in enumerate(PARTS):
                last = pe.matmul(to, weight(cw, k), moving(cx, k), start=(k == 0 and n == 0),
                                 stop=(k == KC - 1 and n == len(PARTS) - 1))
        return last

    def split_rounds(pe, to, operand, weight, blocks):
        for b in range(blocks):
            for n, (co, cw) in enumerate(PARTS):
                last = pe.matmul(to, operand(co, b), weight(cw, b), start=(b == 0 and n == 0),
                                 stop=(b == blocks - 1 and n == len(PARTS) - 1))
        return last

    def group_rows(t, g):
        return t[ds(g * GRP, GRP), :].rearrange("(a p) d -> p a d", p=P)

    outer = ExitStack()
    with outer:
        def keep(name, shape, dt=F32):
            return outer.enter_context(nc.sbuf_tensor(name, shape, dt))

        xnT = keep("xnT", [P, KC, 2, TOK], F16)
        win = keep("win", [P, 2, KC, CIN], F16)
        ident16 = keep("ident16", [P, P], F16)
        ident = keep("ident", [P, P])
        ones = keep("ones", [P, P])
        slot = keep("slot", [P, 2, NT], U32)
        wtop = keep("wtop", [P, 2, NT])
        tile_expert = keep("tile_expert", [1, NTILE], I32)
        ms_all = keep("ms_all", [P, NT])
        eps = keep("eps", [P, 2])
        wo = keep("wo", [P, 2, H, DM], F32R)
        cw = keep("cw", [P, XB + 1, 4])
        cb = keep("cb", [P, XB + 1])
        cw3 = keep("cw3", [P, XB + 1])
        rw = keep("rw", [P, H])
        dsk = keep("dsk", [P, H])
        cin = keep("cin", [P, XB + 1, 3 + SEQ])
        cin_row = cin[:].rearrange("p b t -> p (b t)")
        wd = cin_row[:, 0:E * DM].rearrange("p (e d) -> p e d", e=E)
        tok_rows = keep("tok_rows", [NTILE // 2, 2, P])
        dtb = keep("dtb", [P, H])
        alog = keep("alog", [P, H])
        wbuf = keep("wbuf", [P, KC * E * 2 * MF])
        wgu16 = wbuf[:].bitcast(F16).rearrange("p (c k e m) -> p c k e m", c=2, k=KC, e=E)
        scratch = wbuf[:]
        logits = scratch[:, 0:NR * NT].rearrange("p (e j) -> p e j", e=NR)

        with ExitStack() as ctx:
            sb = lambda n, s, d=F32: ctx.enter_context(nc.sbuf_tensor(n, s, d))
            ps = lambda n, s: ctx.enter_context(nc.psum_tensor(n, s, F32))
            sem = lambda n: ctx.enter_context(nc.semaphore(n))
            w_raw = sb("w_raw", [P, KC, CIN + NR])
            wo_raw = sb("wo_raw", [P, H, DM])
            w_rt = sb("w_rt", [P, 2, KC, NR], F16)
            xh4 = [sb(f"xh4_{q}", [P, TPG, 2, DM], F16) for q in range(2)]
            zeros = sb("zeros", [P, NTILE])
            UB = 4
            u4 = [sb(f"u4_{r}", [P, TPG, DM]) for r in range(UB)]
            xn4 = [sb(f"xn4_{q}", [P, TPG, DM]) for q in range(2)]
            stat = [sb(f"stat{q}", [P, TPG, 6]) for q in range(2)]
            mv = [sb(f"mv{q}", [P, TPG, 2]) for q in range(2)]
            std = [sb(f"std{q}", [P, TPG]) for q in range(2)]
            rstd = [sb(f"rstd{q}", [P, TPG]) for q in range(2)]
            lgs = [sb(f"lgs{q}", [NR, GRP]) for q in range(2)]
            ps_t = [[ctx.enter_context(nc.psum_tensor(f"ps_t{q}{k}", [P, 2, GRP], F16)) for k in range(KC)]
                    for q in range(2)]
            ps_l = [ps(f"ps_l{q}", [NR, GRP]) for q in range(2)]
            ps_lt = [ps(f"ps_lt{q}", [P, TPG, NR]) for q in range(2)]
            w_here = sem("w_here")
            u_here = [sem(f"u_here{r}") for r in range(UB)]
            xn_out = [sem(f"xn_out{q}") for q in range(2)]
            zeroed = sem("zeroed")
            c_ident0 = sem("c_ident0")
            c_ident = sem("c_ident")
            c_zero = sem("c_zero")
            stats_done = sem("stats_done")
            mv_done = sem("mv_done")
            std_done = sem("std_done")
            rstd_done = sem("rstd_done")
            xn_done = sem("xn_done")
            hi_done = sem("hi_done")
            lo_done = sem("lo_done")
            whi_done = sem("whi_done")
            wlo_done = sem("wlo_done")
            c_ident16 = sem("c_ident16")
            p_here = sem("p_here")
            wo_done = sem("wo_done")
            wo_high = sem("wo_high")
            tr_done = sem("tr_done")
            xnT_done = sem("xnT_done")
            lg_done = sem("lg_done")
            lgs_done = sem("lgs_done")
            lt_done = sem("lt_done")
            lt_read = sem("lt_read")
            block = ctx.enter_context(nc.Block())

            @block.gpsimd
            def _(pool):
                pool.memset(ident[:], 0.0).then_inc(c_ident0, 1)
                pool.memset(ones[:], 1.0)
                pool.memset(eps[:, 0:1], EPS_LN)
                pool.memset(eps[:, 1:2], EPS_RMS)
                pool.wait_ge(c_ident0, 1)
                pool.affine_select(out=ident[:], in_=ident[:], compare_op=ALU.not_equal, fill=1.0, base=0,
                                   pattern=[[-1, P]], channel_multiplier=1).then_inc(c_ident, 1)
                pool.wait_ge(c_ident, 1)
                pool.tensor_copy(ident16[:], ident[:]).then_inc(c_ident16, 1)

                def low(g, q):
                    pool.wait_ge(hi_done, g + 1)
                    pool.tensor_tensor(xh4[q][:, :, LO, :], xn4[q][:], xh4[q][:, :, HI, :], ALU.subtract
                                       ).then_inc(lo_done, 1)

                steps(pool, 0, NG, low)

            @block.sync
            def _(sp):
                def load(g, r):
                    sp.dma_start(u4[r][:], group_rows(u_rows, g)).then_inc(u_here[r], 16)

                load(0, 0)
                for k in range(KC):
                    sp.dma_start(w_raw[:, k, 0:CIN], w_in[k * P:(k + 1) * P, 0:CIN]).then_inc(w_here, 16)
                    sp.dma_start(w_raw[:, k, CIN:CIN + E], gate_w[k * P:(k + 1) * P, :]).then_inc(w_here, 16)
                    sp.dma_start(w_raw[:, k, CIN + E:], w_in[k * P:(k + 1) * P, CIN:]).then_inc(w_here, 16)

                for g in range(1, UB):
                    load(g, g)
                with nc.allow_non_contiguous_dma(reason="a few parameters per partition"):
                    sp.dma_start(cw[:], conv_w.rearrange("(b p) k -> p b k", p=P)).then_inc(p_here, 16)
                    sp.dma_start(cb[:], conv_b.rearrange("(b p) -> p b", p=P)).then_inc(p_here, 16)
                    sp.dma_start(rw[:], rms_w.rearrange("(h p) -> p h", p=P)).then_inc(p_here, 16)
                sp.dma_start(dtb[:], dt_bias.partition_broadcast(P)).then_inc(p_here, 16)
                sp.dma_start(alog[:], a_log.partition_broadcast(P)).then_inc(p_here, 16)
                sp.dma_start(dsk[:], d_skip.partition_broadcast(P)).then_inc(p_here, 16)
                sp.dma_start(wo_raw[:], w_out.rearrange("(h p) d -> p h d", p=P)).then_inc(p_here, 16)

                def step(g, r):
                    q = r % 2
                    sp.wait_ge(xn_done, g + 1)
                    if not isinstance(g, int) or g + UB < NG:
                        load(g + UB, r)
                    sp.wait_ge(lo_done, g + 1)
                    sp.dma_start(group_rows(xn_d, g), xh4[q][:].rearrange("p a c d -> p a (c d)")
                                 ).then_inc(xn_out[q], 16)

                steps(sp, 0, NG - UB, step, peel=0, period=UB)
                for g in range(NG - UB, NG):
                    step(g, g % UB)
                for q in range(2):
                    sp.wait_ge(xn_out[q], 16 * (NG // 2))

            @block.vector
            def _(dve):
                dve.memset(zeros[:], 0.0).then_inc(c_zero, 1)

                def low_weights():
                    dve.wait_ge(whi_done, 1)
                    dve.scalar_tensor_tensor(win[:, LO], w_raw[:, :, 0:CIN], WS, win[:, HI], ALU.mult, ALU.subtract)
                    dve.scalar_tensor_tensor(w_rt[:, LO], w_raw[:, :, CIN:], WS, w_rt[:, HI], ALU.mult,
                                             ALU.subtract).then_inc(wlo_done, 1)

                def statistics(g, r):
                    q = r % 2
                    dve.wait_ge(u_here[r], times(1, g, r, 1, UB))
                    for a in range(TPG):
                        last = dve.bn_stats(stat[q][:, a, :], u4[r][:, a, :])
                    last.then_inc(stats_done, 1)
                    ge_apart(dve, c_zero, (stats_done, g + 1))
                    for a in range(TPG):
                        last = dve.bn_aggr(mv[q][:, a, :], stat[q][:, a, :])
                    last.then_inc(mv_done, 1)

                def normalise(g, r):
                    q = r % 2
                    dve.wait_ge(std_done, g + 1)
                    dve.reciprocal(rstd[q][:], std[q][:]).then_inc(rstd_done, 1)
                    dve.wait_ge(rstd_done, g + 1)
                    ge(dve, lo_done, g - 1)
                    for a in range(TPG):
                        last = dve.tensor_scalar(xn4[q][:, a, :], u4[r][:, a, :], mv[q][:, a, 0:1],
                                                 rstd[q][:, a:a + 1], ALU.subtract, ALU.mult)
                    last.then_inc(xn_done, 1)

                def logits_out(g, q):
                    dve.wait_ge(lt_done, g + 1)
                    dve.tensor_copy(logits[:, :, ds(g * TPG, TPG)],
                                    ps_lt[q][:].rearrange("p a e -> p e a")).then_inc(lt_read, 1)

                def step(g, r, more=True):
                    normalise(g, r)
                    if more:
                        statistics(g + 1, (r + 1) % UB)
                    if isinstance(g, int) and g == 0:
                        low_weights()
                    if reached(g, 4):
                        logits_out(g - 4, r % 2)

                statistics(0, 0)
                steps(dve, 0, NG - 1, step, peel=5, period=UB)
                step(NG - 1, (NG - 1) % UB, more=False)
                dve.wait_ge(p_here, 16 * 7)
                for h in range(H):
                    last = dve.tensor_scalar(wo_raw[:, h, :], wo_raw[:, h, :], rw[:, h:h + 1], 0.5, ALU.mult, ALU.mult)
                last.then_inc(wo_done, 1)
                dve.tensor_scalar(cw3[:], cw[:, :, 3], 1.0 / WS, None, ALU.mult)
                for g in range(NG - 4, NG):
                    logits_out(g, g % 2)
                dve.wait_ge(wo_high, 1)
                dve.tensor_tensor(wo[:, LO], wo_raw[:], wo[:, HI].bitcast(F32), ALU.subtract)

            @block.scalar
            def _(act):
                act.wait_ge(c_zero, 1)
                act.dma_start(tok_d.rearrange("(p r) o -> p (r o)", p=P), zeros[:]).then_inc(zeroed, 16)
                act.wait_ge(c_ident, 1)

                def stdev(g, q):
                    act.wait_ge(mv_done, g + 1)
                    act.activation(std[q][:], mv[q][:, :, 1], ACT.Sqrt, bias=eps[:, 0:1]).then_inc(std_done, 1)

                def high_weights():
                    act.wait_ge(w_here, 16 * 3 * KC)
                    act.activation(win[:, HI], w_raw[:, :, 0:CIN], ACT.Copy, scale=WS)
                    act.activation(w_rt[:, HI], w_raw[:, :, CIN:], ACT.Copy, scale=WS).then_inc(whi_done, 1)

                def high(g, q):
                    act.wait_ge(xn_done, g + 1)
                    ge(act, xn_out[q], times(1, g, q, 0))
                    ge(act, tr_done, g - 1)
                    act.activation(xh4[q][:, :, HI, :], xn4[q][:], ACT.Copy).then_inc(hi_done, 1)

                def take_back(g, q, k):
                    if k == 0:
                        act.wait_ge(tr_done, g + 1)
                    last = act.activation(xnT[:, k, :, ds(g * GRP, GRP)], ps_t[q][k][:], ACT.Copy)
                    if k == KC - 1:
                        last.then_inc(xnT_done, 1)

                def logits_back(g, q):
                    act.wait_ge(lg_done, g + 1)
                    ge(act, lt_done, g - 1)
                    act.activation(lgs[q][:], ps_l[q][:], ACT.Copy, scale=1.0 / WS).then_inc(lgs_done, 1)

                def step(g, q, more=True):
                    high(g, q)
                    if reached(g, 1):
                        take_back(g - 1, 1 - q, 0)
                    if more:
                        stdev(g + 1, 1 - q)
                    if isinstance(g, int) and g == 0:
                        high_weights()
                    if reached(g, 1):
                        for k in range(1, KC):
                            take_back(g - 1, 1 - q, k)
                    if reached(g, 3):
                        logits_back(g - 3, 1 - q)

                stdev(0, 0)
                steps(act, 0, NG - 1, step, peel=6)
                step(NG - 1, 1, more=False)
                for k in range(KC):
                    take_back(NG - 1, 1, k)
                act.wait_ge(wo_done, 1)
                act.activation(wo[:, HI], wo_raw[:], ACT.Copy).then_inc(wo_high, 1)
                for g in range(NG - 3, NG):
                    logits_back(g, g % 2)
                act.wait_ge(zeroed, 16)

            @block.tensor
            def _(pe):
                pe.wait_ge(c_ident16, 1)
                pe.wait_ge(c_ident, 1)

                def turn(g, q):
                    pe.wait_ge(lo_done, g + 1)
                    ge(pe, xnT_done, g - 1)
                    for a in range(TPG):
                        for k in range(KC):
                            for c in (HI, LO):
                                last = pe.transpose(ps_t[q][k][:, c, a * P:(a + 1) * P],
                                                    xh4[q][:, a, c, k * P:(k + 1) * P], ident16[:])
                    last.then_inc(tr_done, 1)

                def product(g, q):
                    pe.wait_ge(xnT_done, g + 1)
                    pe.wait_ge(wlo_done, 1)
                    ge(pe, lgs_done, g - 1)
                    last = split_product(pe, ps_l[q][:], lambda c, k: w_rt[:, c, k, :],
                                         lambda c, k: xnT[:, k, c, ds(g * GRP, GRP)])
                    last.then_inc(lg_done, 1)

                def turn_logits(g, q):
                    ge_apart(pe, c_ident, (lgs_done, g + 1), (lt_read, g - 1))
                    for a in range(TPG):
                        last = pe.transpose(ps_lt[q][:, a, :], lgs[q][:, a * P:(a + 1) * P], ident[0:NR, 0:NR])
                    last.then_inc(lt_done, 1)

                def step(g, q):
                    turn(g, q)
                    if reached(g, 2):
                        product(g - 2, q)
                    if reached(g, 3):
                        turn_logits(g - 3, 1 - q)

                steps(pe, 0, NG, step, peel=6)
                product(NG - 2, 0)
                turn_logits(NG - 3, 1)
                product(NG - 1, 1)
                turn_logits(NG - 2, 0)
                turn_logits(NG - 1, 1)

        tokf = keep("tokf", [P, NT])
        with ExitStack() as ctx:
            sb = lambda n, s, d=F32: ctx.enter_context(nc.sbuf_tensor(n, s, d))
            ps = lambda n, s: ctx.enter_context(nc.psum_tensor(n, s, F32))
            sem = lambda n: ctx.enter_context(nc.semaphore(n))
            two = lambda n, s, d=F32: [sb(f"{n}{q}", s, d) for q in range(2)]
            cacc = two("cacc", [P, GRP])
            xc = two("xc", [P, XB, GRP])
            bmat = two("bmat", [NS, GRP])
            cmat = two("cmat", [NS, GRP])
            gate = sb("gate", [P, H, P])
            dbc = two("dbc", [P, H, P])
            L = sb("L", [P, H, P])
            lin = two("lin", [NS, H, P])
            eyeD = sb("eyeD", [P, H, P])
            eye4 = sb("eye4", [P, H, P])
            stage = sb("stage", [P, KC, 2 * MF])
            M = two("M", [P, H, P])
            xtok = two("xtok", [P, H, P])
            btok = two("btok", [P, NS])
            CL = two("CL", [NS, H, P])
            BL = two("BL", [P, H, NS])
            yg = sb("yg", [P, 2, H, P], F32R)
            ysq = sb("ysq", [P, H, P])
            state = sb("state", [NS, H, P])
            sout = sb("sout", [P, DM])
            SPS = 5
            sidx = [sb(f"sidx{i}", [P, 2], U32) for i in range(SPS)]
            sval = [sb(f"sval{i}", [P, 1]) for i in range(SPS)]
            score = logits[:, 0:E, :]
            big = lambda i: scratch[:, NR * NT + i * E * NT:NR * NT + (i + 1) * E * NT].rearrange(
                "p (e j) -> p e j", e=E)
            score2, iota_e, hot0, hot1, tmp, cum = [big(i) for i in range(6)]
            hot = [hot0, hot1]
            spare = scratch[:, (NR + 6 * E) * NT:]
            best = spare[:, 0:2 * NT].rearrange("p (c j) -> p c j", c=2)
            pick, den, slot_f = [spare[:, (2 + i) * NT:(3 + i) * NT] for i in range(3)]
            before, count, tiles, tiles_in, offset, tiles_f = [
                spare[:, 5 * NT + i * E:5 * NT + (i + 1) * E] for i in range(6)]
            tiles_i = tiles_f.bitcast(I32)
            iota_t = spare[0:1, 5 * NT + 6 * E:5 * NT + 6 * E + NTILE]
            sums = spare[:, 5 * NT + 6 * E + NTILE:5 * NT + 8 * E + NTILE]
            passed = scratch[0:1, 0:NTILE * E].rearrange("p (t e) -> p t e", e=E)
            owner, owner2 = [tmp[0:1].rearrange("p e j -> p (e j)")[:, i * NTILE:(i + 1) * NTILE] for i in range(2)]
            assert NTILE * E <= (NR + E) * NT
            tri = stage[:].rearrange("p k m -> p (k m)")[:, 0:P]
            arate = sb("arate", [P, H])
            halves = [t[:].rearrange("p h t -> p (h t)")[:, i * NT * H:(i + 1) * NT * H]
                      for t in (L, M[0], M[1], gate) for i in range(2)]
            dtx, dta, dte, dts, dtq, dtp, dec = [t.rearrange("p (j h) -> p j h", h=H) for t in halves[0:7]]
            dec_flat = halves[6]
            decT = ysq[:, 0:2, :]
            linT = ysq[:, 2:4, :]
            ps_p = [ps(f"ps_p{q}", [P, GRP]) for q in range(2)]
            ps_x = ps("ps_x", [P, H, P])
            ps_bg = ps("ps_bg", [P, GRP])
            ps_y = ps("ps_y", [P, H, P])
            ps_s = ps("ps_s", [P, H, P])
            ps_o = ps("ps_o", [P, GRP])
            ps_z = ps("ps_z", [P, H, P])
            c_tri = sem("c_tri")
            c_iota = sem("c_iota")
            scored = sem("scored")
            abs_done = sem("abs_done")
            exp_done = sem("exp_done")
            rate_exp = sem("rate_exp")
            log_done = sem("log_done")
            dec_done = sem("dec_done")
            dec_turned = sem("dec_turned")
            decT_done = sem("decT_done")
            linT_done = sem("linT_done")
            dec_ready = sem("dec_ready")
            dec_out = sem("dec_out")
            exp_here = sem("exp_here")
            wd_here = sem("wd_here")
            tr_here = sem("tr_here")
            late_here = [sem(f"late_here{i}") for i in range(E - (NG - 3))]
            ehi_done = sem("ehi_done")
            elo_done = sem("elo_done")
            lin_here = [sem(f"lin_here{q}") for q in range(2)]
            ysum_seq = sem("ysum_seq")
            ysum_done = sem("ysum_done")
            counted = sem("counted")
            summed = sem("summed")
            counts_read = sem("counts_read")
            router_dve = sem("router_dve")
            router_pool = sem("router_pool")
            slots_done = sem("slots_done")
            routed = sem("routed")
            dve_seq = sem("dve_seq")
            dec_here = [sem(f"dec_here{q}") for q in range(2)]
            s_out = sem("s_out")
            scattered = [sem(f"scattered{i}") for i in range(SPS)]
            idx_done = sem("idx_done")
            consts = sem("consts")
            eye_done = sem("eye_done")
            projected = sem("projected")
            cin_done = sem("cin_done")
            conv_seq = sem("conv_seq")
            conv_done = sem("conv_done")
            silu_done = sem("silu_done")
            turned = sem("turned")
            xtok_done = sem("xtok_done")
            btok_done = sem("btok_done")
            z_done = sem("z_done")
            gate_done = sem("gate_done")
            L_done = sem("L_done")
            M_done = sem("M_done")
            MD_done = sem("MD_done")
            CL_done = sem("CL_done")
            BL_done = sem("BL_done")
            y_done = sem("y_done")
            s_done = sem("s_done")
            st_done = sem("st_done")
            yg_done = sem("yg_done")
            yg_high = sem("yg_high")
            yg_low = sem("yg_low")
            ysq_done = sem("ysq_done")
            o_done = sem("o_done")
            sout_done = sem("sout_done")
            block = ctx.enter_context(nc.Block())
            NB = XB + 1
            ORDER = [XB] + list(range(XB))
            PBLK = [[0, 1], [2], [3], [4]]
            CBLK = [[0], [1], [3], [4]]
            CBLK2 = [[], [2], [], []]
            ABLK = [[0], [1], [2, 3], [4]]
            S0 = 4
            LATE = E - (NG - S0 + 1)
            late = [xc[NG % 2][:, i, :].rearrange("p (k m) -> p k m", k=KC) for i in range(LATE)]
            assert 0 <= LATE <= XB and KC * 2 * MF == GRP
            SBLK = [[0], [1], [2], [3, 4]]
            assert 0 < NT - SPS * (NG - S0) <= 4

            def turns_at(q, j):
                return (NB * q + j) % 2

            def some(n):
                return reached(n, 0)

            def chunks(p, k):
                return 4 * (p - 1) + k, 2 * (p - 1) + k // 2

            @block.sync
            def _(sp):
                sp.wait_ge(dec_ready, 1)
                sp.dma_start(dec_d.rearrange("(c r) t -> r c t", r=P), decT).then_inc(dec_out, 16)
                sp.dma_start(lin_d.rearrange("(c r) t -> r c t", r=P), linT).then_inc(dec_out, 16)
                sp.wait_ge(dec_out, 32)

                def spread(table, n, rows):
                    return table[ds(n * H, H), :].rearrange("h t -> (h t)").partition_broadcast(rows)

                def load(n, q):
                    ge(sp, L_done, n - 1)
                    sp.dma_start(dbc[q][:].rearrange("p h t -> p (h t)"), spread(dec_d, n, P)
                                 ).then_inc(dec_here[q], 16)
                    ge(sp, CL_done, n - 1)
                    ge(sp, st_done, n - 1)
                    sp.dma_start(lin[q][:].rearrange("p h t -> p (h t)"), spread(lin_d, n, NS)
                                 ).then_inc(lin_here[q], 16)

                def store(n):
                    sp.wait_ge(sout_done, n + 1)
                    sp.dma_start(s_d[ds(n * P, P), :], sout[:]).then_inc(s_out, 16)

                def expert(e, to, here):
                    for w, table in enumerate((w_gate, w_up)):
                        sp.dma_start(to[:, :, w * MF:(w + 1) * MF],
                                     table[ds(e, 1)].rearrange("o (k p) m -> p (o k) m", p=P)).then_inc(here, 16)

                def down_weights(m):
                    sp.dma_start(wd[:, m, :], w_down[m].rearrange("e m d -> m e d")).then_inc(wd_here, 16)

                def step(p, _):
                    for k in range(4):
                        n, before = chunks(p, k)
                        load(n, k % 2)
                        if k == 3 and isinstance(p, int) and p == S0 - 1:
                            sp.wait_ge(summed, 1)
                        if k == 2 and reached(p, S0):
                            ge(sp, elo_done, p - S0)
                            expert(p - S0, stage[:], exp_here)
                        if k >= 1 and isinstance(p, int) and p == NG:
                            m = slice((k - 1) * 4, k * 4)
                            if k == 1:
                                sp.wait_ge(conv_done, NB * NG)
                            down_weights(m)
                        if k == 3 and isinstance(p, int) and p == NG:
                            sp.wait_ge(turned, 4 * (NG - 1))
                            for i in range(LATE):
                                expert(E - LATE + i, late[i], late_here[i])
                        if some(n - 3):
                            store(n - 3)

                steps(sp, 1, NG + 1, step)
                down_weights(slice(12, E))
                for n in range(NT - 3, NT - 1):
                    store(n)
                for i in range(SPS):
                    sp.wait_ge(scattered[i], 32 * len(range(i, NT, SPS)))
                sp.dma_start(tok_rows[:], tok_d.rearrange("(c r p) o -> r c (p o)", c=2, p=P)).then_inc(tr_here, 16)
                store(NT - 1)
                sp.wait_ge(s_out, 16 * NT)
                sp.wait_ge(wd_here, 16 * 4)
                sp.wait_ge(tr_here, 16)

            @block.gpsimd
            def _(pool):
                pool.memset(cin[:, :, 0:3], 0.0).then_inc(consts, 1)
                pool.affine_select(out=tri, in_=ones[:], compare_op=ALU.is_gt, fill=0.0, base=0,
                                   pattern=[[1, P]], channel_multiplier=-1).then_inc(c_tri, 1)
                for h in range(H):
                    last = pool.tensor_copy(eye4[:, h, :], ident[:])
                last.then_inc(eye_done, 1)
                pool.iota(iota_e, pattern=[[1, E], [0, NT]], base=-E, channel_multiplier=0,
                          allow_small_or_imprecise_dtypes=True).then_inc(c_iota, 1)
                pool.iota(iota_t, pattern=[[1, NTILE]], base=0, channel_multiplier=0,
                          allow_small_or_imprecise_dtypes=True).then_inc(c_iota, 1)
                pool.iota(tokf[:], pattern=[[P, NT]], base=0, channel_multiplier=1,
                          allow_small_or_imprecise_dtypes=True).then_inc(c_iota, 1)
                for h in range(H):
                    last = pool.tensor_scalar(eyeD[:, h, :], ident[:], dsk[:, h:h + 1], None, ALU.mult)
                last.then_inc(eye_done, 1)
                pool.wait_ge(eye_done, 2)
                pool.wait_ge(c_iota, 3)

                def sum_squares(n):
                    pool.wait_ge(ysq_done, n + 1)
                    pool.tensor_tensor(ysq[:, 0:2, :], ysq[:, 0:2, :], ysq[:, 2:4, :], ALU.add).then_inc(ysum_seq, 1)
                    pool.wait_ge(ysum_seq, n + 1)
                    pool.tensor_tensor(ysq[:, 0, :], ysq[:, 0, :], ysq[:, 1, :], ALU.add).then_inc(ysum_done, 1)

                def scatter(p, i):
                    m = SPS * p + i - SPS * S0
                    ge(pool, scattered[i], 32 * p - 32 * S0)
                    pool.tensor_copy(sidx[i][:], slot[:, :, ds(m, 1)].rearrange("p c o -> p (c o)"))
                    pool.tensor_copy(sval[i][:], tokf[:, ds(m, 1)]).then_inc(idx_done, 1)
                    ge_apart(pool, eye_done, (idx_done, m + 1))
                    for c in range(2):
                        pool.indirect_dma_start(
                            out=tok_d, out_offset=bass.IndirectOffsetOnAxis(ap=sidx[i][:, c:c + 1], axis=0),
                            in_=sval[i][:], in_offset=None).then_inc(scattered[i], 16)

                def router_part(p, k):
                    def done(ins, count):
                        ins.then_inc(router_pool, 1)
                        pool.wait_ge(router_pool, count)

                    if (p, k) == (1, 0):
                        pool.wait_ge(router_dve, 1)
                        done(pool.tensor_tensor(tmp, tmp, iota_e, ALU.mult), 1)
                    if (p, k) == (1, 3):
                        pool.wait_ge(router_dve, 2)
                        done(pool.tensor_tensor(tmp, tmp, iota_e, ALU.mult), 2)
                    if (p, k) == (2, 0):
                        pool.wait_ge(router_dve, 3)
                        done(pool.tensor_tensor(tmp, hot[0], hot[1], ALU.add), 3)
                    if (p, k) == (2, 2):
                        pool.wait_ge(counted, 1)
                        done(pool.tensor_tensor(cum, cum, tmp, ALU.subtract), 4)
                    if (p, k) == (3, 0):
                        pool.wait_ge(router_dve, 4)
                        done(pool.tensor_tensor(cum, cum, offset.unsqueeze(2).broadcast_to([P, E, NT]), ALU.add), 5)
                    if (p, k) == (3, 1):
                        done(pool.tensor_tensor(tmp, hot[0], cum, ALU.mult), 6)
                    if (p, k) == (3, 2):
                        done(pool.tensor_tensor(iota_e, hot[1], cum, ALU.mult), 7)
                    if (p, k) == (3, 3):
                        pool.wait_ge(slots_done, 1)

                def step(p, _):
                    for k in range(4):
                        n, before = chunks(p, k)
                        q = k % 2
                        pool.wait_ge(btok_done, n + 1)
                        pool.wait_ge(L_done, n + 1)
                        ge(pool, s_done, n - 1)
                        pool.tensor_tensor(BL[q][:], L[:, :, P - 1:P].broadcast_to([P, H, NS]),
                                           btok[q][:].unsqueeze(1).broadcast_to([P, H, NS]),
                                           ALU.mult).then_inc(BL_done, 1)
                        pool.wait_ge(M_done, n + 1)
                        pool.tensor_tensor(M[q][:], M[q][:], eyeD[:], ALU.add).then_inc(MD_done, 1)
                        if some(n - 1):
                            sum_squares(n - 1)
                        pool.wait_ge(silu_done, (XB + 2) * p)
                        pool.wait_ge(lin_here[q], 16 * before + 16)
                        ge(pool, y_done, n - 1)
                        pool.tensor_tensor(CL[q][:], lin[q][:],
                                           cmat_of[0](p)[:, k * P:(k + 1) * P].unsqueeze(1).broadcast_to([NS, H, P]),
                                           ALU.mult).then_inc(CL_done, 1)
                        if isinstance(p, int) and p == NG:
                            if k < NT - SPS * (NG - S0):
                                scatter(p, k)
                        elif reached(p, S0):
                            for i in SBLK[k]:
                                scatter(p, i)

                        if isinstance(p, int) and 1 <= p < S0:
                            router_part(p, k)

                cmat_of = [None]

                def with_parity(p, q):
                    cmat_of[0] = lambda _: cmat[1 - q]
                    step(p, q)

                steps(pool, 1, NG, with_parity)
                with_parity(NG, NG % 2)
                sum_squares(NT - 1)
                for i in range(SPS):
                    pool.wait_ge(scattered[i], 32 * len(range(i, NT, SPS)))

            @block.scalar
            def _(act):
                act.wait_ge(consts, 1)
                act.activation(arate[:], alog[:], ACT.Exp).then_inc(rate_exp, 1)

                def expert_high(e, src, here, value):
                    act.wait_ge(here, value)
                    act.activation(wgu16[:, HI, :, ds(e, 1), :].rearrange("p k o m -> p (k o) m"), src, ACT.Copy,
                                   scale=WS).then_inc(ehi_done, 1)

                def evac(p, q, j):
                    b = ORDER[j]
                    act.wait_ge(projected, NB * p + j + 1)
                    ge(act, conv_done, NB * (p - 1) + j + 1)
                    act.activation(cin[:, b, 3 + q * GRP:3 + (q + 1) * GRP], ps_p[turns_at(q, j)][:], ACT.Copy,
                                   scale=1.0 / WS)
                    ge(act, silu_done, (XB + 2) * p + j if j >= 2 else (XB + 2) * p - 1 + j)
                    act.activation(cacc[turns_at(q, j)][:], ps_p[turns_at(q, j)][:], ACT.Identity,
                                   bias=cb[:, b:b + 1], scale=cw3[:, b:b + 1]).then_inc(cin_done, 1)

                def silu(p, q, j):
                    if j == 0:
                        ge(act, turned, 4 * (p - 1))
                        ge(act, CL_done, 4 * (p - 1))
                    act.wait_ge(conv_done, NB * p + j + 1)
                    src = cacc[turns_at(q, j)]
                    if ORDER[j] < XB:
                        act.activation(xc[q][:, ORDER[j], :], src[:], ACT.Silu).then_inc(silu_done, 1)
                    else:
                        act.activation(bmat[q][:], src[0:NS, :], ACT.Silu).then_inc(silu_done, 1)
                        act.activation(cmat[q][:], src[NS:2 * NS, :], ACT.Silu).then_inc(silu_done, 1)

                def token_side(n, q):
                    act.wait_ge(turned, n + 1)
                    ge(act, s_done, n - 1)
                    ge(act, BL_done, n - 1)
                    act.activation(btok[q][:], ps_bg[:, 0:NS], ACT.Copy).then_inc(btok_done, 1)
                    act.activation(xtok[q][:], ps_x[:], ACT.Copy).then_inc(xtok_done, 1)

                def gates(n):
                    act.wait_ge(z_done, n + 1)
                    ge(act, yg_low, n)
                    act.activation(gate[:], ps_z[:], ACT.Tanh, scale=0.5 / WS).then_inc(gate_done, 1)

                def square(n):
                    act.wait_ge(yg_done, n + 1)
                    ge(act, o_done, n)
                    act.activation(ysq[:], ps_y[:], ACT.Square).then_inc(ysq_done, 1)
                    act.activation(yg[:, HI], gate[:], ACT.Copy).then_inc(yg_high, 1)

                def result(n):
                    act.wait_ge(o_done, n + 1)
                    ge(act, s_out, 16 * n)
                    act.activation(ms_all[:, ds(n, 1)], ps_o[:, DM:DM + 1], ACT.Copy)
                    act.activation(sout[:], ps_o[:, 0:DM], ACT.Copy).then_inc(sout_done, 1)

                def step(p, q, proj=True, scan=True):
                    for k in range(4):
                        n, before = chunks(p, k)
                        if scan:
                            token_side(n, k % 2)
                            if some(n - 1):
                                gates(n - 1)
                        if proj:
                            for j in PBLK[k]:
                                evac(p, q, j)
                        if scan and some(n - 2):
                            result(n - 2)
                        if not scan and k == 0:
                            act.wait_ge(log_done, 1)
                            act.activation(dec, dta, ACT.Exp, scale=-1.0).then_inc(dec_done, 1)
                        if not scan and k == 1:
                            act.wait_ge(dec_turned, 1)
                            act.activation(decT, ps_s[:, 0:2, :], ACT.Copy).then_inc(decT_done, 1)
                        if proj:
                            for j in ABLK[k]:
                                silu(p, q, j)
                        if scan and some(n - 1):
                            square(n - 1)
                        if k == 3 and isinstance(p, int) and p == S0 - 1:
                            act.wait_ge(routed, 1)
                            act.wait_ge(slots_done, 1)
                        if k == 3 and reached(p, S0):
                            expert_high(p - S0, stage[:], exp_here, 32 * p - 32 * (S0 - 1))

                act.wait_ge(abs_done, 1)
                act.activation(dte, dta, ACT.Exp, scale=-1.0).then_inc(exp_done, 1)
                step(0, 0, scan=False)
                act.activation(score, score, ACT.Sigmoid).then_inc(scored, 1)
                steps(act, 1, NG, step)
                step(NG, 0, proj=False)
                gates(NT - 1)
                square(NT - 1)
                for i in range(LATE):
                    expert_high(E - LATE + i, late[i], late_here[i], 32)
                result(NT - 2)
                result(NT - 1)

            @block.vector
            def _(dve):
                seq = [0]

                def link(ins):
                    seq[0] += 1
                    ins.then_inc(dve_seq, 1)
                    dve.wait_ge(dve_seq, seq[0])

                bc = [P, NT, H]

                def step_size_in():
                    link(dve.tensor_tensor(dtx, logits[:, E:NR, :].rearrange("p h j -> p j h"),
                                           dtb[:].unsqueeze(1).broadcast_to(bc), ALU.add))
                    dve.scalar_tensor_tensor(dta, dtx, -1.0, dtx, ALU.mult, ALU.max).then_inc(abs_done, 1)

                def step_size_out():
                    dve.wait_ge(exp_done, 1)
                    link(dve.tensor_scalar(dtp, dte, 2.0, None, ALU.add))
                    link(dve.reciprocal(dtp, dtp))
                    link(dve.tensor_tensor(dts, dte, dtp, ALU.mult))
                    link(dve.tensor_tensor(dtq, dts, dts, ALU.mult))
                    link(dve.tensor_scalar(dtp, dtq, 1.0 / 17, None, ALU.mult))
                    for c in (15, 13, 11, 9, 7, 5, 3):
                        link(dve.scalar_tensor_tensor(dtp, dtp, 1.0 / c, dtq, ALU.add, ALU.mult))
                    link(dve.scalar_tensor_tensor(dts, dtp, 1.0, dts, ALU.add, ALU.mult))
                    link(dve.tensor_scalar(dts, dts, 2.0, None, ALU.mult))
                    link(dve.scalar_tensor_tensor(dtx, dtx, 0.0, dts, ALU.max, ALU.add))
                    dve.wait_ge(rate_exp, 1)
                    dve.tensor_tensor(dta, dtx, arate[:].unsqueeze(1).broadcast_to(bc), ALU.mult
                                      ).then_inc(log_done, 1)

                by_tok = [P, E, NT]

                def largest(c, src):
                    link(dve.tensor_reduce(best[:, c, :], src.rearrange("p e j -> p j e"), AX.X, ALU.max))

                def where_largest(c, src):
                    dve.tensor_tensor(tmp, src, best[:, c, :].unsqueeze(1).broadcast_to(by_tok), ALU.is_equal
                                      ).then_inc(router_dve, 1)

                def first_index(c):
                    dve.wait_ge(router_pool, c + 1)
                    link(dve.tensor_reduce(pick, tmp.rearrange("p e j -> p j e"), AX.X, ALU.min))
                    last = dve.tensor_tensor(hot[c], iota_e, pick.unsqueeze(1).broadcast_to(by_tok), ALU.is_equal)
                    if c == 0:
                        link(last)
                    else:
                        last.then_inc(router_dve, 1)
                        dve.wait_ge(router_dve, 3)

                def without_first():
                    link(dve.scalar_tensor_tensor(score2, hot[0], -4.0, score, ALU.mult, ALU.add))

                def weigh_choices():
                    link(dve.tensor_tensor(den, best[:, 0, :], best[:, 1, :], ALU.add))
                    link(dve.tensor_scalar(den, den, 1e-20, None, ALU.add))
                    link(dve.reciprocal(den, den))
                    for c in range(2):
                        link(dve.tensor_tensor(wtop[:, c, :], best[:, c, :], den, ALU.mult))
                    link(dve.tensor_scalar(wtop[:], wtop[:], SCALE, None, ALU.mult))

                def count_choices():
                    flat = lambda t: t.rearrange("p e j -> p (e j)")
                    dve.wait_ge(router_pool, 3)
                    link(dve.tensor_tensor_scan(flat(cum), flat(tmp), flat(tmp), 0.0, ALU.add, ALU.max))

                def counts():
                    link(dve.memset(before, 0.0))
                    link(dve.tensor_copy(before[:, 1:E], cum[:, 0:E - 1, NT - 1]))
                    dve.tensor_tensor(count, cum[:, :, NT - 1], before, ALU.subtract).then_inc(counted, 1)

                def counts_in():
                    dve.wait_ge(summed, 1)
                    dve.tensor_copy(sums, ps_bg[:, 2 * P:2 * P + 2 * E]).then_inc(counts_read, 1)

                def place_experts():
                    dve.wait_ge(counts_read, 1)
                    link(dve.tensor_scalar(tiles_i, sums[:, E:2 * E], float(P - 1), None, ALU.add))
                    link(dve.tensor_scalar(tiles_i, tiles_i, 7, None, ALU.logical_shift_right))
                    link(dve.tensor_copy(tiles, tiles_i))
                    link(dve.tensor_tensor_scan(tiles_in, tiles, tiles, 0.0, ALU.add, ALU.max))
                    link(dve.tensor_tensor(offset, tiles_in, tiles, ALU.subtract))
                    link(dve.scalar_tensor_tensor(offset, offset, float(P), sums[:, 0:E], ALU.mult, ALU.add))
                    dve.tensor_tensor(offset, offset, before, ALU.subtract).then_inc(router_dve, 1)

                def place_tokens(c):
                    dve.wait_ge(router_pool, 6 + c)
                    link(dve.tensor_reduce(slot_f, (tmp, iota_e)[c].rearrange("p e j -> p j e"), AX.X, ALU.add))
                    last = dve.tensor_copy(slot[:, c, :], slot_f)
                    if c == 0:
                        link(last)
                    else:
                        last.then_inc(slots_done, 1)

                def own_tiles():
                    te = [1, NTILE, E]
                    link(dve.tensor_tensor(passed, tiles_in[0:1, :].unsqueeze(1).broadcast_to(te),
                                           iota_t.unsqueeze(2).broadcast_to(te), ALU.is_le))

                def own_tiles_out():
                    link(dve.tensor_reduce(owner, passed, AX.X, ALU.add))
                    link(dve.tensor_scalar(owner2, owner, float(E - 1), None, ALU.min))
                    dve.tensor_copy(tile_expert[:], owner2).then_inc(routed, 1)

                def conv(p, q, j):
                    b = ORDER[j]
                    acc = cacc[turns_at(q, j)]
                    src = cin[:, b, q * GRP:q * GRP + GRP + 3]
                    dve.wait_ge(cin_done, NB * p + j + 1)
                    for t in range(3):
                        if t > 0:
                            dve.wait_ge(conv_seq, 2 * (NB * p + j) + t)
                        dve.scalar_tensor_tensor(acc[:], src[:, t:t + GRP], cw[:, b, t:t + 1], acc[:], ALU.mult,
                                                 ALU.add).then_inc(conv_seq if t < 2 else conv_done, 1)

                def scan_lin():
                    dve.wait_ge(decT_done, 1)
                    for c in range(2):
                        last = dve.tensor_tensor_scan(linT[:, c, :], decT[:, c, :], ones[:], 1.0, ALU.mult, ALU.mult)
                    last.then_inc(linT_done, 1)
                    dve.wait_ge(linT_done, 1)
                    dve.memset(decT[:, :, 0], 0.0).then_inc(dec_ready, 1)

                def scans(n, before, q):
                    dve.wait_ge(dec_here[q], 16 * before + 16)
                    row = lambda t: t.rearrange("p h t -> p (h t)")
                    if isinstance(n, int) and n == 0:
                        dve.wait_ge(eye_done, 1)
                    ge(dve, BL_done, n)
                    ge(dve, M_done, n)
                    dve.tensor_tensor_scan(row(L[:]), row(dbc[q][:]), row(eye4[:]), 0.0, ALU.mult, ALU.add
                                           ).then_inc(L_done, 1)

                def mix(n, q):
                    dve.wait_ge(btok_done, n + 1)
                    dve.wait_ge(L_done, n + 1)
                    ge(dve, y_done, n - 1)
                    dve.tensor_tensor(M[q][:], L[:], ps_bg[:, P:2 * P].unsqueeze(1).broadcast_to([P, H, P]),
                                      ALU.mult).then_inc(M_done, 1)

                def gated(n):
                    dve.wait_ge(y_done, n + 1)
                    dve.wait_ge(gate_done, n + 1)
                    ge(dve, o_done, n)
                    dve.scalar_tensor_tensor(gate[:], gate[:], 1.0, ps_y[:], ALU.add, ALU.mult).then_inc(yg_done, 1)

                def gated_low(n):
                    dve.wait_ge(yg_high, n + 1)
                    dve.tensor_tensor(yg[:, LO], gate[:], yg[:, HI].bitcast(F32), ALU.subtract).then_inc(yg_low, 1)

                def carry(n, q, fresh):
                    dve.wait_ge(s_done, n + 1)
                    ge(dve, st_done, n)
                    if fresh:
                        dve.tensor_copy(state[:], ps_s[0:NS]).then_inc(st_done, 1)
                        return
                    for h in range(H):
                        last = dve.scalar_tensor_tensor(state[:, h, :], state[:, h, :], lin[q][:, h, P - 1:P],
                                                        ps_s[0:NS, h, :], ALU.mult, ALU.add)
                    last.then_inc(st_done, 1)

                def router_part(p, k):
                    if (p, k) == (1, 0):
                        dve.wait_ge(scored, 1)
                        dve.wait_ge(c_iota, 3)
                        largest(0, score)
                        where_largest(0, score)
                    if (p, k) == (1, 1):
                        first_index(0)
                    if (p, k) == (1, 2):
                        without_first()
                        largest(1, score2)
                    if (p, k) == (1, 3):
                        where_largest(1, score2)
                    if (p, k) == (2, 0):
                        first_index(1)
                    if (p, k) == (2, 1):
                        weigh_choices()
                        count_choices()
                    if (p, k) == (2, 2):
                        counts()
                    if (p, k) == (3, 0):
                        place_experts()
                    if (p, k) == (3, 1):
                        own_tiles()
                    if (p, k) == (3, 2):
                        place_tokens(0)
                        own_tiles_out()
                    if (p, k) == (3, 3):
                        place_tokens(1)

                def expert_low(e, src):
                    dve.wait_ge(ehi_done, e + 1)
                    row = wgu16[:, :, :, ds(e, 1), :].rearrange("p c k o m -> p c (k o) m")
                    dve.scalar_tensor_tensor(row[:, LO], src, WS, row[:, HI], ALU.mult, ALU.subtract
                                             ).then_inc(elo_done, 1)

                def step(p, q, proj=True, scan=True):
                    for k in range(4):
                        n, before = chunks(p, k)
                        if scan:
                            scans(n, before, k % 2)
                            mix(n, k % 2)
                        if not scan and k == 0:
                            step_size_in()
                            step_size_out()
                        if isinstance(p, int) and p == 3 and k == 0:
                            counts_in()
                        if proj:
                            for j in CBLK[k]:
                                conv(p, q, j)
                        if not scan and k == 1:
                            scan_lin()
                        if scan and some(n - 1):
                            gated(n - 1)
                            carry(n - 1, 1 - k % 2, fresh=(q == 1 and k == 1))
                            gated_low(n - 1)
                        if proj:
                            for j in CBLK2[k]:
                                conv(p, q, j)
                        if isinstance(p, int) and 1 <= p < S0:
                            router_part(p, k)
                        if k == 3 and reached(p, S0):
                            expert_low(p - S0, stage[:])

                step(0, 0, scan=False)
                steps(dve, 1, NG, step)
                step(NG, 0, proj=False)
                gated(NT - 1)
                gated_low(NT - 1)
                for i in range(LATE):
                    expert_low(E - LATE + i, late[i])

            @block.tensor
            def _(pe):
                def project(p, q, j):
                    b = ORDER[j]
                    ge(pe, cin_done, NB * p + j - 1)
                    last = split_product(pe, ps_p[turns_at(q, j)][:],
                                         lambda c, k: win[:, c, k, DI + b * P:DI + (b + 1) * P],
                                         lambda c, k: xnT[:, k, c, ds(p * GRP, GRP)])
                    last.then_inc(projected, 1)

                def turn(p, q, n, k):
                    if isinstance(p, int) and p == 3 and k == 1:
                        pe.wait_ge(counts_read, 1)
                    pe.wait_ge(silu_done, (XB + 2) * p)
                    ge(pe, xtok_done, n)
                    ge(pe, btok_done, n)
                    ge(pe, M_done, n)
                    if isinstance(p, int) and p == 3 and k == 0:
                        pe.wait_ge(c_tri, 1)
                        pe.wait_ge(counted, 1)
                        pe.matmul(ps_bg[:, 2 * P:2 * P + E], tri, count, start=True, stop=True)
                        pe.matmul(ps_bg[:, 2 * P + E:2 * P + 2 * E], ones[:], count, start=True, stop=True
                                  ).then_inc(summed, 1)
                    t = slice(k * P, (k + 1) * P)
                    for b in range(XB):
                        pe.transpose(ps_x[:, b, :], xc[1 - q][:, b, t], ident[:])
                    pe.transpose(ps_bg[:, 0:NS], bmat[1 - q][:, t], ident[0:NS, 0:NS])
                    pe.matmul(ps_bg[:, P:2 * P], bmat[1 - q][:, t], cmat[1 - q][:, t], start=True, stop=True
                              ).then_inc(turned, 1)

                def zed(n):
                    ge(pe, gate_done, n)
                    for h in range(H):
                        last = split_product(pe, ps_z[:, h, :], lambda c, k: win[:, c, k, h * P:(h + 1) * P],
                                             lambda c, k: xnT[:, k, c, ds(n * P, P)])
                    last.then_inc(z_done, 1)

                def mixed(n, q, fresh):
                    pe.wait_ge(MD_done, n + 1)
                    pe.wait_ge(xtok_done, n + 1)
                    pe.wait_ge(CL_done, n + 1)
                    ge(pe, st_done, n)
                    ge(pe, yg_done, n)
                    ge(pe, ysq_done, n)
                    for h in range(H):
                        last = pe.matmul(ps_y[:, h, :], xtok[q][:, h, :], M[q][:, h, :], start=True, stop=fresh)
                        if not fresh:
                            last = pe.matmul(ps_y[:, h, :], state[:, h, :], CL[q][:, h, :], start=False, stop=True)
                    last.then_inc(y_done, 1)

                def new_state(n, q):
                    pe.wait_ge(BL_done, n + 1)
                    for h in range(H):
                        last = pe.matmul(ps_s[0:NS, h, :], BL[q][:, h, :], xtok[q][:, h, :], start=True, stop=True)
                    last.then_inc(s_done, 1)

                def output(n):
                    pe.wait_ge(yg_low, n + 1)
                    pe.wait_ge(ysum_done, n + 1)
                    ge(pe, sout_done, n)
                    split_rounds(pe, ps_o[:, 0:DM], lambda c, h: yg[:, c, h, :], lambda c, h: wo[:, c, h, :], H)
                    last = pe.matmul(ps_o[:, DM:DM + 1], ysq[:, 0, :], ones[:, 0:1], start=True, stop=True)
                    last.then_inc(o_done, 1)

                def step(p, q, proj=True, scan=True):
                    for k in range(4):
                        n, _ = chunks(p, k)
                        if scan:
                            turn(p, q, n, k)
                        if proj:
                            for j in PBLK[k]:
                                project(p, q, j)
                        if scan and some(n - 2):
                            output(n - 2)
                        if not scan and k == 1:
                            pe.wait_ge(dec_done, 1)
                            for c in range(2):
                                last = pe.transpose(ps_s[:, c, :], dec_flat[:, c * P:(c + 1) * P], ident[:])
                            last.then_inc(dec_turned, 1)
                        if scan:
                            if some(n - 1):
                                mixed(n - 1, 1 - k % 2, fresh=(q == 1 and k == 1))
                                new_state(n - 1, 1 - k % 2)
                            zed(n)

                step(0, 0, scan=False)
                steps(pe, 1, NG, step)
                step(NG, 0, proj=False)
                output(NT - 2)
                mixed(NT - 1, 1, fresh=False)
                output(NT - 1)

        NX = NTILE // TPG
        with ExitStack() as ctx:
            sb = lambda n, s, d=F32: ctx.enter_context(nc.sbuf_tensor(n, s, d))
            ps = lambda n, s: ctx.enter_context(nc.psum_tensor(n, s, F32))
            sem = lambda n: ctx.enter_context(nc.semaphore(n))
            two = lambda n, s, d=F32: [sb(f"{n}{q}", s, d) for q in range(2)]
            x4 = two("x4", [P, TPG, 2 * DM], F16)
            RT = NTILE // 2
            tok_all = sb("tok_all", [P, 2, RT], U32)
            gi4 = two("gi4", [P, TPG], U32)
            y4 = two("y4", [P, TPG, DM])
            xT = two("xT", [P, 2, KC, P], F16)
            sg = two("sg", [P, MF])
            hid = two("hid", [P, MF])
            hidT = two("hidT", [P, P])
            ps_t = [ctx.enter_context(nc.psum_tensor(f"px_t{q}", [P, 2, KC, P], F16)) for q in range(2)]
            ps_g = [ps(f"px_g{q}", [P, 2 * MF]) for q in range(2)]
            ps_h = [ps(f"px_h{q}", [P, P]) for q in range(2)]
            ps_y = [ps(f"px_y{q}", [P, DM]) for q in range(2)]
            tr_turned = sem("tr_turned")
            tok_done = sem("tok_done")
            gi_done = sem("gi4_done")
            x_here = [[sem(f"x_here{q}{a}") for a in range(TPG)] for q in range(2)]
            y_out = [sem(f"y_out{q}") for q in range(2)]
            x_turned = sem("x_turned")
            xT_done = sem("xT_done")
            gu_done = sem("gu_done")
            sg_done = sem("sg_done")
            hid_done = sem("hid_done")
            h_turned = sem("h_turned")
            hidT_done = sem("hidT_done")
            down_done = sem("down_done")
            y4_done = sem("y4_done")
            block = ctx.enter_context(nc.Block())

            @block.sync
            def _(sp):
                def store(p, q):
                    sp.wait_ge(y4_done, TPG * (p + 1))
                    sp.dma_start(group_rows(ys_d, p), y4[q][:]).then_inc(y_out[q], 16)

                steps(sp, 0, NX, store)
                for q in range(2):
                    sp.wait_ge(y_out[q], 16 * (NX // 2))

            @block.gpsimd
            def _(pool):
                pool.wait_ge(tok_done, 1)
                numbers = tok_all[:].rearrange("p c r -> p (c r)")

                def step(p, q):
                    for a in range(TPG):
                        ge(pool, x_here[q][a], times(1, p, q, 0))
                    pool.tensor_copy(gi4[q][:], numbers[:, ds(TPG * p, TPG)]).then_inc(gi_done, 1)
                    pool.wait_ge(gi_done, p + 1)
                    for a in range(TPG):
                        ge_apart(pool, tok_done, (gi_done, p + 1), (x_turned, TPG * (p - 2) + a + 1))
                        pool.indirect_dma_start(
                            out=x4[q][:, a, :], out_offset=None, in_=xn_d,
                            in_offset=bass.IndirectOffsetOnAxis(ap=gi4[q][:, a:a + 1], axis=0)
                        ).then_inc(x_here[q][a], 16)

                steps(pool, 0, NX, step)

            @block.tensor
            def _(pe):
                def turn(p, q, a):
                    n = TPG * p + a
                    pe.wait_ge(x_here[q][a], times(1, p, q, 1))
                    ge(pe, xT_done, n - 1)
                    for c in (HI, LO):
                        for k in range(KC):
                            last = pe.transpose(ps_t[a % 2][:, c, k, :],
                                                x4[q][:, a, c * DM + k * P:c * DM + (k + 1) * P], ident16[:])
                    last.then_inc(x_turned, 1)

                owners = [[pe.alloc_register(f"owner{q}{a}") for a in range(TPG)] for q in range(2)]

                def owner_of(q, a):
                    return pe.snap(owners[q][a], min_val=0, max_val=E - 1)

                def up(n, q, gq, a):
                    e = owner_of(gq, a)
                    pe.wait_ge(xT_done, n + 1)
                    ge(pe, hid_done, n - 1)
                    last = split_product(pe, ps_g[q][:], lambda c, k: xT[q][:, c, k, :],
                                         lambda c, k: wgu16[:, c, k, e, :])
                    last.then_inc(gu_done, 1)

                def turn_hidden(n, q):
                    pe.wait_ge(hid_done, n + 1)
                    ge(pe, hidT_done, n - 1)
                    pe.transpose(ps_h[q][:], hid[q][:], ident[:]).then_inc(h_turned, 1)

                def down(n, q, gq, a):
                    e = owner_of(gq, a)
                    pe.wait_ge(hidT_done, n + 1)
                    ge(pe, y4_done, n - 1)
                    pe.matmul(ps_y[q][:], hidT[q][:], wd[:, e, :], start=True, stop=True).then_inc(down_done, 1)

                def step(p, q):
                    pe.load(owners[q], tile_expert[0:1, ds(TPG * p, TPG)])
                    for a in range(TPG):
                        n = TPG * p + a
                        turn(p, q, a)
                        if some(n - 1):
                            up(n - 1, 1 - a % 2, 1 - q if a == 0 else q, (a - 1) % TPG)
                        if some(n - 3):
                            down(n - 3, 1 - a % 2, q if a == 3 else 1 - q, (a + 1) % TPG)
                        if some(n - 2):
                            turn_hidden(n - 2, a % 2)

                for c in range(2):
                    last = pe.transpose(ps_g[0][:, c * P:c * P + RT], tok_rows[:, c, :], ident[0:RT, 0:RT])
                last.then_inc(tr_turned, 1)
                pe.wait_ge(tok_done, 1)
                steps(pe, 0, NX, lambda p, r: step(p, r % 2), period=4)
                down(NTILE - 3, 1, 1, 1)
                up(NTILE - 1, 1, 1, 3)
                turn_hidden(NTILE - 2, 0)
                down(NTILE - 2, 0, 1, 2)
                turn_hidden(NTILE - 1, 1)
                down(NTILE - 1, 1, 1, 3)

            @block.scalar
            def _(act):
                def xT_copy(n, q):
                    act.wait_ge(x_turned, n + 1)
                    ge(act, gu_done, n - 1)
                    act.activation(xT[q][:], ps_t[q][:], ACT.Copy).then_inc(xT_done, 1)

                def silu(n, q):
                    act.wait_ge(gu_done, n + 1)
                    ge(act, hid_done, n - 1)
                    act.activation(sg[q][:], ps_g[q][:, 0:MF], ACT.Silu, scale=1.0 / WS).then_inc(sg_done, 1)

                def hidT_copy(n, q):
                    act.wait_ge(h_turned, n + 1)
                    ge(act, down_done, n - 1)
                    act.activation(hidT[q][:], ps_h[q][:], ACT.Copy).then_inc(hidT_done, 1)

                def step(p, q):
                    for a in range(TPG):
                        n = TPG * p + a
                        xT_copy(n, a % 2)
                        if some(n - 1):
                            silu(n - 1, 1 - a % 2)
                        if some(n - 2):
                            hidT_copy(n - 2, a % 2)

                steps(act, 0, NX, step)
                silu(NTILE - 1, 1)
                hidT_copy(NTILE - 2, 0)
                hidT_copy(NTILE - 1, 1)

            @block.vector
            def _(dve):
                def hidden(n, q):
                    dve.wait_ge(sg_done, n + 1)
                    ge(dve, h_turned, n - 1)
                    dve.scalar_tensor_tensor(hid[q][:], ps_g[q][:, MF:2 * MF], 1.0 / WS, sg[q][:], ALU.mult,
                                             ALU.mult).then_inc(hid_done, 1)

                def result(p, q, a, qa):
                    dve.wait_ge(down_done, TPG * p + a + 1)
                    if a == 0:
                        ge(dve, y_out[q], times(1, p, q, 0))
                    dve.tensor_copy(y4[q][:, a, :], ps_y[qa][:]).then_inc(y4_done, 1)

                def step(p, q):
                    for a in range(TPG):
                        n = TPG * p + a
                        if some(n - 1):
                            hidden(n - 1, 1 - a % 2)
                        if some(n - 3):
                            if a == 3:
                                result(p, q, 0, 0)
                            else:
                                result(p - 1, 1 - q, a + 1, (a + 1) % 2)

                dve.wait_ge(tr_turned, 1)
                dve.tensor_copy(tok_all[:], ps_g[0][:].rearrange("p (c t) -> p c t", c=2)[:, :, 0:RT]
                                ).then_inc(tok_done, 1)
                steps(dve, 0, NX, step)
                result(NX - 1, 1, 1, 1)
                hidden(NTILE - 1, 1)
                result(NX - 1, 1, 2, 0)
                result(NX - 1, 1, 3, 1)

        with ExitStack() as ctx:
            sb = lambda n, s, d=F32: ctx.enter_context(nc.sbuf_tensor(n, s, d))
            ps = lambda n, s: ctx.enter_context(nc.psum_tensor(n, s, F32))
            sem = lambda n: ctx.enter_context(nc.semaphore(n))
            two = lambda n, s, d=F32: [sb(f"{n}{q}", s, d) for q in range(2)]
            ws_raw = sb("ws_raw", [P, 2, KC, MF])
            wsgu = sb("wsgu", [P, 2, 2, KC, MF], F16)
            wsd = sb("wsd", [MF, DM])
            msq = sb("msq", [P, NT])
            rms = sb("rms", [P, NT])
            u4 = two("fu4", [P, TPG, DM])
            s4 = two("fs4", [P, TPG, DM])
            o4 = two("fo4", [P, TPG, DM])
            RING = 2
            rows = [[[sb(f"rows{q}{a}{c}", [P, DM]) for c in range(2)] for a in range(TPG)] for q in range(RING)]
            hsg = two("hsg", [P, GRP])
            hs = two("hs", [P, GRP])
            acc = two("acc", [P, DM])
            gsil = two("gsil", [P, DM])
            gidx = two("gidx", [P, TPG, 2], U32)
            ps_g = [ps(f"pf_g{q}", [P, GRP]) for q in range(2)]
            ps_u = [ps(f"pf_u{q}", [P, GRP]) for q in range(2)]
            ps_y = [ps(f"pf_y{q}", [P, DM]) for q in range(2)]
            ws_here = sem("ws_here")
            us_here = [sem(f"us_here{q}") for q in range(2)]
            rows_here = [[sem(f"rows_here{q}{a}") for a in range(TPG)] for q in range(2)]
            o_out = [sem(f"o_out{q}") for q in range(2)]
            gi_done = sem("gi_done")
            shi_done = sem("shi_done")
            slo_done = sem("slo_done")
            rms_done = sem("rms_done")
            rms_inv = sem("rms_inv")
            up_done = sem("up_done")
            hsg_done = sem("hsg_done")
            hs_done = sem("hs_done")
            dn_done = sem("dn_done")
            m_seq = sem("m_seq")
            acc_done = sem("acc_done")
            gs_done = sem("gs_done")
            sg_done = sem("fsg_done")
            o4_done = sem("o4_done")
            block = ctx.enter_context(nc.Block())

            @block.sync
            def _(sp):
                for k in range(KC):
                    sp.dma_start(ws_raw[:, 0, k, :], ws_gate[k * P:(k + 1) * P, :]).then_inc(ws_here, 16)
                    sp.dma_start(ws_raw[:, 1, k, :], ws_up[k * P:(k + 1) * P, :]).then_inc(ws_here, 16)
                sp.dma_start(wsd[:], ws_down).then_inc(ws_here, 16)

                def store(p, q):
                    sp.wait_ge(o4_done, TPG * (p + 1))
                    sp.dma_start(group_rows(out_rows, p), o4[q][:]).then_inc(o_out[q], 16)

                def step(p, q):
                    ge(sp, o4_done, TPG * (p - 1))
                    sp.dma_start(u4[q][:], group_rows(u_rows, p)).then_inc(us_here[q], 16)
                    sp.dma_start(s4[q][:], group_rows(s_d, p)).then_inc(us_here[q], 16)
                    if some(p - 2):
                        store(p - 2, q)

                steps(sp, 0, NG, step)
                store(NG - 2, 0)
                store(NG - 1, 1)
                for q in range(2):
                    sp.wait_ge(o_out[q], 16 * (NG // 2))

            @block.gpsimd
            def _(pool):
                def step(p, q):
                    for a in range(TPG):
                        ge(pool, rows_here[q][a], times(2, p, q, 0))
                    pool.tensor_copy(gidx[q][:], slot[:, :, ds(TPG * p, TPG)].rearrange("p c a -> p a c")
                                     ).then_inc(gi_done, 1)
                    pool.wait_ge(gi_done, p + 1)
                    for a in range(TPG):
                        ge_apart(pool, gi_done, (acc_done, TPG * (p - 2) + a + 1))
                        for c in range(2):
                            pool.indirect_dma_start(
                                out=rows[q][a][c][:], out_offset=None, in_=ys_d,
                                in_offset=bass.IndirectOffsetOnAxis(ap=gidx[q][:, a, c:c + 1], axis=0)
                            ).then_inc(rows_here[q][a], 16)

                steps(pool, 0, NG, step)

            @block.tensor
            def _(pe):
                pe.wait_ge(slo_done, 1)

                def up(p, q):
                    ge(pe, hs_done, p - 1)
                    for w, bank in enumerate((ps_g, ps_u)):
                        last = split_product(pe, bank[q][:], lambda c, k: wsgu[:, c, w, k, :],
                                             lambda c, k: xnT[:, k, c, ds(p * GRP, GRP)])
                    last.then_inc(up_done, 1)

                def down(p, q):
                    pe.wait_ge(hs_done, p + 1)
                    for a in range(TPG):
                        ge(pe, acc_done, TPG * p + a - 1)
                        pe.matmul(ps_y[a % 2][:], hs[q][:, a * P:(a + 1) * P], wsd[:], start=True, stop=True
                                  ).then_inc(dn_done, 1)

                def step(p, q):
                    up(p, q)
                    if some(p - 1):
                        down(p - 1, 1 - q)

                steps(pe, 0, NG, step)
                down(NG - 1, 1)

            @block.scalar
            def _(act):
                act.activation(rms[:], ms_all[:], ACT.Sqrt, bias=eps[:, 1:2], scale=1.0 / DI).then_inc(rms_done, 1)
                act.wait_ge(ws_here, 16 * (2 * KC + 1))
                act.activation(wsgu[:, HI], ws_raw[:], ACT.Copy, scale=WS).then_inc(shi_done, 1)

                def silu_up(p, q):
                    act.wait_ge(up_done, p + 1)
                    ge(act, hs_done, p - 1)
                    act.activation(hsg[q][:], ps_g[q][:], ACT.Silu, scale=1.0 / WS).then_inc(hsg_done, 1)

                def silu_out(n, q):
                    act.wait_ge(acc_done, n + 1)
                    ge(act, sg_done, n - 1)
                    act.activation(gsil[q][:], acc[q][:], ACT.Silu).then_inc(gs_done, 1)

                def step(p, q):
                    silu_up(p, q)
                    if some(p - 1):
                        for a in range(TPG):
                            silu_out(TPG * (p - 1) + a, a % 2)

                steps(act, 0, NG, step)
                for a in range(TPG):
                    silu_out(TPG * (NG - 1) + a, a % 2)

            @block.vector
            def _(dve):
                dve.wait_ge(rms_done, 1)
                dve.reciprocal(msq[:], rms[:]).then_inc(rms_inv, 1)
                dve.wait_ge(shi_done, 1)
                dve.scalar_tensor_tensor(wsgu[:, LO], ws_raw[:], WS, wsgu[:, HI], ALU.mult, ALU.subtract
                                         ).then_inc(slo_done, 1)
                dve.wait_ge(rms_inv, 1)

                def hidden(p, q):
                    dve.wait_ge(hsg_done, p + 1)
                    ge(dve, dn_done, TPG * (p - 1))
                    dve.scalar_tensor_tensor(hs[q][:], ps_u[q][:], 1.0 / WS, hsg[q][:], ALU.mult, ALU.mult
                                             ).then_inc(hs_done, 1)

                def merge(p, q, a):
                    n = TPG * p + a
                    dve.wait_ge(dn_done, n + 1)
                    dve.wait_ge(rows_here[q][a], times(2, p, q, 1))
                    ge(dve, gs_done, n - 1)
                    y = acc[a % 2]
                    dve.scalar_tensor_tensor(y[:], rows[q][a][0][:], wtop[:, 0, ds(n, 1)], ps_y[a % 2][:], ALU.mult,
                                             ALU.add).then_inc(m_seq, 1)
                    dve.wait_ge(m_seq, n + 1)
                    dve.scalar_tensor_tensor(y[:], rows[q][a][1][:], wtop[:, 1, ds(n, 1)], y[:], ALU.mult,
                                             ALU.add).then_inc(acc_done, 1)

                def gate_out(p, q, a):
                    n = TPG * p + a
                    if a == 0:
                        dve.wait_ge(us_here[q], times(2, p, q, 1))
                        ge(dve, o_out[q], times(1, p, q, 0))
                    dve.wait_ge(gs_done, n + 1)
                    dve.scalar_tensor_tensor(o4[q][:, a, :], s4[q][:, a, :], msq[:, ds(n, 1)], gsil[a % 2][:],
                                             ALU.mult, ALU.mult).then_inc(sg_done, 1)
                    dve.wait_ge(sg_done, n + 1)
                    dve.tensor_tensor(o4[q][:, a, :], o4[q][:, a, :], u4[q][:, a, :], ALU.add).then_inc(o4_done, 1)

                def pair(p, q):
                    for a in range(TPG):
                        merge(p, q, a)
                        if a >= 1:
                            gate_out(p, q, a - 1)
                    gate_out(p, q, TPG - 1)

                def step(p, q):
                    hidden(p, q)
                    if some(p - 1):
                        pair(p - 1, 1 - q)

                steps(dve, 0, NG, step)
                pair(NG - 1, 1)


_INS = ['L0_attn_u', 'L0_attn_in_proj_w', 'L0_attn_conv_w', 'L0_attn_conv_b', 'L0_attn_dt_bias', 'L0_attn_A_log',
        'L0_attn_D', 'L0_attn_rms_w', 'L0_attn_out_w', 'L0_ffn_gate_w', 'L0_ffn_w_gate', 'L0_ffn_w_up',
        'L0_ffn_w_down', 'L0_ffn_ws_gate', 'L0_ffn_ws_up', 'L0_ffn_ws_down']
_TURNED = ('L0_attn_in_proj_w', 'L0_attn_out_w', 'L0_ffn_gate_w')


def kernel(**inputs):
    import numpy as _np
    import concourse.bacc as _bacc
    from concourse import mybir as _mybir
    from concourse.bass_utils import run_bass_kernel_spmd as _run

    nc = _bacc.Bacc("TRN2", target_bir_lowering=False, num_devices=1)
    arrays, args = {}, []
    for name in _INS:
        a = _np.asarray(inputs[name])
        a = _np.ascontiguousarray(a.T if name in _TURNED else a)
        arrays[f"in_{name}_dram"] = a
        args.append(nc.dram_tensor(f"in_{name}_dram", a.shape, _mybir.dt.from_np(a.dtype), kind="ExternalInput").ap())
    shape = inputs['L0_attn_u'].shape
    args.append(nc.dram_tensor("out_0_dram", shape, _mybir.dt.float32, kind="ExternalOutput").ap())
    bass_mixer_moe(nc, *args)
    r = _run(nc, [arrays], core_ids=[0])
    return r.results[0]["out_0_dram"]
```
